# Optimizing a Trainium2 kernel written in Bass

```python
import numpy as np
import jax
import jax.numpy as jnp

def _softmax(x, axis=-1):
    return jax.nn.softmax(x, axis=axis)

def _gelu(x):
    return jax.nn.gelu(x, approximate=True)

def _silu(x):
    return jax.nn.silu(x)

def _sigmoid(x):
    return jax.nn.sigmoid(x)

def _layernorm(x, axis=-1, eps=1e-05):
    m = jnp.mean(x, axis=axis, keepdims=True)
    v = jnp.var(x, axis=axis, keepdims=True)
    return (x - m) / jnp.sqrt(v + eps)

def _scatter_add(tgt, idx, src, axis=0):
    return tgt.at[idx].add(src)

def _segment_sum(src, seg, n):
    return jax.ops.segment_sum(src, seg, n)
kernel_name = 'mk_gps_d2_gnn_r16_9e2c30'

def setup_inputs(seed: int=0):
    np.random.seed(seed)
    _w = jnp.asarray

    def _rec_inputs():
        import jax
        import jax.numpy as jnp
        _gk = jax.random.key(seed)
        x = -8.776e-05 + 1 * jax.random.normal(jax.random.fold_in(_gk, 1), (3125, 256), jnp.float32)
        src = jax.random.randint(jax.random.fold_in(_gk, 2), (100000,), 0, 3125, jnp.int32)
        dst = jnp.minimum((3125 * jax.random.uniform(jax.random.fold_in(_gk, 3), (100000,)) ** 2.0).astype(jnp.int32), 49999)
        _o = jnp.argsort(dst, stable=True)
        src = src[_o]
        dst = dst[_o]
        return (x, src, dst)
    x, src, dst = _rec_inputs()

    def _L0_gnn_setup():
        import jax, jax.numpy as jnp
        import numpy as np
        N, E, D, H, DK, DV, L, HUS = (1250, 20000, 256, 8, 32, 32, 2, 1024)

        def _layer_norm(x, g, b, eps=1e-05):
            mu = jnp.mean(x, axis=-1, keepdims=True)
            var = jnp.mean((x - mu) ** 2, axis=-1, keepdims=True)
            return (x - mu) * jax.lax.rsqrt(var + eps) * g + b

        def _ga_layer(h, src, dst, Wq, Wk, Wv, Wo, g, b):
            n = h.shape[0]
            q = (h @ Wq).reshape(n, H, DK)
            k = (h @ Wk).reshape(n, H, DK)
            v = (h @ Wv).reshape(n, H, DV)
            e = jnp.sum(q[dst] * k[src], axis=-1) / np.sqrt(DK).astype(np.float32)
            m = jax.ops.segment_max(e, dst, num_segments=n)
            a = jnp.exp(e - m[dst])
            z = jax.ops.segment_sum(a, dst, num_segments=n)
            alpha = a / (z[dst] + 1e-09)
            msg = v[src] * alpha[:, :, None]
            agg = jax.ops.segment_sum(msg, dst, num_segments=n).reshape(n, H * DV)
            out = agg @ Wo
            return _layer_norm(out + h, g, b)
        key = jax.random.key(seed)
        ks = jax.random.split(key, 12)
        s = 0.02
        return {'h': jax.random.normal(ks[0], (N, D), jnp.float32), 'src': jax.random.randint(ks[1], (E,), 0, N, jnp.int32), 'dst': jax.random.randint(ks[2], (E,), 0, N, jnp.int32), 'Wq': jax.random.normal(ks[3], (L, D, H * DK), jnp.float32) * s, 'Wk': jax.random.normal(ks[4], (L, D, H * DK), jnp.float32) * s, 'Wv': jax.random.normal(ks[5], (L, D, H * DV), jnp.float32) * s, 'Wo': jax.random.normal(ks[6], (L, H * DV, D), jnp.float32) * s, 'ln_g': jnp.ones((L, D), jnp.float32), 'ln_b': jnp.zeros((L, D), jnp.float32), 'w1': jax.random.normal(ks[7], (D, HUS), jnp.float32) * s, 'b1': jnp.zeros((HUS,), jnp.float32), 'w2': jax.random.normal(ks[8], (HUS, D), jnp.float32) * s, 'b2': jnp.zeros((D,), jnp.float32)}
    _L0_gnn_all = _L0_gnn_setup()
    _L0_gnn_in = {k: v for k, v in _L0_gnn_all.items() if k in ('Wq', 'Wk', 'Wv', 'Wo', 'ln_g', 'ln_b', 'w1', 'b1', 'w2', 'b2')}
    del _L0_gnn_all

    def _L0_mix_setup():
        import jax, jax.numpy as jnp
        import numpy as np
        C_CURV = 1.0
        MIN_NORM = 1e-15
        BALL_EPS = 1e-05
        ATT_EPS = 1e-15
        DIM = 32

        def _norm(x):
            return jnp.clip(jnp.linalg.norm(x, axis=-1, keepdims=True), MIN_NORM)

        def proj(x, c):
            maxnorm = (1.0 - BALL_EPS) / jnp.sqrt(c)
            n = _norm(x)
            return jnp.where(n > maxnorm, x / n * maxnorm, x)

        def expmap0(u, c):
            sc = jnp.sqrt(c)
            n = _norm(u)
            return jnp.tanh(sc * n) * u / (sc * n)

        def logmap0(p, c):
            sc = jnp.sqrt(c)
            n = _norm(p)
            return jnp.arctanh(jnp.clip(sc * n, -1.0 + 1e-07, 1.0 - 1e-07)) * p / (sc * n)

        def mobius_add(x, y, c):
            x2 = jnp.sum(x * x, -1, keepdims=True)
            y2 = jnp.sum(y * y, -1, keepdims=True)
            xy = jnp.sum(x * y, -1, keepdims=True)
            num = (1 + 2 * c * xy + c * y2) * x + (1 - c * x2) * y
            den = 1 + 2 * c * xy + c * c * x2 * y2
            return num / jnp.clip(den, MIN_NORM)

        def conv1d(x, w, pad, groups=1):
            return jax.lax.conv_general_dilated(x, w, (1,), [(pad, pad)], dimension_numbers=('NCH', 'OIH', 'NCH'), feature_group_count=groups)

        def batchnorm(x, gamma, beta):
            mean = jnp.mean(x, axis=(0, 2), keepdims=True)
            var = jnp.var(x, axis=(0, 2), keepdims=True)
            xn = (x - mean) * jax.lax.rsqrt(var + 1e-05)
            return gamma[None, :, None] * xn + beta[None, :, None]

        def _reference_tuple_inner(x, w_qkv, bn_gamma, bn_beta, w_dw, w_pw, w_res, b_res):
            c = C_CURV
            h = logmap0(proj(x, c), c)
            h = jnp.transpose(h, (1, 2, 0))
            h = conv1d(h, w_qkv, pad=2)
            h = batchnorm(h, bn_gamma, bn_beta)
            h = jax.nn.relu(jnp.transpose(h, (2, 0, 1)))
            qkv = proj(expmap0(h, c), c)
            t = jnp.transpose(logmap0(proj(qkv, c), c), (1, 2, 0))
            s = conv1d(t, w_dw, pad=2, groups=t.shape[1])
            s = conv1d(s, w_pw, pad=0, groups=t.shape[1] // DIM)
            cat = jnp.concatenate([t, s], axis=1)
            ai = proj(expmap0(jnp.transpose(cat, (2, 0, 1)), c), c)
            t2 = logmap0(proj(ai, c), c)
            L, N, C2 = t2.shape
            g = C2 // (3 * DIM)
            qkv3 = jnp.transpose(t2, (1, 2, 0)).reshape(N, g, 3 * DIM, L)
            q, k, v = jnp.split(qkv3, 3, axis=2)
            q = jax.nn.relu(q)
            k = jax.nn.relu(k)
            vk = jnp.einsum('ngdl,ngel->ngde', v, k)
            out = jnp.einsum('ngde,ngdl->ngdl', vk, q)
            out = out / (jnp.sum(v, -1, keepdims=True) + ATT_EPS)
            out = jnp.transpose(out.reshape(N, g * DIM, L), (2, 0, 1))
            fx_h = proj(expmap0(out, c), c)
            ft = jnp.transpose(logmap0(proj(fx_h, c), c), (1, 2, 0))
            ft = conv1d(ft, w_res, pad=0) + b_res[None, :, None]
            fx = proj(expmap0(jnp.transpose(ft, (2, 0, 1)), c), c)
            residual = mobius_add(fx, x, c)
            return (fx, residual)
        key = jax.random.key(seed)
        ks = jax.random.split(key, 6)
        L, N, C, TD = (128, 16, 256, 256)
        x = jax.random.normal(ks[0], (L, N, C), jnp.float32) * 0.05
        w_qkv = jax.random.normal(ks[1], (3 * TD, C, 5), jnp.float32) / np.sqrt(C * 5)
        bn_gamma = jnp.ones((3 * TD,), jnp.float32)
        bn_beta = jnp.zeros((3 * TD,), jnp.float32)
        w_dw = jax.random.normal(ks[2], (3 * TD, 1, 5), jnp.float32) / np.sqrt(5.0)
        w_pw = jax.random.normal(ks[3], (3 * TD, DIM, 1), jnp.float32) / np.sqrt(DIM)
        w_res = jax.random.normal(ks[4], (C, 2 * TD, 1), jnp.float32) / np.sqrt(2 * TD)
        b_res = jnp.zeros((C,), jnp.float32)
        return {'x': x, 'w_qkv': w_qkv, 'bn_gamma': bn_gamma, 'bn_beta': bn_beta, 'w_dw': w_dw, 'w_pw': w_pw, 'w_res': w_res, 'b_res': b_res}
    _L0_mix_all = _L0_mix_setup()
    _L0_mix_in = {k: v for k, v in _L0_mix_all.items() if k in ('w_qkv', 'bn_gamma', 'bn_beta', 'w_dw', 'w_pw', 'w_res', 'b_res')}
    del _L0_mix_all

    def _L0_ffn_setup():
        import jax, jax.numpy as jnp
        import numpy as np
        B, S, D = (8, 256, 256)
        H = 4 * D
        CAPACITY = 0.5
        key = jax.random.key(seed)
        ks = jax.random.split(key, 6)
        x = jax.random.normal(ks[0], (B, S, D), dtype=jnp.float32)
        attention_mask = jnp.zeros((B, 1, 1, S), dtype=jnp.float32)
        wr = jax.random.normal(ks[1], (D, 1), dtype=jnp.float32) * 0.02
        br = jnp.zeros((1,), dtype=jnp.float32)
        w1 = jax.random.normal(ks[2], (D, H), dtype=jnp.float32) * 0.02
        b1 = jnp.zeros((H,), dtype=jnp.float32)
        w2 = jax.random.normal(ks[3], (H, D), dtype=jnp.float32) * 0.02
        b2 = jnp.zeros((D,), dtype=jnp.float32)
        return {'x': x, 'attention_mask': attention_mask, 'wr': wr, 'br': br, 'w1': w1, 'b1': b1, 'w2': w2, 'b2': b2}
    _L0_ffn_all = _L0_ffn_setup()
    _L0_ffn_in = {k: v for k, v in _L0_ffn_all.items() if k in ('attention_mask', 'wr', 'br', 'w1', 'b1', 'w2', 'b2')}
    del _L0_ffn_all

    def _L1_gnn_setup():
        import jax, jax.numpy as jnp
        import numpy as np
        N_NODES = 3125
        key = jax.random.key(seed)
        k1, k2, k3 = jax.random.split(key, 3)
        x = jax.random.normal(k1, (N_NODES, 256), dtype=jnp.float32)
        W = jax.random.normal(k2, (256, 256), dtype=jnp.float32) * (1.0 / np.sqrt(256))
        edge_index = jax.random.randint(k3, (2, 100000), 0, N_NODES, dtype=jnp.int64)
        return {'x': x, 'W': W, 'edge_index': edge_index}
    _L1_gnn_all = _L1_gnn_setup()
    _L1_gnn_in = {k: v for k, v in _L1_gnn_all.items() if k in ('W',)}
    del _L1_gnn_all

    def _L1_mix_setup():
        import jax, jax.numpy as jnp
        import numpy as np
        EMB, HEADS, DEPTH, SEQ, BATCH = (256, 8, 4, 512, 4)
        DH = EMB // HEADS
        FF = 4 * EMB
        EPS = 1e-05

        def _layernorm(x, g, b):
            mu = x.mean(-1, keepdims=True)
            var = ((x - mu) ** 2).mean(-1, keepdims=True)
            return (x - mu) * jax.lax.rsqrt(var + EPS) * g + b

        def _linear_attn(x, Wq, Wk, Wv, Wo, bo):
            b, n, dm = x.shape
            split = lambda t: t.reshape(b, n, HEADS, DH).transpose(0, 2, 1, 3)
            scale = DH ** (-0.25)
            q = jax.nn.softmax(split(x @ Wq) * scale, axis=-1)
            k = jax.nn.softmax(split(x @ Wk) * scale, axis=-2)
            v = split(x @ Wv)
            context = jnp.einsum('bhnd,bhne->bhde', k, v)
            out = jnp.einsum('bhnd,bhde->bhne', q, context)
            out = out.transpose(0, 2, 1, 3).reshape(b, n, dm)
            return out @ Wo + bo

        def _forward(x, Wq, Wk, Wv, Wo, bo, ln1_g, ln1_b, W1, b1, W2, b2, ln2_g, ln2_b):
            for i in range(DEPTH):
                h = _layernorm(x, ln1_g[i], ln1_b[i])
                x = x + _linear_attn(h, Wq[i], Wk[i], Wv[i], Wo[i], bo[i])
                h = _layernorm(x, ln2_g[i], ln2_b[i])
                x = x + (jax.nn.gelu(h @ W1[i] + b1[i], approximate=False) @ W2[i] + b2[i])
            return x
        key = jax.random.key(seed)
        ks = jax.random.split(key, 8)
        w = lambda k, shape: jax.random.normal(k, shape, dtype=jnp.float32) * 0.02
        D = DEPTH
        return {'x': jax.random.normal(ks[0], (BATCH, SEQ, EMB), dtype=jnp.float32), 'Wq': w(ks[1], (D, EMB, EMB)), 'Wk': w(ks[2], (D, EMB, EMB)), 'Wv': w(ks[3], (D, EMB, EMB)), 'Wo': w(ks[4], (D, EMB, EMB)), 'bo': jnp.zeros((D, EMB), jnp.float32), 'ln1_g': jnp.ones((D, EMB), jnp.float32), 'ln1_b': jnp.zeros((D, EMB), jnp.float32), 'W1': w(ks[5], (D, EMB, FF)), 'b1': jnp.zeros((D, FF), jnp.float32), 'W2': w(ks[6], (D, FF, EMB)), 'b2': jnp.zeros((D, EMB), jnp.float32), 'ln2_g': jnp.ones((D, EMB), jnp.float32), 'ln2_b': jnp.zeros((D, EMB), jnp.float32)}
    _L1_mix_all = _L1_mix_setup()
    _L1_mix_in = {k: v for k, v in _L1_mix_all.items() if k in ('Wq', 'Wk', 'Wv', 'Wo', 'bo', 'ln1_g', 'ln1_b', 'W1', 'b1', 'W2', 'b2', 'ln2_g', 'ln2_b')}
    del _L1_mix_all

    def _L1_ffn_setup():
        import jax, jax.numpy as jnp
        import numpy as np
        B, N, D = (16, 256, 256)
        NUM_EXPERTS, TOP_K, HEADS = (4, 2, 4)
        N_EDGES = 65536
        LN_EPS = 1e-05

        def _layernorm(x, g, b):
            mu = x.mean(-1, keepdims=True)
            var = ((x - mu) ** 2).mean(-1, keepdims=True)
            return (x - mu) * jax.lax.rsqrt(var + LN_EPS) * g + b

        def _forward(x, edge_index, W_gat, att_src, att_dst, b_gat, ln_gamma, ln_beta, W1, b1, W2, b2):
            Bc, Nc, Dc = x.shape
            M = Bc * Nc
            x_flat = x.reshape(M, Dc)
            h = (x_flat @ W_gat).reshape(M, HEADS, NUM_EXPERTS)
            loops = jnp.arange(M, dtype=edge_index.dtype)
            src = jnp.concatenate([edge_index[0], loops])
            dst = jnp.concatenate([edge_index[1], loops])
            a_src = (h * att_src).sum(-1)
            a_dst = (h * att_dst).sum(-1)
            e = jax.nn.leaky_relu(a_src[src] + a_dst[dst], negative_slope=0.2)
            e_max = jax.ops.segment_max(e, dst, num_segments=M)
            ee = jnp.exp(e - e_max[dst])
            denom = jax.ops.segment_sum(ee, dst, num_segments=M)
            alpha = ee / (denom[dst] + 1e-16)
            msg = h[src] * alpha[:, :, None]
            agg = jax.ops.segment_sum(msg, dst, num_segments=M).reshape(M, HEADS * NUM_EXPERTS) + b_gat
            scores = _layernorm(agg, ln_gamma, ln_beta).reshape(M, HEADS, NUM_EXPERTS).mean(1)
            scores = scores.reshape(Bc, Nc, NUM_EXPERTS)
            topk_s, topk_i = jax.lax.top_k(scores, TOP_K)
            w = jax.nn.softmax(topk_s, axis=-1)
            out = jnp.zeros_like(x)
            for ei in range(NUM_EXPERTS):
                g = jnp.where(topk_i == ei, w, 0.0).sum(-1)
                hh = jax.nn.gelu(x @ W1[ei] + b1[ei], approximate=False)
                out = out + g[..., None] * (hh @ W2[ei] + b2[ei])
            return out
        key = jax.random.key(seed)
        ks = jax.random.split(key, 8)
        s = 0.05
        return {'x': jax.random.normal(ks[0], (B, N, D), jnp.float32), 'W_gat': jax.random.normal(ks[1], (D, HEADS * NUM_EXPERTS), jnp.float32) * s, 'att_src': jax.random.normal(ks[2], (HEADS, NUM_EXPERTS), jnp.float32) * s, 'att_dst': jax.random.normal(ks[3], (HEADS, NUM_EXPERTS), jnp.float32) * s, 'b_gat': jnp.zeros((HEADS * NUM_EXPERTS,), jnp.float32), 'ln_gamma': jnp.ones((HEADS * NUM_EXPERTS,), jnp.float32), 'ln_beta': jnp.zeros((HEADS * NUM_EXPERTS,), jnp.float32), 'W1': jax.random.normal(ks[4], (NUM_EXPERTS, D, 2 * D), jnp.float32) * s, 'b1': jnp.zeros((NUM_EXPERTS, 2 * D), jnp.float32), 'W2': jax.random.normal(ks[5], (NUM_EXPERTS, 2 * D, D), jnp.float32) * s, 'b2': jnp.zeros((NUM_EXPERTS, D), jnp.float32), 'edge_index': jax.random.randint(ks[6], (2, N_EDGES), 0, B * N, jnp.int32)}
    _L1_ffn_all = _L1_ffn_setup()
    _L1_ffn_in = {k: v for k, v in _L1_ffn_all.items() if k in ('W_gat', 'att_src', 'att_dst', 'b_gat', 'ln_gamma', 'ln_beta', 'W1', 'b1', 'W2', 'b2', 'edge_index')}
    del _L1_ffn_all
    return {'x': x, 'src': src, 'dst': dst, 'L0_gnn_Wq': _L0_gnn_in['Wq'], 'L0_gnn_Wk': _L0_gnn_in['Wk'], 'L0_gnn_Wv': _L0_gnn_in['Wv'], 'L0_gnn_Wo': _L0_gnn_in['Wo'], 'L0_gnn_ln_g': _L0_gnn_in['ln_g'], 'L0_gnn_ln_b': _L0_gnn_in['ln_b'], 'L0_gnn_w1': _L0_gnn_in['w1'], 'L0_gnn_b1': _L0_gnn_in['b1'], 'L0_gnn_w2': _L0_gnn_in['w2'], 'L0_gnn_b2': _L0_gnn_in['b2'], 'L0_mix_w_qkv': _L0_mix_in['w_qkv'], 'L0_mix_bn_gamma': _L0_mix_in['bn_gamma'], 'L0_mix_bn_beta': _L0_mix_in['bn_beta'], 'L0_mix_w_dw': _L0_mix_in['w_dw'], 'L0_mix_w_pw': _L0_mix_in['w_pw'], 'L0_mix_w_res': _L0_mix_in['w_res'], 'L0_mix_b_res': _L0_mix_in['b_res'], 'L0_ffn_attention_mask': _L0_ffn_in['attention_mask'], 'L0_ffn_wr': _L0_ffn_in['wr'], 'L0_ffn_br': _L0_ffn_in['br'], 'L0_ffn_w1': _L0_ffn_in['w1'], 'L0_ffn_b1': _L0_ffn_in['b1'], 'L0_ffn_w2': _L0_ffn_in['w2'], 'L0_ffn_b2': _L0_ffn_in['b2'], 'L1_gnn_W': _L1_gnn_in['W'], 'L1_mix_Wq': _L1_mix_in['Wq'], 'L1_mix_Wk': _L1_mix_in['Wk'], 'L1_mix_Wv': _L1_mix_in['Wv'], 'L1_mix_Wo': _L1_mix_in['Wo'], 'L1_mix_bo': _L1_mix_in['bo'], 'L1_mix_ln1_g': _L1_mix_in['ln1_g'], 'L1_mix_ln1_b': _L1_mix_in['ln1_b'], 'L1_mix_W1': _L1_mix_in['W1'], 'L1_mix_b1': _L1_mix_in['b1'], 'L1_mix_W2': _L1_mix_in['W2'], 'L1_mix_b2': _L1_mix_in['b2'], 'L1_mix_ln2_g': _L1_mix_in['ln2_g'], 'L1_mix_ln2_b': _L1_mix_in['ln2_b'], 'L1_ffn_W_gat': _L1_ffn_in['W_gat'], 'L1_ffn_att_src': _L1_ffn_in['att_src'], 'L1_ffn_att_dst': _L1_ffn_in['att_dst'], 'L1_ffn_b_gat': _L1_ffn_in['b_gat'], 'L1_ffn_ln_gamma': _L1_ffn_in['ln_gamma'], 'L1_ffn_ln_beta': _L1_ffn_in['ln_beta'], 'L1_ffn_W1': _L1_ffn_in['W1'], 'L1_ffn_b1': _L1_ffn_in['b1'], 'L1_ffn_W2': _L1_ffn_in['W2'], 'L1_ffn_b2': _L1_ffn_in['b2'], 'L1_ffn_edge_index': _L1_ffn_in['edge_index']}

def reference(x, src, dst, L0_gnn_Wq, L0_gnn_Wk, L0_gnn_Wv, L0_gnn_Wo, L0_gnn_ln_g, L0_gnn_ln_b, L0_gnn_w1, L0_gnn_b1, L0_gnn_w2, L0_gnn_b2, L0_mix_w_qkv, L0_mix_bn_gamma, L0_mix_bn_beta, L0_mix_w_dw, L0_mix_w_pw, L0_mix_w_res, L0_mix_b_res, L0_ffn_attention_mask, L0_ffn_wr, L0_ffn_br, L0_ffn_w1, L0_ffn_b1, L0_ffn_w2, L0_ffn_b2, L1_gnn_W, L1_mix_Wq, L1_mix_Wk, L1_mix_Wv, L1_mix_Wo, L1_mix_bo, L1_mix_ln1_g, L1_mix_ln1_b, L1_mix_W1, L1_mix_b1, L1_mix_W2, L1_mix_b2, L1_mix_ln2_g, L1_mix_ln2_b, L1_ffn_W_gat, L1_ffn_att_src, L1_ffn_att_dst, L1_ffn_b_gat, L1_ffn_ln_gamma, L1_ffn_ln_beta, L1_ffn_W1, L1_ffn_b1, L1_ffn_W2, L1_ffn_b2, L1_ffn_edge_index):
    import jax
    import jax.numpy as jnp

    def _L0_gnn_ref(h, src, dst, Wq, Wk, Wv, Wo, ln_g, ln_b, w1, b1, w2, b2):
        import jax, jax.numpy as jnp
        import numpy as np
        N, E, D, H, DK, DV, L, HUS = (1250, 20000, 256, 8, 32, 32, 2, 1024)

        def _layer_norm(x, g, b, eps=1e-05):
            mu = jnp.mean(x, axis=-1, keepdims=True)
            var = jnp.mean((x - mu) ** 2, axis=-1, keepdims=True)
            return (x - mu) * jax.lax.rsqrt(var + eps) * g + b

        def _ga_layer(h, src, dst, Wq, Wk, Wv, Wo, g, b):
            n = h.shape[0]
            q = (h @ Wq).reshape(n, H, DK)
            k = (h @ Wk).reshape(n, H, DK)
            v = (h @ Wv).reshape(n, H, DV)
            e = jnp.sum(q[dst] * k[src], axis=-1) / np.sqrt(DK).astype(np.float32)
            m = jax.ops.segment_max(e, dst, num_segments=n)
            a = jnp.exp(e - m[dst])
            z = jax.ops.segment_sum(a, dst, num_segments=n)
            alpha = a / (z[dst] + 1e-09)
            msg = v[src] * alpha[:, :, None]
            agg = jax.ops.segment_sum(msg, dst, num_segments=n).reshape(n, H * DV)
            out = agg @ Wo
            return _layer_norm(out + h, g, b)
        for l in range(Wq.shape[0]):
            h = _ga_layer(h, src, dst, Wq[l], Wk[l], Wv[l], Wo[l], ln_g[l], ln_b[l])
        return jax.nn.relu(h @ w1 + b1) @ w2 + b2

    def _L0_mix_ref(x, w_qkv, bn_gamma, bn_beta, w_dw, w_pw, w_res, b_res):
        import jax, jax.numpy as jnp
        import numpy as np
        C_CURV = 1.0
        MIN_NORM = 1e-15
        BALL_EPS = 1e-05
        ATT_EPS = 1e-15
        DIM = 32

        def _norm(x):
            return jnp.clip(jnp.linalg.norm(x, axis=-1, keepdims=True), MIN_NORM)

        def proj(x, c):
            maxnorm = (1.0 - BALL_EPS) / jnp.sqrt(c)
            n = _norm(x)
            return jnp.where(n > maxnorm, x / n * maxnorm, x)

        def expmap0(u, c):
            sc = jnp.sqrt(c)
            n = _norm(u)
            return jnp.tanh(sc * n) * u / (sc * n)

        def logmap0(p, c):
            sc = jnp.sqrt(c)
            n = _norm(p)
            return jnp.arctanh(jnp.clip(sc * n, -1.0 + 1e-07, 1.0 - 1e-07)) * p / (sc * n)

        def mobius_add(x, y, c):
            x2 = jnp.sum(x * x, -1, keepdims=True)
            y2 = jnp.sum(y * y, -1, keepdims=True)
            xy = jnp.sum(x * y, -1, keepdims=True)
            num = (1 + 2 * c * xy + c * y2) * x + (1 - c * x2) * y
            den = 1 + 2 * c * xy + c * c * x2 * y2
            return num / jnp.clip(den, MIN_NORM)

        def conv1d(x, w, pad, groups=1):
            return jax.lax.conv_general_dilated(x, w, (1,), [(pad, pad)], dimension_numbers=('NCH', 'OIH', 'NCH'), feature_group_count=groups)

        def batchnorm(x, gamma, beta):
            mean = jnp.mean(x, axis=(0, 2), keepdims=True)
            var = jnp.var(x, axis=(0, 2), keepdims=True)
            xn = (x - mean) * jax.lax.rsqrt(var + 1e-05)
            return gamma[None, :, None] * xn + beta[None, :, None]

        def _reference_tuple_inner(x, w_qkv, bn_gamma, bn_beta, w_dw, w_pw, w_res, b_res):
            c = C_CURV
            h = logmap0(proj(x, c), c)
            h = jnp.transpose(h, (1, 2, 0))
            h = conv1d(h, w_qkv, pad=2)
            h = batchnorm(h, bn_gamma, bn_beta)
            h = jax.nn.relu(jnp.transpose(h, (2, 0, 1)))
            qkv = proj(expmap0(h, c), c)
            t = jnp.transpose(logmap0(proj(qkv, c), c), (1, 2, 0))
            s = conv1d(t, w_dw, pad=2, groups=t.shape[1])
            s = conv1d(s, w_pw, pad=0, groups=t.shape[1] // DIM)
            cat = jnp.concatenate([t, s], axis=1)
            ai = proj(expmap0(jnp.transpose(cat, (2, 0, 1)), c), c)
            t2 = logmap0(proj(ai, c), c)
            L, N, C2 = t2.shape
            g = C2 // (3 * DIM)
            qkv3 = jnp.transpose(t2, (1, 2, 0)).reshape(N, g, 3 * DIM, L)
            q, k, v = jnp.split(qkv3, 3, axis=2)
            q = jax.nn.relu(q)
            k = jax.nn.relu(k)
            vk = jnp.einsum('ngdl,ngel->ngde', v, k)
            out = jnp.einsum('ngde,ngdl->ngdl', vk, q)
            out = out / (jnp.sum(v, -1, keepdims=True) + ATT_EPS)
            out = jnp.transpose(out.reshape(N, g * DIM, L), (2, 0, 1))
            fx_h = proj(expmap0(out, c), c)
            ft = jnp.transpose(logmap0(proj(fx_h, c), c), (1, 2, 0))
            ft = conv1d(ft, w_res, pad=0) + b_res[None, :, None]
            fx = proj(expmap0(jnp.transpose(ft, (2, 0, 1)), c), c)
            residual = mobius_add(fx, x, c)
            return (fx, residual)
        return _reference_tuple_inner(x, w_qkv, bn_gamma, bn_beta, w_dw, w_pw, w_res, b_res)[0]

    def _L0_ffn_ref(x, attention_mask, wr, br, w1, b1, w2, b2):
        import jax, jax.numpy as jnp
        import numpy as np
        B, S, D = (8, 256, 256)
        H = 4 * D
        CAPACITY = 0.5
        b, s, d = x.shape
        weights = (jnp.einsum('bsd,do->bso', x, wr) + br)[..., 0]
        k = max(1, int(CAPACITY * s))
        kk = k - 1 if k > 1 else 1
        _, idx = jax.lax.top_k(weights, k)
        sel_idx = idx[:, :kk]
        sel = jnp.take_along_axis(x, sel_idx[:, :, None], axis=1)
        h = jax.nn.gelu(jnp.einsum('bkd,dh->bkh', sel, w1) + b1)
        y = jnp.einsum('bkh,hd->bkd', h, w2) + b2
        w_sel = jnp.take_along_axis(weights, sel_idx, axis=1)
        y = y * w_sel[..., None]
        batch_idx = jnp.arange(b)[:, None]
        processed = jnp.zeros_like(x).at[batch_idx, sel_idx].set(y)
        return processed + x

    def _L1_gnn_ref(x, W, edge_index):
        import jax, jax.numpy as jnp
        import numpy as np
        N_NODES = 3125
        N = x.shape[0]
        src, dst = (edge_index[0], edge_index[1])
        h = x @ W
        deg = jax.ops.segment_sum(jnp.ones_like(dst, dtype=h.dtype), dst, num_segments=N)
        deg_inv_sqrt = jnp.where(deg > 0, jax.lax.rsqrt(jnp.maximum(deg, 1)), 0.0)
        norm = deg_inv_sqrt[src] * deg_inv_sqrt[dst]
        msgs = h[src] * norm[:, None]
        out = jax.ops.segment_sum(msgs, dst, num_segments=N)
        return out

    def _L1_mix_ref(x, Wq, Wk, Wv, Wo, bo, ln1_g, ln1_b, W1, b1, W2, b2, ln2_g, ln2_b):
        import jax, jax.numpy as jnp
        import numpy as np
        EMB, HEADS, DEPTH, SEQ, BATCH = (256, 8, 4, 512, 4)
        DH = EMB // HEADS
        FF = 4 * EMB
        EPS = 1e-05

        def _layernorm(x, g, b):
            mu = x.mean(-1, keepdims=True)
            var = ((x - mu) ** 2).mean(-1, keepdims=True)
            return (x - mu) * jax.lax.rsqrt(var + EPS) * g + b

        def _linear_attn(x, Wq, Wk, Wv, Wo, bo):
            b, n, dm = x.shape
            split = lambda t: t.reshape(b, n, HEADS, DH).transpose(0, 2, 1, 3)
            scale = DH ** (-0.25)
            q = jax.nn.softmax(split(x @ Wq) * scale, axis=-1)
            k = jax.nn.softmax(split(x @ Wk) * scale, axis=-2)
            v = split(x @ Wv)
            context = jnp.einsum('bhnd,bhne->bhde', k, v)
            out = jnp.einsum('bhnd,bhde->bhne', q, context)
            out = out.transpose(0, 2, 1, 3).reshape(b, n, dm)
            return out @ Wo + bo

        def _forward(x, Wq, Wk, Wv, Wo, bo, ln1_g, ln1_b, W1, b1, W2, b2, ln2_g, ln2_b):
            for i in range(DEPTH):
                h = _layernorm(x, ln1_g[i], ln1_b[i])
                x = x + _linear_attn(h, Wq[i], Wk[i], Wv[i], Wo[i], bo[i])
                h = _layernorm(x, ln2_g[i], ln2_b[i])
                x = x + (jax.nn.gelu(h @ W1[i] + b1[i], approximate=False) @ W2[i] + b2[i])
            return x
        return _forward(x, Wq, Wk, Wv, Wo, bo, ln1_g, ln1_b, W1, b1, W2, b2, ln2_g, ln2_b)

    def _L1_ffn_ref(x, W_gat, att_src, att_dst, b_gat, ln_gamma, ln_beta, W1, b1, W2, b2, edge_index):
        import jax, jax.numpy as jnp
        import numpy as np
        B, N, D = (16, 256, 256)
        NUM_EXPERTS, TOP_K, HEADS = (4, 2, 4)
        N_EDGES = 65536
        LN_EPS = 1e-05

        def _layernorm(x, g, b):
            mu = x.mean(-1, keepdims=True)
            var = ((x - mu) ** 2).mean(-1, keepdims=True)
            return (x - mu) * jax.lax.rsqrt(var + LN_EPS) * g + b

        def _forward(x, edge_index, W_gat, att_src, att_dst, b_gat, ln_gamma, ln_beta, W1, b1, W2, b2):
            Bc, Nc, Dc = x.shape
            M = Bc * Nc
            x_flat = x.reshape(M, Dc)
            h = (x_flat @ W_gat).reshape(M, HEADS, NUM_EXPERTS)
            loops = jnp.arange(M, dtype=edge_index.dtype)
            src = jnp.concatenate([edge_index[0], loops])
            dst = jnp.concatenate([edge_index[1], loops])
            a_src = (h * att_src).sum(-1)
            a_dst = (h * att_dst).sum(-1)
            e = jax.nn.leaky_relu(a_src[src] + a_dst[dst], negative_slope=0.2)
            e_max = jax.ops.segment_max(e, dst, num_segments=M)
            ee = jnp.exp(e - e_max[dst])
            denom = jax.ops.segment_sum(ee, dst, num_segments=M)
            alpha = ee / (denom[dst] + 1e-16)
            msg = h[src] * alpha[:, :, None]
            agg = jax.ops.segment_sum(msg, dst, num_segments=M).reshape(M, HEADS * NUM_EXPERTS) + b_gat
            scores = _layernorm(agg, ln_gamma, ln_beta).reshape(M, HEADS, NUM_EXPERTS).mean(1)
            scores = scores.reshape(Bc, Nc, NUM_EXPERTS)
            topk_s, topk_i = jax.lax.top_k(scores, TOP_K)
            w = jax.nn.softmax(topk_s, axis=-1)
            out = jnp.zeros_like(x)
            for ei in range(NUM_EXPERTS):
                g = jnp.where(topk_i == ei, w, 0.0).sum(-1)
                hh = jax.nn.gelu(x @ W1[ei] + b1[ei], approximate=False)
                out = out + g[..., None] * (hh @ W2[ei] + b2[ei])
            return out
        return _forward(x, edge_index, W_gat, att_src, att_dst, b_gat, ln_gamma, ln_beta, W1, b1, W2, b2)
    edge_index = jnp.stack([src, dst])
    xn = _layernorm(x, axis=-1)
    x = x + _L0_gnn_ref(xn, src, dst, L0_gnn_Wq, L0_gnn_Wk, L0_gnn_Wv, L0_gnn_Wo, L0_gnn_ln_g, L0_gnn_ln_b, L0_gnn_w1, L0_gnn_b1, L0_gnn_w2, L0_gnn_b2) + _L0_mix_ref(xn[None], L0_mix_w_qkv, L0_mix_bn_gamma, L0_mix_bn_beta, L0_mix_w_dw, L0_mix_w_pw, L0_mix_w_res, L0_mix_b_res)[0]
    x = x + _L0_ffn_ref(_layernorm(x, axis=-1)[None], L0_ffn_attention_mask, L0_ffn_wr, L0_ffn_br, L0_ffn_w1, L0_ffn_b1, L0_ffn_w2, L0_ffn_b2)[0]
    xn = _layernorm(x, axis=-1)
    x = x + _L1_gnn_ref(xn, L1_gnn_W, edge_index) + _L1_mix_ref(xn[None], L1_mix_Wq, L1_mix_Wk, L1_mix_Wv, L1_mix_Wo, L1_mix_bo, L1_mix_ln1_g, L1_mix_ln1_b, L1_mix_W1, L1_mix_b1, L1_mix_W2, L1_mix_b2, L1_mix_ln2_g, L1_mix_ln2_b)[0]
    x = x + _L1_ffn_ref(_layernorm(x, axis=-1)[None], L1_ffn_W_gat, L1_ffn_att_src, L1_ffn_att_dst, L1_ffn_b_gat, L1_ffn_ln_gamma, L1_ffn_ln_beta, L1_ffn_W1, L1_ffn_b1, L1_ffn_W2, L1_ffn_b2, L1_ffn_edge_index)[0]
    return x

_drawn_inputs = setup_inputs


def setup_inputs(seed=0):
    import zlib

    import numpy as np

    out = dict(_drawn_inputs(seed))
    spreads = {'L0_gnn_ln_g': (1.0, 0.2),
     'L0_gnn_ln_b': (0.0, 0.397),
     'L0_gnn_b1': (0.0, 0.1),
     'L0_gnn_b2': (0.0, 0.1),
     'L0_mix_bn_gamma': (1.0, 0.6),
     'L0_mix_bn_beta': (0.0, 0.485),
     'L0_mix_b_res': (0.0, 0.349),
     'L0_ffn_b1': (0.0, 0.8),
     'L0_ffn_b2': (0.0, 0.8),
     'L1_mix_bo': (0.0, 0.1),
     'L1_mix_ln1_g': (1.0, 0.6),
     'L1_mix_ln1_b': (0.0, 0.8),
     'L1_mix_b1': (0.0, 0.326),
     'L1_mix_b2': (0.0, 0.1),
     'L1_mix_ln2_g': (1.0, 0.6),
     'L1_mix_ln2_b': (0.0, 0.8),
     'L1_ffn_b_gat': (0.0, 0.297),
     'L1_ffn_ln_gamma': (1.0, 0.6),
     'L1_ffn_ln_beta': (0.0, 0.76),
     'L1_ffn_b1': (0.0, 0.42),
     'L1_ffn_b2': (0.0, 0.32)}
    factors = {'L0_gnn_Wq': 8.0,
     'L0_gnn_Wk': 8.0,
     'L0_gnn_Wv': 8.0,
     'L0_gnn_Wo': 8.0,
     'L0_mix_w_dw': 7.091,
     'L0_mix_w_pw': 7.033,
     'L0_ffn_wr': 4.183,
     'L0_ffn_w1': 5.469,
     'L0_ffn_w2': 5.035,
     'L1_mix_Wq': 8.0,
     'L1_mix_Wk': 8.0,
     'L1_mix_Wv': 2.943,
     'L1_mix_Wo': 3.12,
     'L1_ffn_att_src': 29.467,
     'L1_ffn_att_dst': 174.089}
    for name, (base, spread) in spreads.items():
        noise = np.random.default_rng([zlib.crc32(name.encode()), seed]).standard_normal(out[name].shape)
        drawn = base * np.exp(spread * noise) if base else spread * noise
        out[name] = jnp.asarray(drawn.astype(out[name].dtype))
    for name, factor in factors.items():
        out[name] = (out[name] * factor).astype(out[name].dtype)
    return out
```

```python
from contextlib import ExitStack, contextmanager
import math

import numpy as np
import concourse.bass as bass
from concourse import mybir

F32 = mybir.dt.float32
I32 = mybir.dt.int32
ALU = mybir.AluOpType
ACT = mybir.ActivationFunctionType
AX = mybir.AxisListType.X

N, D, E = 3125, 256, 100000
P = 125
NT = N // P
ET = E // P
NV = 832
CH, CS = 16, NV // 16
HEADS, DK = 8, 32
SEQ = CS * P
G = 8
GG = 4
BIG = 1.0e30
MIX = 768
E2 = 65536
MAXNORM = float(np.float32(1.0) - np.float32(1e-5))
ATANH_MAX = 0.5 * math.log((1.0 + MAXNORM) / (1.0 - MAXNORM))


class Names:
    pass


COUNT = [0]


@contextmanager
def phase(nc, g, *names):
    COUNT[0] += 1
    sems = [nc.alloc_semaphore(f"{n}_{COUNT[0]}") for n in names]
    with nc.Block() as block:
        yield block, dict(zip(names, sems))
    nc.clear_and_free_semaphores(sems)
    nc.all_engine_barrier()


def hold(eng, sem, value):
    eng.wait_ge(sem, value)
    if not isinstance(value, int):
        eng.sem_inc(HELD[str(eng.engine)], 1)


HELD = {}


def before(eng, sem, t, unit=1):
    hold(eng, sem, (t + 1) * unit)


def this(eng, sem, t, unit=1):
    hold(eng, sem, (t + 2) * unit)


def landed(eng, sem, t, unit):
    hold(eng, sem, (t + 1) * unit)


class Steps:

    def __init__(self, eng, sem, t=None, per=0):
        self.eng, self.sem, self.t, self.per, self.n = eng, sem, t, per, 0

    def __call__(self, ins):
        self.n += 1
        ins.then_inc(self.sem, 1)
        hold(self.eng, self.sem, self.n if self.t is None else self.t * self.per + self.n)

    def end(self):
        assert self.t is None or self.n == self.per, (self.n, self.per)


def col(ap, t, width=1):
    return ap[:, bass.ds(t * width, width)]


def setup(nc, ctx):
    g = Names()
    arena = ctx.enter_context(nc.sbuf_tensor("arena", [128, 38976], F32))

    def view(off, size, parts=128):
        return arena[0:parts, off:off + size]

    g.view = view
    g.x = view(0, NT * D, P)
    g.h = view(6400, NT * D, P)
    g.b2 = view(12800, NT * D, P)
    g.b3 = view(19200, NT * D, P)
    g.b4 = view(25600, NT * D, P)
    g.b5 = view(32000, NT * D, P)
    g.score = view(19300, NV * HEADS, P)
    g.scan = view(25956, SEQ)
    g.link = view(32460, SEQ + 1)
    g.fwd = view(12800, SEQ)

    def sb(name, shape, dt=F32):
        return ctx.enter_context(nc.sbuf_tensor(name, shape, dt))

    visit_src, visit_dst = sb("visit_src", [128, NV], I32), sb("visit_dst", [128, NV], I32)
    visit_rel = sb("visit_rel", [128, NV])
    g.srcv, g.dstv, g.relv = visit_src[0:P, :], visit_dst[0:P, :], visit_rel[0:P, :]
    EC = E2 // 128
    g.srcv_e, g.dstv_e, g.dlo = visit_src[:, 0:EC], visit_dst[:, 0:EC], visit_rel[:, 0:EC].bitcast(I32)
    g.wrow = sb("wrow", [1, NV], I32)
    g.ident = sb("ident", [128, 128])
    g.iota = sb("iota", [128, 128])
    g.ones = sb("ones", [128, 128])
    g.unit = sb("unit", [P, NT])
    g.zacc = sb("zacc", [P, NT * 9])
    g.dinv = sb("dinv", [P, NT])
    g.stat = sb("stat", [P, 8 * NT])
    g.coef = sb("coef", [P, 4 * NT])
    g.eps = sb("eps", [128, 1])
    g.w1 = sb("w1", [128, 2048])
    g.w2 = sb("w2", [128, 2048])
    g.vec = sb("vec", [128, 64])
    g.brow = sb("brow", [1, 256])
    g.stage = sb("stage", [P, 512])
    g.ht = sb("ht", [128, MIX])
    g.h1 = sb("h1", [128, 2 * MIX])
    g.o = sb("o", [P, MIX])
    g.dhi = g.h1[:, 0:EC].bitcast(I32)
    g.ps = ctx.enter_context(nc.psum_tensor("ps", [128, 8, 512], F32))
    g.psT = g.ps[:, 0, 0:500]
    for e in (nc.sync, nc.scalar, nc.vector, nc.gpsimd, nc.tensor):
        HELD[str(e.engine)] = nc.alloc_semaphore("held_" + str(e.engine).split(".")[-1])
    return g


def constants(nc, g):
    with phase(nc, g, "made", "filled") as (block, s):
        it = g.view(0, 128).bitcast(I32)

        @block.gpsimd
        def _(pool):
            nc.gpsimd.iota(it, [[1, 128]], base=0, channel_multiplier=0).then_inc(s["made"], 1)
            nc.gpsimd.memset(g.ident[:, :], 0.0).then_inc(s["made"], 1)
            nc.gpsimd.memset(g.ones[:, :], 1.0).then_inc(s["made"], 1)
            nc.gpsimd.memset(g.unit[:, :], 1.0).then_inc(s["made"], 1)
            nc.gpsimd.memset(g.eps[:, :], 1e-5).then_inc(s["made"], 1)
            pool.wait_ge(s["made"], 5)
            nc.gpsimd.affine_select(out=g.ident[:, :], in_=g.ident[:, :], compare_op=ALU.not_equal, fill=1.0,
                                    base=0, pattern=[[-1, 128]], channel_multiplier=1).then_inc(s["filled"], 1)

        @block.vector
        def _(dve):
            dve.wait_ge(s["made"], 5)
            nc.vector.tensor_copy(g.iota[:, :], it).then_inc(s["filled"], 1)


def plan_visits(nc, g, src, dst, d):
    VP, VC = 104, 8
    src_rows = src.rearrange("(t e) -> t e", e=P)
    dst_rows = dst.rearrange("(t e) -> t e", e=P)
    v = g.view
    d0 = v(0, 8 * P, 100).bitcast(I32)
    last = v(1000, 8, 100)
    thr_i = v(1010, 24, 100).bitcast(I32)
    thr = v(1040, 24, 100)
    cmp = v(1070, 8 * 24, 100)
    wl = v(1270, 8, 100)
    tau_i = v(1280, 8, 100).bitcast(I32)
    tau_f = v(1290, 8, 100)
    key = v(1300, 8, 100)
    keyrow = v(1400, ET, VP)
    junk = v(2300, ET, VP)
    vi = v(3200, VC, VP).bitcast(I32)
    vf = v(3210, VC, VP)
    tau = v(3220, VC, VP)
    taui = v(3230, VC, VP).bitcast(I32)
    w = v(3240, VC, VP)
    wi = v(3250, VC, VP).bitcast(I32)
    wbase = v(3260, VC, VP)
    gs = v(4000, VC * P, VP).bitcast(I32)
    gd = v(5000, VC * P, VP).bitcast(I32)
    sf = v(6000, VC * P, VP)
    df = v(7000, VC * P, VP)
    rel = v(8000, VC * P, VP)
    inn = v(9000, VC * P, VP)
    pad = v(10000, 8, 1)
    keys = v(10100, SEQ + 2)
    with phase(nc, g, "loaded", "iotas", "step", "key_ready", "key_stored", "key_back", "tau_ready", "gathered",
               "made", "turned", "kept", "keys_stored", "keys_back", "stored", "pad_ready") as (block, s):

        @block.gpsimd
        def _(pool):
            nc.gpsimd.iota(thr_i, [[P, 24]], base=P, channel_multiplier=0).then_inc(s["iotas"], 1)
            nc.gpsimd.iota(tau_i, [[100, 8]], base=0, channel_multiplier=1).then_inc(s["iotas"], 1)
            nc.gpsimd.iota(vi, [[VP, VC]], base=0, channel_multiplier=1).then_inc(s["iotas"], 1)
            pool.wait_ge(s["tau_ready"], 1)
            for c in range(VC):
                at = bass.IndirectOffsetOnAxis(taui[:, c:c + 1], 0)
                nc.gpsimd.indirect_dma_start(gs[:, c * P:(c + 1) * P], None, src_rows, at).then_inc(s["gathered"], 16)
                nc.gpsimd.indirect_dma_start(gd[:, c * P:(c + 1) * P], None, dst_rows, at).then_inc(s["gathered"], 16)

        @block.sync
        def _(sp):
            sp.dma_start(d0.rearrange("p (k e) -> p k e", k=8),
                         dst.rearrange("(k p e) -> p k e", k=8, e=P)).then_inc(s["loaded"], 16)
            sp.wait_ge(s["key_ready"], 1)
            sp.dma_start(d.key.rearrange("(k p) -> p k", p=100), key,
                         allow_slow_non_contiguous=True).then_inc(s["key_stored"], 16)
            sp.wait_ge(s["key_stored"], 16)
            sp.dma_start(keyrow, d.key.partition_broadcast(VP)).then_inc(s["key_back"], 16)
            sp.wait_ge(s["tau_ready"], 2)
            sp.dma_start(d.w.rearrange("(c p) -> p c", p=VP), wi,
                         allow_slow_non_contiguous=True).then_inc(s["stored"], 16)
            sp.wait_ge(s["stored"], 16)
            sp.dma_start(g.wrow[:, :], d.w.rearrange("(a v) -> a v", a=1)).then_inc(s["stored"], 16)
            sp.wait_ge(s["pad_ready"], 1)
            sp.dma_start(d.keys[0:8].rearrange("(a v) -> a v", a=1), pad).then_inc(s["keys_stored"], 16)
            sp.dma_start(d.keys[8 + NV * P:16 + NV * P].rearrange("(a v) -> a v", a=1), pad).then_inc(s["keys_stored"], 16)
            sp.wait_ge(s["made"], 1)
            sp.dma_start(d.keys[8:8 + NV * P].rearrange("(c p e) -> p c e", c=VC, p=VP),
                         inn.rearrange("p (c e) -> p c e", c=VC)).then_inc(s["keys_stored"], 16)
            sp.wait_ge(s["keys_stored"], 48)
            for c in range(CH):
                sp.dma_start(keys[HEADS * c:HEADS * c + HEADS, :],
                             d.keys[7 + c * SEQ:9 + (c + 1) * SEQ].partition_broadcast(HEADS)).then_inc(s["keys_back"], 16)
            sp.wait_ge(s["stored"], 32)

        @block.vector
        def _(dve):
            step = Steps(dve, s["step"])
            V = nc.vector
            V.memset(pad, -5.0).then_inc(s["pad_ready"], 1)
            dve.wait_ge(s["iotas"], 3)
            dve.wait_ge(s["loaded"], 16)
            step(V.tensor_copy(last, d0[:, P - 1:8 * P:P]))
            step(V.tensor_copy(thr, thr_i))
            step(V.tensor_copy(tau_f, tau_i))
            step(V.tensor_copy(vf, vi))
            c3 = cmp.rearrange("p (k t) -> p k t", t=24)
            step(V.tensor_tensor(c3, last.unsqueeze(2).to_broadcast([100, 8, 24]),
                                 thr.unsqueeze(1).to_broadcast([100, 8, 24]), ALU.is_ge))
            step(V.tensor_reduce(wl, c3, AX, ALU.add))
            V.tensor_tensor(key, wl, tau_f, ALU.add).then_inc(s["key_ready"], 1)
            dve.wait_ge(s["key_back"], 16)
            for c in range(VC):
                step(V.tensor_scalar(junk[:, 0:ET - 1], keyrow[:, 0:ET - 1], vf[:, c:c + 1], 0.0, ALU.is_lt, ALU.add,
                                     accum_out=tau[:, c:c + 1]))
            V.tensor_copy(taui, tau).then_inc(s["tau_ready"], 1)
            step(V.tensor_tensor(w, vf, tau, ALU.subtract))
            step(V.tensor_scalar(wbase, w, float(P), None, ALU.mult))
            step(V.tensor_scalar(w, w, float(NT - 1), None, ALU.min))
            V.tensor_copy(wi, w).then_inc(s["tau_ready"], 1)
            dve.wait_ge(s["gathered"], 32 * VC)
            step(V.tensor_copy(sf, gs))
            step(V.tensor_copy(df, gd))
            for c in range(VC):
                a, b = c * P, (c + 1) * P
                step(V.tensor_scalar(rel[:, a:b], df[:, a:b], wbase[:, c:c + 1], None, ALU.subtract))
            step(V.tensor_scalar(inn, rel, 0.0, None, ALU.is_ge))
            step(V.scalar_tensor_tensor(inn, rel, float(P), inn, ALU.is_lt, ALU.mult))
            V.scalar_tensor_tensor(inn, df, 1.0, inn, ALU.add, ALU.mult).then_inc(s["made"], 1)
            for c in range(VC):
                dve.wait_ge(s["turned"], c + 1)
                out = slice(c * VP, (c + 1) * VP)
                b = g.ps[0:P, 2 * (c % 2), 0:512]
                V.tensor_copy(g.srcv[:, out], b[:, 0:VP])
                V.tensor_copy(g.dstv[:, out], b[:, 128:128 + VP])
                V.tensor_copy(g.relv[:, out], b[:, 256:256 + VP]).then_inc(s["kept"], 1)
            dve.wait_ge(s["keys_back"], 16 * CH)
            dve.wait_ge(s["kept"], VC)
            step(V.tensor_tensor(g.link, keys[:, 1:SEQ + 2], keys[:, 0:SEQ + 1], ALU.not_equal))
            V.tensor_scalar(g.link, g.link, -BIG, None, ALU.mult)

        @block.tensor
        def _(pe):
            pe.wait_ge(s["made"], 1)
            for c in range(VC):
                if c >= 2:
                    pe.wait_ge(s["kept"], c - 1)
                a, b = c * P, (c + 1) * P
                bank = g.ps[0:P, 2 * (c % 2), 0:512]
                nc.tensor.transpose(bank[:, 0:VP], sf[:, a:b], g.ident[0:VP, 0:VP])
                nc.tensor.transpose(bank[:, 128:128 + VP], df[:, a:b], g.ident[0:VP, 0:VP])
                nc.tensor.transpose(bank[:, 256:256 + VP], rel[:, a:b], g.ident[0:VP, 0:VP]).then_inc(s["turned"], 1)


def spill(nc, g, links, out):
    with phase(nc, g, "moved") as (block, s):
        @block.sync
        def _(sp):
            sp.dma_start(links if out else g.link, g.link if out else links).then_inc(s["moved"], 16)
            sp.wait_ge(s["moved"], 16)


def dump(nc, g, ap, out):
    with phase(nc, g, "written") as (block, s):
        @block.sync
        def _(sp):
            sp.dma_start(out.rearrange("(t p) n -> p t n", p=P),
                         ap.rearrange("p (t n) -> p t n", t=NT)).then_inc(s["written"], 16)
            sp.wait_ge(s["written"], 16)


def layernorm(nc, g, x, out, scratch, gamma=None, beta=None):
    X3, O3, S3 = (a.rearrange("p (t n) -> p t n", t=NT) for a in (x, out, scratch))
    mean, var, std, rstd = (g.stat[:, k * NT:(k + 1) * NT] for k in range(4))
    wide = [P, NT, D]
    with phase(nc, g, "step", "centred", "squared", "var_ready", "std_ready", "loaded") as (block, s):
        if gamma is not None:
            @block.sync
            def _(sp):
                sp.dma_start(g.w1[0:P, 0:D], gamma.partition_broadcast(P)).then_inc(s["loaded"], 16)
                sp.dma_start(g.w1[0:P, D:2 * D], beta.partition_broadcast(P)).then_inc(s["loaded"], 16)

        @block.vector
        def _(dve):
            step = Steps(dve, s["step"])
            V = nc.vector
            step(V.tensor_reduce(mean, X3, AX, ALU.add))
            step(V.tensor_scalar(mean, mean, 1.0 / D, None, ALU.mult))
            V.tensor_tensor(O3, X3, mean.unsqueeze(2).to_broadcast(wide), ALU.subtract).then_inc(s["centred"], 1)
            dve.wait_ge(s["squared"], 1)
            V.tensor_reduce(var, S3, AX, ALU.add).then_inc(s["var_ready"], 1)
            dve.wait_ge(s["std_ready"], 1)
            step(V.reciprocal(rstd, std))
            dve.wait_ge(s["centred"], 1)
            step(V.tensor_tensor(O3, O3, rstd.unsqueeze(2).to_broadcast(wide), ALU.mult))
            if gamma is not None:
                dve.wait_ge(s["loaded"], 32)
                step(V.tensor_tensor(O3, O3, g.w1[0:P, 0:D].unsqueeze(1).to_broadcast(wide), ALU.mult))
                step(V.tensor_tensor(O3, O3, g.w1[0:P, D:2 * D].unsqueeze(1).to_broadcast(wide), ALU.add))

        @block.scalar
        def _(act):
            act.wait_ge(s["centred"], 1)
            nc.scalar.activation(scratch, out, ACT.Square).then_inc(s["squared"], 1)
            act.wait_ge(s["var_ready"], 1)
            nc.scalar.activation(std, var, ACT.Sqrt, bias=g.eps[0:P, :], scale=1.0 / D).then_inc(s["std_ready"], 1)


def tile_pass(nc, g, src, nk, outs, loads, finish, scale=None, affine=None, hidden=None, bias=False, tables=None):
    C = nk * 128
    nj = hidden[0] // 128 if hidden else 0
    half = nj // 2
    hT = g.ht[:, 0:nk * P].rearrange("p (k r) -> p k r", r=P)
    psT = g.psT[:, 0:nk * P].rearrange("p (k r) -> p k r", r=P)
    h1 = g.h1[:, 0:8 * P].rearrange("p (j r) -> p j r", r=P)

    def up(j):
        return g.ps[:, 2 + j // half, (j % half) * P:(j % half + 1) * P]

    with phase(nc, g, "loaded", "staged", "turned", "fetched", "up_a", "up_b", "act_a", "act_b", "down",
               "stored", "written", "step") as (block, s):

        @block.sync
        def _(sp):
            for dst, dram in loads:
                sp.dma_start(dst, dram, allow_slow_non_contiguous=True).then_inc(s["loaded"], 16)
            if tables:
                n = 16 * len(tables)
                sp.sem_inc(s["written"], n)
                with sp.Fori(0, NT) as t:
                    this(sp, s["stored"], t)
                    for dram, ap in tables:
                        sp.dma_start(dram[bass.ds(t * P, P), :], ap).then_inc(s["written"], 16)
                this(sp, s["written"], NT - 1, n)

        @block.scalar
        def _(act):
            act.sem_inc(s["staged"], 1)
            act.sem_inc(s["act_a"], 1)
            act.sem_inc(s["act_b"], 1)
            if hidden:
                act.wait_ge(s["loaded"], 16 * len(loads))

            def stage(t):
                kw = {} if scale is None else {"scale": col(scale, t)}
                nc.scalar.activation(g.stage[:, 0:C], col(src, t, C), ACT.Copy, **kw).then_inc(s["staged"], 1)

            def round_(t, last):
                if not last:
                    this(act, s["turned"], t)
                    stage(t + 1)
                if hidden:
                    for j in range(nj):
                        if j % half == 0:
                            this(act, s["up_b"] if j else s["up_a"], t)
                            if not j:
                                before(act, s["down"], t)
                        ins = nc.scalar.activation(h1[:, j, :], up(j), hidden[1], bias=g.vec[:, j:j + 1])
                        if j % half == half - 1:
                            ins.then_inc(s["act_b"] if j == nj - 1 else s["act_a"], 1)

            stage(0)
            with act.Fori(0, NT - 1) as t:
                round_(t, False)
            round_(NT - 1, True)

        @block.tensor
        def _(pe):
            pe.sem_inc(s["turned"], 1)
            pe.sem_inc(s["up_a"], 1)
            pe.sem_inc(s["up_b"], 1)
            pe.sem_inc(s["down"], 1)

            def turn(t):
                this(pe, s["staged"], t)
                for k in range(nk):
                    ins = nc.tensor.transpose(psT[:, k, :], g.stage[:, k * 128:(k + 1) * 128], g.ident[0:P, 0:P])
                ins.then_inc(s["turned"], 1)

            def round_(t, last):
                this(pe, s["fetched"], t)
                if hidden:
                    for j in range(nj):
                        for k in range(nk):
                            ins = nc.tensor.matmul(up(j), g.w1[:, k * hidden[0] + j * 128:k * hidden[0] + (j + 1) * 128],
                                                   hT[:, k, :], start=(k == 0), stop=(k == nk - 1))
                        if j % half == half - 1:
                            ins.then_inc(s["up_b"] if j == nj - 1 else s["up_a"], 1)
                if not last:
                    turn(t + 1)
                before(pe, s["stored"], t)
                lhs = [h1[:, j, :] for j in range(nj)] if hidden else [hT[:, k, :] for k in range(nk)]
                for m, left in enumerate(lhs):
                    if hidden and m % half == 0:
                        this(pe, s["act_b"] if m else s["act_a"], t)
                    for wt, ps in outs:
                        ins = nc.tensor.matmul(ps, left, wt(m), start=(m == 0), stop=(m == len(lhs) - 1 and not bias))
                if bias:
                    for wt, ps in outs:
                        ins = nc.tensor.matmul(ps, g.ones[0:1, 0:P], g.brow[0:1, :], start=False, stop=True)
                ins.then_inc(s["down"], 1)

            pe.wait_ge(s["loaded"], 16 * len(loads))
            turn(0)
            with pe.Fori(0, NT - 1) as t:
                round_(t, False)
            round_(NT - 1, True)

        @block.vector
        def _(dve):
            dve.sem_inc(s["fetched"], 1)
            dve.sem_inc(s["stored"], 1)
            dve.wait_ge(s["loaded"], 16 * len(loads))

            def fetch(t):
                this(dve, s["turned"], t)
                if affine is None:
                    ins = nc.vector.tensor_copy(hT, psT)
                else:
                    for k in range(nk):
                        ins = nc.vector.tensor_scalar(hT[:, k, :], psT[:, k, :], affine[0][:, k:k + 1],
                                                      affine[1][:, k:k + 1], ALU.mult, ALU.add)
                ins.then_inc(s["fetched"], 1)

            def round_(t, last):
                if hidden and not last:
                    this(dve, s["up_b"], t)
                    fetch(t + 1)
                this(dve, s["down"], t)
                if not hidden and not last:
                    fetch(t + 1)
                if tables:
                    before(dve, s["written"], t, 16 * len(tables))
                finish(nc.vector, t, lambda per: Steps(dve, s["step"], t, per)).then_inc(s["stored"], 1)

            fetch(0)
            with dve.Fori(0, NT - 1) as t:
                round_(t, False)
            round_(NT - 1, True)


def add_into(ps, dst, coef, width=D):
    def finish(V, t, steps):
        return V.scalar_tensor_tensor(col(dst, t, width), ps, col(coef, t), col(dst, t, width), ALU.mult, ALU.add)
    return finish


def mm_weights(buf, n):
    return lambda k: buf[:, k * n:(k + 1) * n]


def split_k(dram, nk):
    return dram.rearrange("(k p) n -> p k n", k=nk)


def w3(buf, nk, n):
    return buf[:, 0:nk * n].rearrange("p (k n) -> p k n", k=nk)


def mlp(nc, g, src, w1, b1, w2, b2, func, dst, coef, affine=None, scale=None, extra=()):
    H = w1.shape[1]
    nj = H // 128
    down = g.ps[0:P, 4, 0:D]
    loads = [(w3(g.w1, 2, H), split_k(w1, 2)), (w3(g.w2, nj, D), split_k(w2, nj)),
             (g.vec[:, 0:nj], b1.rearrange("(j p) -> p j", p=128)),
             (g.brow[:, :], b2.rearrange("(a n) -> a n", a=1))] + list(extra)
    tile_pass(nc, g, src, 2, [(mm_weights(g.w2, D), down)], loads, add_into(down, dst, coef),
              scale=scale, hidden=(H, func), bias=True, affine=affine)



def edge_scores(nc, g, q_table, k_table):
    qb = [g.w1[0:P, j * D:(j + 1) * D] for j in range(G)]
    kb = [g.w2[0:P, j * D:(j + 1) * D] for j in range(G)]
    pr = [g.h1[0:P, j * D:(j + 1) * D] for j in range(GG)]
    ix = g.ht[0:P, 0:2 * G].bitcast(I32)
    names = [f"{n}{j}" for n in ("got", "used") for j in range(G)]
    with phase(nc, g, "indexed", "reduced", *names) as (block, s):
        got = [s["got0"], s["got1"], s["got2"], s["got3"], s["got4"], s["got5"], s["got6"], s["got7"]]
        used = [s["used0"], s["used1"], s["used2"], s["used3"], s["used4"], s["used5"], s["used6"], s["used7"]]

        @block.gpsimd
        def _(pool):
            with pool.Fori(0, NV // G) as i:
                for a in range(0, G, GG):
                    for j in range(a, a + GG):
                        before(pool, used[j], i)
                    for n, at in enumerate((g.dstv, g.srcv)):
                        nc.gpsimd.tensor_copy(ix[:, n * G + a:n * G + a + GG],
                                              at[:, bass.ds(i * G + a, GG)]).then_inc(s["indexed"], 1)
                    hold(pool, s["indexed"], i * 4 + (2 if a == 0 else 4))
                    for j in range(a, a + GG):
                        nc.gpsimd.indirect_dma_start(qb[j], None, q_table,
                                                     bass.IndirectOffsetOnAxis(ix[:, j:j + 1], 0)).then_inc(got[j], 16)
                        nc.gpsimd.indirect_dma_start(kb[j], None, k_table,
                                                     bass.IndirectOffsetOnAxis(ix[:, G + j:G + j + 1], 0)).then_inc(got[j], 16)

        @block.vector
        def _(dve):
            for q in used + [s["reduced"]]:
                dve.sem_inc(q, 1)
            with dve.Fori(0, NV // G) as i:
                for a in range(0, G, GG):
                    hold(dve, s["reduced"], i * 2 + 1 + a // GG)
                    for j in range(a, a + GG):
                        landed(dve, got[j], i, 32)
                        nc.vector.tensor_tensor(pr[j - a], qb[j], kb[j], ALU.mult).then_inc(used[j], 1)
                    for j in range(a, a + GG):
                        this(dve, used[j], i)
                        ins = nc.vector.tensor_reduce(g.score[:, bass.ds(i * (G * HEADS) + j * HEADS, HEADS)],
                                                      pr[j - a].rearrange("p (h d) -> p h d", h=HEADS), AX, ALU.add)
                    ins.then_inc(s["reduced"], 1)


def segment_softmax(nc, g):
    sc4 = g.score.rearrange("p (c s h) -> p c s h", c=CH, s=CS)
    with ExitStack() as ctx:
        def sb(name, shape):
            return ctx.enter_context(nc.sbuf_tensor(name, shape, F32))
        st = g.o[0:P, 0:128]
        st2 = g.h1[:, 0:P]
        fwd = g.fwd
        ends = g.w1[:, 0:2]
        rows = g.w2[0:1, 0:4 * 128]
        init = g.w1[:, 4:5]
        psA = g.ps[:, 0, 0:P]
        with phase(nc, g, "staged", "turned", "kept") as (block, s):
            @block.vector
            def _(dve):
                dve.sem_inc(s["staged"], 1)
                with dve.Fori(0, CS) as i:
                    before(dve, s["turned"], i)
                    nc.vector.tensor_copy(st.rearrange("p (c h) -> p c h", c=CH),
                                          sc4[:, :, bass.ds(i, 1), :].rearrange("p c s h -> p c (s h)")).then_inc(s["staged"], 1)

            @block.tensor
            def _(pe):
                pe.sem_inc(s["turned"], 1)
                with pe.Fori(0, CS) as i:
                    this(pe, s["staged"], i)
                    before(pe, s["kept"], i)
                    nc.tensor.transpose(psA, st, g.ident[0:P, 0:P]).then_inc(s["turned"], 1)

            @block.scalar
            def _(act):
                act.sem_inc(s["kept"], 1)
                with act.Fori(0, CS) as i:
                    this(act, s["turned"], i)
                    nc.scalar.copy(col(g.scan, i, P), psA).then_inc(s["kept"], 1)

        with phase(nc, g, "step", "put", "rowed", "carried", "turned_back") as (block, s):
            psR = g.ps[0:1, 1, 0:256]
            psC = g.ps[:, 2, 0:1]

            @block.vector
            def _(dve):
                V = nc.vector
                step = Steps(dve, s["step"])
                for n in range(2):
                    if n == 0:
                        dst, data, link = fwd, g.scan, g.link[:, 0:SEQ]
                        end = SEQ - 1
                    else:
                        dst, data, link = g.scan[:, ::-1], fwd[:, ::-1], g.link[:, 1:SEQ + 1][:, ::-1]
                        end = 0
                    step(V.tensor_reduce(ends[:, 0:1], g.link[:, n:SEQ + n], AX, ALU.min))
                    step(V.tensor_tensor_scan(dst, link, data, -BIG, ALU.add, ALU.max))
                    tail = fwd[:, end:end + 1] if n == 0 else g.scan[:, end:end + 1]
                    V.tensor_copy(ends[:, 1:2], tail).then_inc(s["put"], 1)
                    dve.wait_ge(s["rowed"], n + 1)
                    step(V.tensor_copy(rows[:, 0:256], psR))
                    step(V.memset(rows[:, 384:512], -BIG))
                    for h in range(HEADS):
                        a = rows[0:1, h:128:HEADS]
                        b = rows[0:1, 128 + h:256:HEADS]
                        o = rows[0:1, 256 + h:384:HEADS]
                        if n:
                            a, b, o = a[:, ::-1], b[:, ::-1], o[:, ::-1]
                        step(V.tensor_tensor_scan(o, a, b, -BIG, ALU.add, ALU.max))
                    if n == 0:
                        V.tensor_copy(rows[:, 384 + HEADS:512], rows[:, 256:384 - HEADS]).then_inc(s["carried"], 1)
                    else:
                        V.tensor_copy(rows[:, 384:512 - HEADS], rows[:, 256 + HEADS:384]).then_inc(s["carried"], 1)
                    dve.wait_ge(s["turned_back"], n + 1)
                    step(V.tensor_copy(init[:, :], psC))
                    if n == 0:
                        step(V.tensor_tensor_scan(fwd, link, data, init[:, :], ALU.add, ALU.max))
                    else:
                        step(V.tensor_tensor_scan(dst, link, data, init[:, :], ALU.add, ALU.max))

            @block.tensor
            def _(pe):
                for n in range(2):
                    pe.wait_ge(s["put"], n + 1)
                    nc.tensor.transpose(psR[:, 0:128], ends[:, 0:1], g.ident[:, :])
                    nc.tensor.transpose(psR[:, 128:256], ends[:, 1:2], g.ident[:, :]).then_inc(s["rowed"], 1)
                    pe.wait_ge(s["carried"], n + 1)
                    nc.tensor.matmul(psC, rows[0:1, 384:512], g.ones[0:1, 0:1], start=True, stop=True).then_inc(s["turned_back"], 1)

        with phase(nc, g, "staged", "turned", "kept", "maxed") as (block, s):
            psB = g.ps[0:P, 0, 0:128]
            psM = g.ps[0:P, 1, 0:128]
            @block.scalar
            def _(act):
                act.sem_inc(s["staged"], 1)
                with act.Fori(0, CS) as i:
                    before(act, s["turned"], i)
                    nc.scalar.copy(st2, col(g.scan, i, P)).then_inc(s["staged"], 1)

            @block.tensor
            def _(pe):
                pe.sem_inc(s["turned"], 1)
                with pe.Fori(0, CS) as i:
                    this(pe, s["staged"], i)
                    before(pe, s["kept"], i)
                    nc.tensor.transpose(psB, st2, g.ident[:, :]).then_inc(s["turned"], 1)

            @block.vector
            def _(dve):
                dve.sem_inc(s["kept"], 1)
                with dve.Fori(0, CS) as i:
                    this(dve, s["turned"], i)
                    sl = sc4[:, :, bass.ds(i, 1), :].rearrange("p c s h -> p c (s h)")
                    nc.vector.tensor_tensor(sl, sl, psB.rearrange("p (c h) -> p c h", c=CH), ALU.subtract).then_inc(s["kept"], 1)

        with phase(nc, g, "done") as (block, s):
            @block.scalar
            def _(act):
                nc.scalar.activation(g.score, g.score, ACT.Exp, scale=1.0 / math.sqrt(DK)).then_inc(s["done"], 1)
                act.wait_ge(s["done"], 1)


def edge_sums(nc, g, table, acc, weighted):
    ncol = D + 9 if weighted else D
    vb = [g.w1[0:P, j * D:(j + 1) * D] for j in range(G)]
    ms = [g.scan[0:P, j * (D + 9):(j + 1) * (D + 9)] for j in range(G)] if weighted else vb
    oh = [g.w2[0:P, j * P:(j + 1) * P] for j in range(G)]
    ix = g.ht[0:P, 0:G].bitcast(I32)
    names = [f"{n}{j}" for n in ("got", "hot", "weighed", "summed", "added") for j in range(G)]
    with phase(nc, g, "indexed", "zeroed", "side", *names) as (block, s):
        got = [s["got0"], s["got1"], s["got2"], s["got3"], s["got4"], s["got5"], s["got6"], s["got7"]]
        hot = [s["hot0"], s["hot1"], s["hot2"], s["hot3"], s["hot4"], s["hot5"], s["hot6"], s["hot7"]]
        weighed = [s["weighed0"], s["weighed1"], s["weighed2"], s["weighed3"], s["weighed4"], s["weighed5"], s["weighed6"], s["weighed7"]]
        summed = [s["summed0"], s["summed1"], s["summed2"], s["summed3"], s["summed4"], s["summed5"], s["summed6"], s["summed7"]]
        added = [s["added0"], s["added1"], s["added2"], s["added3"], s["added4"], s["added5"], s["added6"], s["added7"]]

        @block.gpsimd
        def _(pool):
            with pool.Fori(0, NV // G) as i:
                for a in range(0, G, GG):
                    for j in range(a, a + GG):
                        before(pool, weighed[j] if weighted else summed[j], i)
                    nc.gpsimd.tensor_copy(ix[:, a:a + GG], g.srcv[:, bass.ds(i * G + a, GG)]).then_inc(s["indexed"], 1)
                    hold(pool, s["indexed"], i * 2 + (1 if a == 0 else 2))
                    for j in range(a, a + GG):
                        nc.gpsimd.indirect_dma_start(vb[j], None, table,
                                                     bass.IndirectOffsetOnAxis(ix[:, j:j + 1], 0)).then_inc(got[j], 16)

        @block.scalar
        def _(act):
            if weighted:
                act.sem_inc(s["side"], G)
                act.wait_ge(s["zeroed"], 3)
                with act.Fori(0, NV // G) as i:
                    for j in range(G):
                        before(act, summed[j], i)
                        nc.scalar.copy(ms[j][:, D:D + HEADS],
                                       g.score[:, bass.ds(i * (G * HEADS) + j * HEADS, HEADS)]).then_inc(s["side"], 1)

        @block.vector
        def _(dve):
            V = nc.vector
            V.memset(acc, 0.0).then_inc(s["zeroed"], 1)
            V.memset(g.zacc[:, :], 0.0).then_inc(s["zeroed"], 1)
            for j in range(G if weighted else 0):
                ins = V.memset(ms[j][:, D:D + 9], 1.0)
            if weighted:
                ins.then_inc(s["zeroed"], 1)
            dve.wait_ge(s["zeroed"], 3 if weighted else 2)
            for q in hot + weighed + added:
                dve.sem_inc(q, 1)

            def weigh(i, j):
                before(dve, summed[j], i)
                V.tensor_scalar(oh[j], g.iota[0:P, 0:P], g.relv[:, bass.ds(i * G + j, 1)], None,
                                ALU.is_equal).then_inc(hot[j], 1)
                if weighted:
                    landed(dve, got[j], i, 16)
                    V.tensor_tensor(ms[j][:, 0:D].rearrange("p (h d) -> p h d", h=HEADS),
                                    vb[j].rearrange("p (h d) -> p h d", h=HEADS),
                                    g.score[:, bass.ds(i * (G * HEADS) + j * HEADS, HEADS)].unsqueeze(2)
                                    .to_broadcast([P, HEADS, DK]), ALU.mult).then_inc(weighed[j], 1)

            def add(i, j):
                tile = dve.value_load(g.wrow[0:1, bass.ds(i * G + j, 1)], min_val=0, max_val=NT - 1)
                this(dve, summed[j], i)
                if j:
                    this(dve, added[j - 1], i)
                else:
                    before(dve, added[G - 1], i)
                if weighted:
                    V.tensor_tensor(g.zacc[:, bass.ds(tile * 9, 9)], g.zacc[:, bass.ds(tile * 9, 9)],
                                    g.ps[0:P, j, D:D + 9], ALU.add)
                V.tensor_tensor(acc[:, bass.ds(tile * D, D)], acc[:, bass.ds(tile * D, D)],
                                g.ps[0:P, j, 0:D], ALU.add).then_inc(added[j], 1)

            with dve.Fori(0, NV // G) as i:
                for j in range(GG):
                    weigh(i, j)
                for j in range(GG, G):
                    weigh(i, j)
                    add(i, j - GG)
                for j in range(GG, G):
                    add(i, j)

        @block.tensor
        def _(pe):
            for q in summed:
                pe.sem_inc(q, 1)
            with pe.Fori(0, NV // G) as i:
                for j in range(G):
                    this(pe, hot[j], i)
                    if weighted:
                        this(pe, weighed[j], i)
                        hold(pe, s["side"], i * G + (G + j + 1))
                    else:
                        landed(pe, got[j], i, 16)
                    before(pe, added[j], i)
                    nc.tensor.matmul(g.ps[0:P, j, 0:ncol], oh[j], ms[j][:, 0:ncol],
                                     start=True, stop=True).then_inc(summed[j], 1)



def norm_factor(V, step, out, sumsq_root, limit):
    step(V.tensor_scalar(sumsq_root, sumsq_root, 1e-15, None, ALU.max))
    step(V.reciprocal(out, sumsq_root))
    step(V.tensor_scalar(out, out, limit, 1.0, ALU.mult, ALU.min))


def mix(nc, g, xn, x, w_qkv, gamma, beta, w_dw, w_pw, w_res, b_res):
    nq, n2 = g.stat[:, 0:NT], g.stat[:, NT:2 * NT]
    za, zb = g.stat[:, 2 * NT:3 * NT], g.stat[:, 3 * NT:4 * NT]
    s1 = g.coef[:, 0:NT]
    XN3 = xn.rearrange("p (t n) -> p t n", t=NT)
    S3 = g.b2.rearrange("p (t n) -> p t n", t=NT)
    with phase(nc, g, "step", "squared", "summed", "rooted", "ready", "logged") as (block, s):
        @block.scalar
        def _(act):
            nc.scalar.activation(g.b2, xn, ACT.Square).then_inc(s["squared"], 1)
            act.wait_ge(s["summed"], 1)
            nc.scalar.activation(nq, n2, ACT.Sqrt).then_inc(s["rooted"], 1)
            act.wait_ge(s["ready"], 1)
            nc.scalar.activation(za, n2, ACT.Ln, bias=1.0, scale=1.0)
            nc.scalar.activation(zb, n2, ACT.Ln, bias=1.0, scale=-1.0).then_inc(s["logged"], 1)

        @block.vector
        def _(dve):
            V = nc.vector
            step = Steps(dve, s["step"])
            dve.wait_ge(s["squared"], 1)
            V.tensor_reduce(n2, S3, AX, ALU.add).then_inc(s["summed"], 1)
            dve.wait_ge(s["rooted"], 1)
            step(V.tensor_scalar(nq, nq, 1e-15, None, ALU.max))
            step(V.reciprocal(s1, nq))
            V.tensor_scalar(n2, nq, MAXNORM, None, ALU.min).then_inc(s["ready"], 1)
            dve.wait_ge(s["logged"], 1)
            step(V.tensor_tensor(za, za, zb, ALU.subtract))
            step(V.scalar_tensor_tensor(s1, za, 0.5, s1, ALU.mult, ALU.mult))

    H1T = g.view(19200, 6 * N)
    H3 = H1T.rearrange("p (j n) -> p j n", j=6)
    psA = g.ps[:, 2, 0:4 * P].rearrange("p (j r) -> p j r", r=P)
    psB = g.ps[:, 3, 0:2 * P].rearrange("p (j r) -> p j r", r=P)
    psT = g.psT[:, 0:2 * P].rearrange("p (k r) -> p k r", r=P)
    hT = g.ht[:, 0:2 * P].rearrange("p (k r) -> p k r", r=P)
    with phase(nc, g, "loaded", "staged", "turned", "fetched", "made", "kept") as (block, s):
        @block.sync
        def _(sp):
            sp.dma_start(w3(g.w1, 2, MIX), split_k(w_qkv[2], 2)).then_inc(s["loaded"], 16)

        @block.scalar
        def _(act):
            act.sem_inc(s["staged"], 1)
            with act.Fori(0, NT) as t:
                before(act, s["turned"], t)
                nc.scalar.activation(g.stage[:, 0:D], col(xn, t, D), ACT.Copy, scale=col(s1, t)).then_inc(s["staged"], 1)

        @block.tensor
        def _(pe):
            pe.sem_inc(s["turned"], 1)
            pe.sem_inc(s["made"], 1)
            pe.wait_ge(s["loaded"], 16)
            with pe.Fori(0, NT) as t:
                this(pe, s["staged"], t)
                for k in range(2):
                    ins = nc.tensor.transpose(psT[:, k, :], g.stage[:, k * 128:(k + 1) * 128], g.ident[0:P, 0:P])
                ins.then_inc(s["turned"], 1)
                this(pe, s["fetched"], t)
                before(pe, s["kept"], t)
                for j in range(6):
                    ps = psA[:, j, :] if j < 4 else psB[:, j - 4, :]
                    for k in range(2):
                        ins = nc.tensor.matmul(ps, g.w1[:, k * MIX + j * 128:k * MIX + (j + 1) * 128], hT[:, k, :],
                                               start=(k == 0), stop=(k == 1))
                ins.then_inc(s["made"], 1)

        @block.vector
        def _(dve):
            dve.sem_inc(s["fetched"], 1)
            dve.sem_inc(s["kept"], 1)
            with dve.Fori(0, NT) as t:
                this(dve, s["turned"], t)
                before(dve, s["made"], t)
                nc.vector.tensor_copy(hT, psT).then_inc(s["fetched"], 1)
                this(dve, s["made"], t)
                nc.vector.tensor_copy(H3[:, 0:4, bass.ds(t * P, P)], psA)
                nc.vector.tensor_copy(H3[:, 4:6, bass.ds(t * P, P)], psB).then_inc(s["kept"], 1)

    mean, nmean, var, sc, sh = (g.vec[:, 6 * k:6 * k + 6] for k in range(5))
    gb, bb, dw = (g.vec[:, 6 * k:6 * k + 6] for k in range(5, 8))
    BD = g.w1[:, 0:MIX].rearrange("p (j o) -> p j o", j=6)
    brw = g.w1[0:P, MIX:MIX + D]
    with phase(nc, g, "loaded", "zeroed", "placed", "step", "means", "squares", "rooted", "ready", "done") as (block, s):
        @block.sync
        def _(sp):
            for a, b in ((gb, gamma), (bb, beta), (dw, w_dw[2])):
                sp.dma_start(a, b.rearrange("(j p) -> p j", p=128), allow_slow_non_contiguous=True).then_inc(s["loaded"], 16)
            sp.dma_start(brw, b_res.partition_broadcast(P)).then_inc(s["loaded"], 16)
            sp.dma_start(w3(g.w2, 4, D), split_k(w_res, 4)).then_inc(s["loaded"], 16)
            sp.wait_ge(s["zeroed"], 1)
            for q in range(4):
                sp.dma_start(BD[32 * q:32 * q + 32, :, 32 * q:32 * q + 32], w_pw[q]).then_inc(s["placed"], 16)

        @block.scalar
        def _(act):
            act.wait_ge(s["means"], 1)
            for j in range(6):
                ins = nc.scalar.activation(g.view(12800, N), H3[:, j, :], ACT.Square, bias=nmean[:, j:j + 1],
                                           accum_out=var[:, j:j + 1])
                ins.then_inc(s["squares"], 1)
                act.wait_ge(s["squares"], j + 1)
            nc.scalar.activation(sc, var, ACT.Sqrt, bias=g.eps[:, :], scale=1.0 / N).then_inc(s["rooted"], 1)
            act.wait_ge(s["ready"], 1)
            for j in range(6):
                ins = nc.scalar.activation(H3[:, j, :], H3[:, j, :], ACT.Relu, bias=sh[:, j:j + 1], scale=sc[:, j:j + 1])
            ins.then_inc(s["done"], 1)
            act.wait_ge(s["done"], 1)

        @block.vector
        def _(dve):
            V = nc.vector
            step = Steps(dve, s["step"])
            V.memset(g.w1[:, 0:MIX], 0.0).then_inc(s["zeroed"], 1)
            step(V.tensor_reduce(mean, H3, AX, ALU.add))
            step(V.tensor_scalar(mean, mean, 1.0 / N, None, ALU.mult))
            V.tensor_scalar(nmean, mean, -1.0, None, ALU.mult).then_inc(s["means"], 1)
            dve.wait_ge(s["loaded"], 16 * 5)
            dve.wait_ge(s["placed"], 64)
            for j in range(6):
                V.tensor_scalar(BD[:, j, :], BD[:, j, :], dw[:, j:j + 1], None, ALU.mult)
            dve.wait_ge(s["rooted"], 1)
            step(V.reciprocal(sc, sc))
            step(V.tensor_tensor(sc, sc, gb, ALU.mult))
            step(V.tensor_tensor(sh, mean, sc, ALU.mult))
            V.tensor_tensor(sh, bb, sh, ALU.subtract).then_inc(s["ready"], 1)

    FT = g.b2
    psR = g.ps[0:P, 0:2, 0:384]
    psS = g.ps[0:P, 2:4, 0:384]
    psO = g.ps[:, 4, 0:4 * P].rearrange("p (k r) -> p k r", r=P)
    psF = g.ps[0:P, 5, 0:D]
    with ExitStack() as ctx:
        def sb(name, shape):
            return ctx.enter_context(nc.sbuf_tensor(name, shape, F32))
        cat = sb("cat", [P, 2 * MIX])
        nn = sb("nn", [P, 8])
        ks = sb("ks", [P, 16])
        junk = g.h1[0:P, :]
        num = g.stage[:, 0:512]
        den = g.o[:, 0:512]
        hjT = g.ht[:, 0:6 * P].rearrange("p (j r) -> p j r", r=P)
        oT = g.h1[:, 0:4 * P].rearrange("p (k r) -> p k r", r=P)
        PER = 15
        with phase(nc, g, "taken", "turned", "sq1", "nn1", "sq2", "nn2", "cat_ready", "sq3", "nn3", "out_ready",
                   "oturned", "ofetched", "made", "kept", "step") as (block, s):
            @block.tensor
            def _(pe):
                for q in (s["turned"], s["oturned"], s["made"]):
                    pe.sem_inc(q, 1)
                with pe.Fori(0, NT) as t:
                    this(pe, s["taken"], t)
                    before(pe, s["cat_ready"], t)
                    for j in range(6):
                        nc.tensor.transpose(psR[:, j // 3, (j % 3) * 128:(j % 3 + 1) * 128], hjT[:, j, :], g.ident[:, :])
                    for j in range(6):
                        ins = nc.tensor.matmul(psS[:, j // 3, (j % 3) * 128:(j % 3 + 1) * 128], hjT[:, j, :], BD[:, j, :],
                                               start=True, stop=True)
                    ins.then_inc(s["turned"], 1)
                    this(pe, s["out_ready"], t)
                    for k in range(4):
                        ins = nc.tensor.transpose(psO[:, k, :], num[:, k * 128:(k + 1) * 128], g.ident[0:P, 0:P])
                    ins.then_inc(s["oturned"], 1)
                    this(pe, s["ofetched"], t)
                    before(pe, s["kept"], t)
                    for k in range(4):
                        ins = nc.tensor.matmul(psF, oT[:, k, :], g.w2[:, k * D:(k + 1) * D], start=(k == 0), stop=(k == 3))
                    ins.then_inc(s["made"], 1)

            @block.scalar
            def _(act):
                for q in (s["sq1"], s["nn1"], s["sq2"], s["nn2"], s["sq3"], s["nn3"], s["ofetched"]):
                    act.sem_inc(q, 1)
                with act.Fori(0, NT) as t:
                    this(act, s["turned"], t)
                    nc.scalar.activation(junk[:, 0:MIX].rearrange("p (a b) -> p a b", a=2), psR, ACT.Square, accum_out=nn[:, 0:1]).then_inc(s["sq1"], 1)
                    this(act, s["sq1"], t)
                    nc.scalar.activation(nn[:, 1:2], nn[:, 0:1], ACT.Sqrt).then_inc(s["nn1"], 1)
                    this(act, s["cat_ready"], t)
                    nc.scalar.activation(junk, cat[:, :], ACT.Square, accum_out=nn[:, 2:3]).then_inc(s["sq2"], 1)
                    this(act, s["sq2"], t)
                    nc.scalar.activation(nn[:, 3:4], nn[:, 2:3], ACT.Sqrt).then_inc(s["nn2"], 1)
                    this(act, s["out_ready"], t)
                    nc.scalar.activation(junk[:, 0:512], num, ACT.Square, accum_out=nn[:, 5:6]).then_inc(s["sq3"], 1)
                    this(act, s["sq3"], t)
                    nc.scalar.activation(nn[:, 6:7], nn[:, 5:6], ACT.Sqrt).then_inc(s["nn3"], 1)
                    this(act, s["oturned"], t)
                    this(act, s["nn3"], t)
                    nc.scalar.copy(oT, psO).then_inc(s["ofetched"], 1)

            @block.vector
            def _(dve):
                V = nc.vector
                for q in (s["taken"], s["cat_ready"], s["out_ready"], s["kept"]):
                    dve.sem_inc(q, 1)
                with dve.Fori(0, NT) as t:
                    step = Steps(dve, s["step"], t, PER)
                    before(dve, s["made"], t)
                    V.tensor_copy(hjT, H3[:, :, bass.ds(t * P, P)]).then_inc(s["taken"], 1)
                    this(dve, s["nn1"], t)
                    norm_factor(V, step, nn[:, 7:8], nn[:, 1:2], ATANH_MAX)
                    step(V.tensor_scalar(cat[:, 0:MIX].rearrange("p (a b) -> p a b", a=2), psR, nn[:, 7:8], None, ALU.mult))
                    V.tensor_scalar(cat[:, MIX:2 * MIX].rearrange("p (a b) -> p a b", a=2), psS, nn[:, 7:8], None,
                                    ALU.mult).then_inc(s["cat_ready"], 1)
                    this(dve, s["nn2"], t)
                    norm_factor(V, step, nn[:, 4:5], nn[:, 3:4], ATANH_MAX)
                    c3 = cat[:, :].rearrange("p (g c) -> p g c", g=16)
                    q, k, v = (c3[:, :, c * 32:(c + 1) * 32] for c in range(3))
                    n3 = num.rearrange("p (g d) -> p g d", g=16)
                    d3 = den.rearrange("p (g d) -> p g d", g=16)
                    V.tensor_scalar(c3[:, :, 0:64], c3[:, :, 0:64], nn[:, 4:5], 0.0, ALU.mult, ALU.max)
                    step(V.tensor_scalar(v, v, nn[:, 4:5], None, ALU.mult))
                    V.tensor_reduce(ks[:, :], k, AX, ALU.add)
                    step(V.tensor_scalar(d3, v, 1e-15, None, ALU.add))
                    step(V.reciprocal(den, den))
                    step(V.tensor_tensor(n3, q, v, ALU.mult))
                    step(V.tensor_tensor(n3, n3, ks[:, :].unsqueeze(2).to_broadcast([P, 16, 32]), ALU.mult))
                    V.tensor_tensor(num, num, den, ALU.mult).then_inc(s["out_ready"], 1)
                    this(dve, s["nn3"], t)
                    norm_factor(V, step, nn[:, 7:8], nn[:, 6:7], ATANH_MAX)
                    this(dve, s["made"], t)
                    V.scalar_tensor_tensor(col(FT, t, D), psF, nn[:, 7:8], brw, ALU.mult, ALU.add).then_inc(s["kept"], 1)
                    step.end()

    F3 = FT.rearrange("p (t n) -> p t n", t=NT)
    sq = g.b3
    with phase(nc, g, "squared", "summed", "rooted", "tanhed", "step") as (block, s):
        @block.scalar
        def _(act):
            nc.scalar.activation(sq, FT, ACT.Square).then_inc(s["squared"], 1)
            act.wait_ge(s["summed"], 1)
            nc.scalar.activation(nq, n2, ACT.Sqrt).then_inc(s["rooted"], 1)
            act.wait_ge(s["rooted"], 1)
            nc.scalar.activation(za, nq, ACT.Tanh).then_inc(s["tanhed"], 1)

        @block.vector
        def _(dve):
            V = nc.vector
            step = Steps(dve, s["step"])
            dve.wait_ge(s["squared"], 1)
            V.tensor_reduce(n2, sq.rearrange("p (t n) -> p t n", t=NT), AX, ALU.add).then_inc(s["summed"], 1)
            dve.wait_ge(s["tanhed"], 1)
            step(V.tensor_scalar(za, za, MAXNORM, None, ALU.min))
            step(V.tensor_scalar(nq, nq, 1e-15, None, ALU.max))
            step(V.reciprocal(zb, nq))
            step(V.tensor_tensor(za, za, zb, ALU.mult))
            step(V.tensor_tensor(F3, F3, za.unsqueeze(2).to_broadcast([P, NT, D]), ALU.mult))
            step(V.tensor_tensor(x, x, FT, ALU.add))



def vector_phase(nc, g, program):
    with phase(nc, g, "step") as (block, s):
        @block.vector
        def _(dve):
            program(nc.vector, Steps(dve, s["step"]))


def graph_attention_layer(nc, g, d, Wq, Wk, Wv, Wo, gam, bet, first):
    ps = [g.ps[0:P, 4, 0:D], g.ps[0:P, 5, 0:D], g.ps[0:P, 6, 0:D]]
    wts = [g.w1[:, 0:512], g.w1[:, 512:1024], g.w1[:, 1024:1536]]

    def to_tables(V, t, steps):
        for m in range(3):
            ins = V.tensor_copy(g.o[:, m * D:(m + 1) * D], ps[m])
        return ins

    tile_pass(nc, g, g.h, 2, [(mm_weights(wts[m], D), ps[m]) for m in range(3)],
              [(w3(wts[m], 2, D), split_k(w, 2)) for m, w in enumerate((Wq, Wk, Wv))], to_tables,
              tables=[(tb, g.o[:, m * D:(m + 1) * D]) for m, tb in enumerate((d.q, d.k, d.v))])
    edge_scores(nc, g, d.q, d.k)
    segment_softmax(nc, g)
    edge_sums(nc, g, d.v, g.b2, True)

    Z3 = g.zacc[:, :].rearrange("p (t c) -> p t c", c=9)
    A4 = g.b2.rearrange("p (n d) -> p n d", d=DK)

    def normalise(V, step):
        if first:
            step(V.tensor_scalar(g.coef[:, 0:NT], Z3[:, :, 8], 0.0, None, ALU.is_gt))
            step(V.tensor_scalar(g.coef[:, NT:2 * NT], Z3[:, :, 8], 1.0, None, ALU.max))
        z = g.ht[0:P, 0:NT * HEADS]
        step(V.tensor_scalar(z.rearrange("p (t h) -> p t h", h=HEADS), Z3[:, :, 0:8], 1e-9, None, ALU.add))
        step(V.reciprocal(z, z))
        step(V.tensor_tensor(A4, A4, z.unsqueeze(2).to_broadcast([P, NT * HEADS, DK]), ALU.mult))

    vector_phase(nc, g, normalise)
    if first:
        with phase(nc, g, "rooted", "step") as (block, s):
            @block.scalar
            def _(act):
                nc.scalar.activation(g.coef[:, 2 * NT:3 * NT], g.coef[:, NT:2 * NT], ACT.Sqrt).then_inc(s["rooted"], 1)

            @block.vector
            def _(dve):
                step = Steps(dve, s["step"])
                dve.wait_ge(s["rooted"], 1)
                step(nc.vector.reciprocal(g.dinv[:, :], g.coef[:, 2 * NT:3 * NT]))
                step(nc.vector.tensor_tensor(g.dinv[:, :], g.dinv[:, :], g.coef[:, 0:NT], ALU.mult))
    down = g.ps[0:P, 4, 0:D]
    tile_pass(nc, g, g.b2, 2, [(mm_weights(g.w2, D), down)], [(w3(g.w2, 2, D), split_k(Wo, 2))],
              add_into(down, g.h, g.unit))
    layernorm(nc, g, g.h, g.h, g.b2, gam, bet)


def routed_ffn(nc, g, a, d):
    xn, x = g.h, g.x
    layernorm(nc, g, x, xn, g.b2)
    K1 = max(1, int(0.5 * N))
    K1 = K1 - 1 if K1 > 1 else 1
    wr = g.w1[0:P, 0:D]
    br = g.vec[0:P, 0:1]
    wt, rank = g.stat[:, 0:NT], g.stat[:, NT:2 * NT]
    later = g.stat[:, 2 * NT:3 * NT]
    part = g.stat[:, 3 * NT:4 * NT]
    wrow = g.view(19200, N, P)
    junk = g.view(22400, N, P)
    tri = g.view(25600, P, P)
    tri2 = g.view(25800, P, P)
    X3 = lambda b: b.rearrange("p (t n) -> p t n", t=NT)
    with phase(nc, g, "loaded", "step", "turned", "rowed", "stored", "back", "tri") as (block, s):
        @block.sync
        def _(sp):
            sp.dma_start(wr, a["L0_ffn_wr"].rearrange("n o -> (n o)").partition_broadcast(P)).then_inc(s["loaded"], 16)
            sp.dma_start(br, a["L0_ffn_br"].partition_broadcast(P)).then_inc(s["loaded"], 16)
            sp.wait_ge(s["rowed"], 1)
            sp.dma_start(d.rowa.rearrange("(t p) -> t p", p=P), g.o[0:NT, 0:P]).then_inc(s["stored"], 16)
            sp.wait_ge(s["stored"], 16)
            sp.dma_start(wrow, d.rowa.partition_broadcast(P)).then_inc(s["back"], 16)

        @block.gpsimd
        def _(pool):
            nc.gpsimd.memset(tri, 1.0).then_inc(s["tri"], 1)
            pool.wait_ge(s["tri"], 1)
            nc.gpsimd.affine_select(out=tri, in_=tri, compare_op=ALU.is_gt, fill=0.0, base=0, pattern=[[-1, P]],
                                    channel_multiplier=1).then_inc(s["tri"], 1)

        @block.tensor
        def _(pe):
            pe.wait_ge(s["turned"], 1)
            nc.tensor.transpose(g.ps[0:NT, 0, 0:P], wt, g.ident[0:P, 0:P]).then_inc(s["turned"], 1)

        @block.vector
        def _(dve):
            V = nc.vector
            step = Steps(dve, s["step"])
            dve.wait_ge(s["loaded"], 32)
            step(V.tensor_tensor(X3(g.b2), X3(xn), wr.unsqueeze(1).to_broadcast([P, NT, D]), ALU.mult))
            step(V.tensor_reduce(wt, X3(g.b2), AX, ALU.add))
            V.tensor_scalar(wt, wt, br, None, ALU.add).then_inc(s["turned"], 1)
            dve.wait_ge(s["turned"], 2)
            V.tensor_copy(g.o[0:NT, 0:P], g.ps[0:NT, 0, 0:P]).then_inc(s["rowed"], 1)
            dve.wait_ge(s["back"], 16)
            dve.wait_ge(s["tri"], 2)
            step(V.memset(g.stat[:, NT:2 * NT], 0.0))
            step(V.memset(later, 0.0))
            for t in range(NT):
                me = wt[:, t:t + 1]
                a0, a1 = t * P, (t + 1) * P
                if t:
                    step(V.tensor_scalar(junk[:, 0:a0], wrow[:, 0:a0], me, 0.0, ALU.is_ge, ALU.add, accum_out=rank[:, t:t + 1]))
                step(V.tensor_scalar(junk[:, a0:N], wrow[:, a0:N], me, 0.0, ALU.is_gt, ALU.add, accum_out=later[:, t:t + 1]))
                step(V.scalar_tensor_tensor(tri2, wrow[:, a0:a1], me, tri, ALU.is_equal, ALU.mult))
                step(V.tensor_reduce(part[:, t:t + 1], tri2, AX, ALU.add))
            step(V.tensor_tensor(rank, rank, later, ALU.add))
            step(V.tensor_tensor(rank, rank, part, ALU.add))
            step(V.scalar_tensor_tensor(g.coef[:, 0:NT], rank, float(K1), wt, ALU.is_lt, ALU.mult))
            step(V.tensor_tensor(x, x, xn, ALU.add))
    mlp(nc, g, xn, a["L0_ffn_w1"], a["L0_ffn_b1"], a["L0_ffn_w2"], a["L0_ffn_b2"], ACT.Gelu_apprx_tanh, x, g.coef[:, 0:NT])


def graph_convolution(nc, g, a, d):
    layernorm(nc, g, g.x, g.h, g.b2)
    ps = g.ps[0:P, 4, 0:D]

    def to_table(V, t, steps):
        return V.tensor_scalar(g.o[:, 0:D], ps, col(g.dinv, t), None, ALU.mult)

    tile_pass(nc, g, g.h, 2, [(mm_weights(g.w1, D), ps)], [(w3(g.w1, 2, D), split_k(a["L1_gnn_W"], 2))], to_table,
              tables=[(d.q, g.o[:, 0:D])])
    edge_sums(nc, g, d.q, g.b2, False)

    def add(V, step):
        A3 = g.b2.rearrange("p (t n) -> p t n", t=NT)
        step(V.tensor_tensor(A3, A3, g.dinv[:, :].unsqueeze(2).to_broadcast([P, NT, D]), ALU.mult))
        step(V.tensor_tensor(g.x, g.x, g.b2, ALU.add))
    vector_phase(nc, g, add)


def linear_attention(nc, g, a, l):
    y, xh = g.h, g.b5
    q, k, v = g.b2, g.b3, g.b4
    layernorm(nc, g, y, xh, q)
    ps = [g.ps[0:P, 4, 0:D], g.ps[0:P, 5, 0:D], g.ps[0:P, 6, 0:D]]
    wts = [g.w1[:, 0:512], g.w1[:, 512:1024], g.w1[:, 1024:1536]]
    aff = (g.vec[:, 32:34], g.vec[:, 34:36])

    def keep(V, t, steps):
        for m, b in enumerate((q, k, v)):
            ins = V.tensor_copy(col(b, t, D), ps[m])
        return ins

    tile_pass(nc, g, xh, 2, [(mm_weights(wts[m], D), ps[m]) for m in range(3)],
              [(w3(wts[m], 2, D), split_k(w[l], 2)) for m, w in enumerate((a["L1_mix_Wq"], a["L1_mix_Wk"], a["L1_mix_Wv"]))]
              + [(aff[0], a["L1_mix_ln1_g"][l].rearrange("(k p) -> p k", p=128)),
                 (aff[1], a["L1_mix_ln1_b"][l].rearrange("(k p) -> p k", p=128))], keep, affine=aff)

    S = float(DK) ** -0.25
    Q4 = q.rearrange("p (n d) -> p n d", d=DK)
    K3 = k.rearrange("p (t n) -> p t n", t=NT)
    KT = k.rearrange("p (t n) -> p n t", t=NT)
    qm = g.ht[0:P, 0:NT * HEADS]
    kcol = g.o[:, 0:D]
    kmT = g.vec[:, 0:2]
    bd = g.h1[:, 0:256].rearrange("p (k n) -> p k n", k=2)
    with phase(nc, g, "step", "kcol", "kturn", "kmax", "krow", "ksub", "qsub", "kexp", "qexp") as (block, s):
        @block.vector
        def _(dve):
            V = nc.vector
            step = Steps(dve, s["step"])
            V.tensor_reduce(kcol, KT, AX, ALU.max).then_inc(s["kcol"], 1)
            step(V.tensor_reduce(qm, Q4, AX, ALU.max))
            V.tensor_tensor(Q4, Q4, qm.unsqueeze(2).to_broadcast([P, NT * HEADS, DK]), ALU.subtract).then_inc(s["qsub"], 1)
            dve.wait_ge(s["kturn"], 1)
            step(V.tensor_reduce(kmT, g.ps[:, 0, 0:2 * P].rearrange("p (k r) -> p k r", r=P), AX, ALU.max))
            for c in range(2):
                ins = V.tensor_scalar(bd[:, c, :], g.ident[:, :], kmT[:, c:c + 1], None, ALU.mult)
            ins.then_inc(s["kmax"], 1)
            dve.wait_ge(s["krow"], 1)
            step(V.tensor_copy(kcol, g.ps[0:P, 1, 0:D]))
            V.tensor_tensor(K3, K3, kcol.unsqueeze(1).to_broadcast([P, NT, D]), ALU.subtract).then_inc(s["ksub"], 1)
            dve.wait_ge(s["qexp"], 1)
            step(V.tensor_reduce(qm, Q4, AX, ALU.add))
            step(V.reciprocal(qm, qm))
            step(V.tensor_tensor(Q4, Q4, qm.unsqueeze(2).to_broadcast([P, NT * HEADS, DK]), ALU.mult))

        @block.tensor
        def _(pe):
            pe.wait_ge(s["kcol"], 1)
            for c in range(2):
                ins = nc.tensor.transpose(g.ps[:, 0, c * P:(c + 1) * P], kcol[:, c * 128:(c + 1) * 128], g.ident[0:P, 0:P])
            ins.then_inc(s["kturn"], 1)
            pe.wait_ge(s["kmax"], 1)
            for c in range(2):
                ins = nc.tensor.matmul(g.ps[0:P, 1, c * 128:(c + 1) * 128], g.ones[:, 0:P], bd[:, c, :], start=True, stop=True)
            ins.then_inc(s["krow"], 1)

        @block.scalar
        def _(act):
            act.wait_ge(s["qsub"], 1)
            nc.scalar.activation(q, q, ACT.Exp, scale=S).then_inc(s["qexp"], 1)
            act.wait_ge(s["ksub"], 1)
            nc.scalar.activation(k, k, ACT.Exp, scale=S).then_inc(s["kexp"], 1)
            act.wait_ge(s["kexp"], 1)

    ctxT = g.h1[:, 0:256].rearrange("p (c n) -> p c n", c=2)
    rk = g.h1[:, 256:512].rearrange("p (c n) -> p c n", c=2)
    wctx = g.w1[:, 0:512]
    hd = g.h1[:, 512:640]
    with phase(nc, g, "masked", "zeroed", "made", "step", "ready", "loaded", "fused", "staged", "read") as (block, s):
        @block.sync
        def _(sp):
            sp.dma_start(w3(g.w2, 2, D), split_k(a["L1_mix_Wo"][l], 2)).then_inc(s["loaded"], 16)

        @block.gpsimd
        def _(pool):
            nc.gpsimd.memset(hd, 0.0).then_inc(s["masked"], 1)
            pool.wait_ge(s["masked"], 1)
            for b in range(4):
                nc.gpsimd.memset(hd[32 * b:32 * b + 32, 32 * b:32 * b + 32], 1.0).then_inc(s["masked"], 1)

        @block.scalar
        def _(act):
            act.sem_inc(s["staged"], 1)
            with act.Fori(0, NT) as t:
                before(act, s["read"], t)
                nc.scalar.copy(g.stage[:, 0:D], col(v, t, D)).then_inc(s["staged"], 1)

        @block.tensor
        def _(pe):
            pe.sem_inc(s["read"], 1)
            pe.wait_ge(s["zeroed"], 1)
            z = g.o[0:1, 0:128]
            for c in range(2):
                nc.tensor.matmul(g.ps[:, 2 + c, 0:128], z, z, start=True, stop=False, skip_group_check=True)
                nc.tensor.matmul(g.ps[:, 4 + c, 0:128], z, z, start=True, stop=False, skip_group_check=True)
            with pe.Fori(0, NT) as t:
                this(pe, s["staged"], t)
                for c in range(2):
                    kt = k[:, bass.ds(t * D + c * 128, 128)]
                    nc.tensor.matmul(g.ps[:, 2 + c, 0:128], g.stage[:, c * 128:(c + 1) * 128], kt, start=False, stop=False,
                                     skip_group_check=True)
                    ins = nc.tensor.matmul(g.ps[:, 4 + c, 0:128], g.ones[0:P, :], kt, start=False, stop=False,
                                           skip_group_check=True)
                ins.then_inc(s["read"], 1)
            for c in range(2):
                nc.tensor.matmul(g.ps[:, 2 + c, 0:128], z, z, start=False, stop=True, skip_group_check=True)
                ins = nc.tensor.matmul(g.ps[:, 4 + c, 0:128], z, z, start=False, stop=True, skip_group_check=True)
            ins.then_inc(s["made"], 1)
            pe.wait_ge(s["ready"], 1)
            pe.wait_ge(s["loaded"], 16)
            for c in range(2):
                ins = nc.tensor.matmul(g.ps[:, 6 + c, 0:D], ctxT[:, c, :], g.w2[:, c * D:(c + 1) * D], start=True, stop=True)
            ins.then_inc(s["fused"], 1)

        @block.vector
        def _(dve):
            V = nc.vector
            step = Steps(dve, s["step"])
            V.memset(g.o[0:1, 0:128], 0.0).then_inc(s["zeroed"], 1)
            dve.wait_ge(s["masked"], 5)
            dve.wait_ge(s["made"], 1)
            step(V.reciprocal(rk, g.ps[:, 4:6, 0:128]))
            for c in range(2):
                step(V.tensor_tensor(rk[:, c, :], rk[:, c, :], hd, ALU.mult))
            V.tensor_tensor(ctxT, g.ps[:, 2:4, 0:128], rk, ALU.mult).then_inc(s["ready"], 1)
            dve.wait_ge(s["fused"], 1)
            step(V.tensor_copy(wctx.rearrange("p (c n) -> p c n", c=2), g.ps[:, 6:8, 0:D]))

    down = g.ps[0:P, 4, 0:D]
    tile_pass(nc, g, q, 2, [(mm_weights(wctx, D), down)],
              [(g.brow[:, :], a["L1_mix_bo"][l].rearrange("(a n) -> a n", a=1))], add_into(down, y, g.unit), bias=True)


def transformer(nc, g, a):
    y = g.h
    for l in range(4):
        linear_attention(nc, g, a, l)
        layernorm(nc, g, y, g.b5, g.b2)
        aff = (g.vec[:, 32:34], g.vec[:, 34:36])
        mlp(nc, g, g.b5, a["L1_mix_W1"][l], a["L1_mix_b1"][l], a["L1_mix_W2"][l], a["L1_mix_b2"][l], ACT.Gelu, y, g.unit, affine=aff,
            extra=[(aff[0], a["L1_mix_ln2_g"][l].rearrange("(k p) -> p k", p=128)),
                   (aff[1], a["L1_mix_ln2_b"][l].rearrange("(k p) -> p k", p=128))])

    def add(V, step):
        step(V.tensor_tensor(g.x, g.x, y, ALU.add))
    vector_phase(nc, g, add)


def experts(nc, g, a, d):
    xn, x = g.h, g.x
    layernorm(nc, g, x, xn, g.b2)
    H, EX = 4, 4
    small = g.view(12800, 6400, P)
    hg = small[:, 0:NT * 16]
    tab = small[:, 400:400 + NT * 20]
    dtab = small[:, 900:900 + NT * 8]
    ps = g.ps[0:P, 4, 0:16]

    def keep(V, t, steps):
        return V.tensor_copy(col(hg, t, 16), ps)

    tile_pass(nc, g, xn, 2, [(lambda k: g.w1[:, k * 16:(k + 1) * 16], ps)],
              [(w3(g.w1, 2, 16), split_k(a["L1_ffn_W_gat"], 2))], keep)

    T3 = tab.rearrange("p (t c) -> p t c", c=20)
    D3 = dtab.rearrange("p (t c) -> p t c", c=8)
    H4 = hg.rearrange("p (n e) -> p n e", e=EX)
    tmp = small[:, 1100:1500]
    aS, aD = small[:, 1500:1516], small[:, 1516:1532]
    sc = small[:, 1600:1700]
    fill = g.view(19200, N, P)
    arow = g.view(19200, 4 * N, P)
    pen = [g.view(31700 + 3200 * b, N, P) for b in range(2)]
    with phase(nc, g, "loaded", "step", "table", "stored", "filled", "penalised") as (block, s):
        @block.sync
        def _(sp):
            sp.dma_start(aS, a["L1_ffn_att_src"].rearrange("h e -> (h e)").partition_broadcast(P)).then_inc(s["loaded"], 16)
            sp.dma_start(aD, a["L1_ffn_att_dst"].rearrange("h e -> (h e)").partition_broadcast(P)).then_inc(s["loaded"], 16)
            sp.wait_ge(s["filled"], 1)
            for t in range(NT):
                sp.dma_start(d.pen[t * P * N:(t + 1) * P * N].rearrange("(p n) -> p n", p=P), fill).then_inc(s["penalised"], 16)
            sp.wait_ge(s["table"], 1)
            sp.dma_start(d.tab.rearrange("(t p) c -> p t c", p=P), T3).then_inc(s["stored"], 16)
            for h in range(H):
                sp.dma_start(d.arow[h * N:(h + 1) * N].rearrange("(t p) -> p t", p=P), T3[:, :, 16 + h],
                             allow_slow_non_contiguous=True).then_inc(s["stored"], 16)
            sp.wait_ge(s["stored"], 16 * 5)
            sp.wait_ge(s["penalised"], 16 * NT)

        @block.vector
        def _(dve):
            V = nc.vector
            step = Steps(dve, s["step"])
            V.memset(fill, -BIG).then_inc(s["filled"], 1)
            dve.wait_ge(s["loaded"], 32)
            t4 = tmp.rearrange("p (t c) -> p t c", c=16)
            h3 = hg.rearrange("p (t c) -> p t c", c=16)
            for n, w in enumerate((aD, aS)):
                step(V.tensor_tensor(t4, h3, w.unsqueeze(1).to_broadcast([P, NT, 16]), ALU.mult))
                step(V.tensor_reduce(sc, tmp.rearrange("p (n e) -> p n e", e=EX), AX, ALU.add))
                out = (D3[:, :, 0:4], T3[:, :, 16:20])[n]
                step(V.tensor_copy(out, sc.rearrange("p (t h) -> p t h", h=H)))
            V.tensor_copy(T3[:, :, 0:16], h3).then_inc(s["table"], 1)

    EC = E2 // 128
    sI = g.view(31700, EC).bitcast(I32)
    dI = g.view(32300, EC).bitcast(I32)
    sF, dF, fl = g.view(32900, EC), g.view(33500, EC), g.view(34100, EC)
    flI = g.view(34700, EC).bitcast(I32)
    srcI, dstI = g.srcv_e, g.dstv_e
    zero = g.ht[:, 0:1]
    ei = a["L1_ffn_edge_index"]
    GS = 16
    with phase(nc, g, "loaded", "step", "ready", "indexed", "scattered", "zeroed") as (block, s):
        @block.sync
        def _(sp):
            sp.dma_start(sI, ei[0].rearrange("(p c) -> p c", p=128)).then_inc(s["loaded"], 16)
            sp.dma_start(dI, ei[1].rearrange("(p c) -> p c", p=128)).then_inc(s["loaded"], 16)

        @block.vector
        def _(dve):
            V = nc.vector
            step = Steps(dve, s["step"])
            V.memset(zero, 0.0).then_inc(s["zeroed"], 1)
            dve.wait_ge(s["loaded"], 32)
            step(V.tensor_copy(sF, sI))
            step(V.tensor_copy(dF, dI))
            step(V.tensor_scalar(sF, sF, float(N - 1), None, ALU.min))
            step(V.tensor_copy(srcI, sF))
            step(V.scalar_tensor_tensor(fl, dF, float(N), sF, ALU.mult, ALU.add))
            step(V.tensor_scalar(dF, dF, float(N - 1), None, ALU.min))
            step(V.tensor_copy(dstI, dF))
            step(V.tensor_scalar(g.dlo, dI, 127, None, ALU.bitwise_and))
            step(V.tensor_scalar(g.dhi, dI, 7, None, ALU.logical_shift_right))
            V.tensor_copy(flI, fl).then_inc(s["ready"], 1)

        @block.gpsimd
        def _(pool):
            ix = g.ht[:, 8:8 + GS].bitcast(I32)
            pool.wait_ge(s["zeroed"], 1)
            pool.wait_ge(s["ready"], 1)
            pool.sem_inc(s["indexed"], 1)
            with pool.Fori(0, EC // GS) as i:
                nc.gpsimd.tensor_copy(ix, col(flI, i, GS)).then_inc(s["indexed"], 1)
                this(pool, s["indexed"], i)
                for j in range(GS):
                    nc.gpsimd.indirect_dma_start(d.pen.rearrange("(n o) -> n o", o=1), bass.IndirectOffsetOnAxis(ix[:, j:j + 1], 0),
                                                 zero, None, bounds_check=N * N - 1, oob_is_err=False).then_inc(s["scattered"], 16)
                    hold(pool, s["scattered"], i * (16 * GS) + 16 * (j + 1))

    mx = small[:, 1700:1700 + NT * H]
    sums = g.ps[0:P, :, :].rearrange("p b c -> p (b c)")[:, 0:N]
    with phase(nc, g, "loaded", "pen0", "pen1", "used0", "used1") as (block, s):
        lp, us = [s["pen0"], s["pen1"]], [s["used0"], s["used1"]]

        @block.sync
        def _(sp):
            for h in range(H):
                sp.dma_start(arow[:, h * N:(h + 1) * N], d.arow[h * N:(h + 1) * N].partition_broadcast(P)).then_inc(s["loaded"], 16)
            for t in range(NT):
                if t >= 2:
                    sp.wait_ge(us[t % 2], H * (t // 2))
                sp.dma_start(pen[t % 2], d.pen[t * P * N:(t + 1) * P * N].rearrange("(p n) -> p n", p=P)).then_inc(lp[t % 2], 16)

        @block.vector
        def _(dve):
            dve.wait_ge(s["loaded"], 64)
            for t in range(NT):
                dve.wait_ge(lp[t % 2], 16 * (t // 2 + 1))
                for h in range(H):
                    if t or h:
                        before_ = (t, h - 1) if h else (t - 1, H - 1)
                        dve.wait_ge(us[before_[0] % 2], H * (before_[0] // 2) + before_[1] + 1)
                    nc.vector.tensor_tensor_reduce(sums, pen[t % 2],
                                                   arow[:, h * N:(h + 1) * N], 1.0, -BIG, ALU.add, ALU.max,
                                                   mx[:, t * H + h:t * H + h + 1]).then_inc(us[t % 2], 1)

    lk = small[:, 1800:1900]
    wself = small[:, 1900:2000]
    agg = small[:, 2100:2600]
    A3 = agg.rearrange("p (t c) -> p t c", c=20)
    with phase(nc, g, "step", "shifted", "expd", "table", "stored") as (block, s):
        @block.vector
        def _(dve):
            V = nc.vector
            step = Steps(dve, s["step"])
            m3 = mx.rearrange("p (t h) -> p t h", h=H)
            l3 = lk.rearrange("p (t h) -> p t h", h=H)
            step(V.tensor_tensor(m3, m3, T3[:, :, 16:20], ALU.max))
            step(V.tensor_tensor(m3, m3, D3[:, :, 0:4], ALU.add))
            step(V.tensor_copy(l3, m3))
            V.scalar_tensor_tensor(D3[:, :, 4:8], l3, 0.2, m3, ALU.mult, ALU.max).then_inc(s["table"], 1)
            dve.wait_ge(s["table"], 1)
            step(V.tensor_tensor(m3, T3[:, :, 16:20], D3[:, :, 0:4], ALU.add))
            step(V.tensor_copy(l3, m3))
            step(V.scalar_tensor_tensor(l3, l3, 0.2, m3, ALU.mult, ALU.max))
            V.tensor_tensor(l3, l3, D3[:, :, 4:8], ALU.subtract).then_inc(s["shifted"], 1)

        @block.scalar
        def _(act):
            act.wait_ge(s["shifted"], 1)
            nc.scalar.activation(wself, lk, ACT.Exp).then_inc(s["expd"], 1)
            act.wait_ge(s["expd"], 1)

        @block.sync
        def _(sp):
            sp.wait_ge(s["table"], 1)
            sp.dma_start(d.dtab.rearrange("(t p) c -> p t c", p=P), D3).then_inc(s["stored"], 16)
            sp.wait_ge(s["stored"], 16)

    GB = 4
    NB = 25
    rows = g.w1[:, 0:GB * 20].rearrange("p (j c) -> p j c", c=20)
    drows = g.w1[:, 100:100 + GB * 8].rearrange("p (j c) -> p j c", c=8)
    ee = g.w1[:, 200:200 + GB * 4].rearrange("p (j c) -> p j c", c=4)
    e2 = g.w1[:, 220:220 + GB * 4].rearrange("p (j c) -> p j c", c=4)
    pay = g.w1[:, 300:300 + GB * 20].rearrange("p (j c) -> p j c", c=20)
    ohl = [g.w1[:, 512 + 128 * j:640 + 128 * j] for j in range(GB)]
    ohh = g.w1[:, 1024:1024 + GB * NB].rearrange("p (j t) -> p j t", t=NB)
    big = [g.w2[:, 500 * j:500 * j + 500] for j in range(GB)]
    loF, hiF = g.loF, g.hiF
    total = g.ps[:, 3, 0:NB * 20]
    ALLD = g.view(31700, NB * 20)
    names = ["gathered", "raw", "expd", "made", "summed", "step", "zeroed", "indexed", "final", "copied", "hot", "stored", "back", "red"]
    with phase(nc, g, *names) as (block, s):
        @block.gpsimd
        def _(pool):
            ix = g.ht[:, 0:2 * GB].bitcast(I32)
            pool.sem_inc(s["indexed"], 2)
            with pool.Fori(0, EC // GB) as i:
                before(pool, s["made"], i)
                nc.gpsimd.tensor_copy(ix[:, 0:GB], col(srcI, i, GB)).then_inc(s["indexed"], 1)
                nc.gpsimd.tensor_copy(ix[:, GB:2 * GB], col(dstI, i, GB)).then_inc(s["indexed"], 1)
                this(pool, s["indexed"], i, 2)
                for j in range(GB):
                    nc.gpsimd.indirect_dma_start(rows[:, j, :], None, d.tab,
                                                 bass.IndirectOffsetOnAxis(ix[:, j:j + 1], 0)).then_inc(s["gathered"], 16)
                    nc.gpsimd.indirect_dma_start(drows[:, j, :], None, d.dtab,
                                                 bass.IndirectOffsetOnAxis(ix[:, GB + j:GB + j + 1], 0)).then_inc(s["gathered"], 16)

        @block.scalar
        def _(act):
            act.sem_inc(s["expd"], 1)
            with act.Fori(0, EC // GB) as i:
                this(act, s["raw"], i)
                nc.scalar.activation(pay[:, :, 16:20], ee, ACT.Exp).then_inc(s["expd"], 1)

        @block.vector
        def _(dve):
            V = nc.vector
            V.memset(g.o[0:1, 0:500], 0.0).then_inc(s["zeroed"], 1)
            V.tensor_copy(loF, g.dlo)
            V.tensor_copy(hiF, g.dhi).then_inc(s["zeroed"], 1)
            dve.wait_ge(s["zeroed"], 2)
            dve.sem_inc(s["raw"], 1)
            dve.sem_inc(s["made"], 1)
            dve.sem_inc(s["hot"], 1)
            with dve.Fori(0, EC // GB) as i:
                step = Steps(dve, s["step"], i, 4)
                landed(dve, s["gathered"], i, 32 * GB)
                step(V.tensor_tensor(ee, rows[:, :, 16:20], drows[:, :, 0:4], ALU.add))
                step(V.scalar_tensor_tensor(e2, ee, 0.2, ee, ALU.mult, ALU.max))
                before(dve, s["summed"], i)
                V.tensor_tensor(ee, e2, drows[:, :, 4:8], ALU.subtract).then_inc(s["raw"], 1)
                for j in range(GB):
                    V.tensor_scalar(ohl[j], g.iota[:, :], loF[:, bass.ds(i * GB + j, 1)], None, ALU.is_equal)
                step(V.tensor_tensor(ohh, g.iota[:, 0:NB].unsqueeze(1).to_broadcast([128, GB, NB]),
                                     col(hiF, i, GB).unsqueeze(2).to_broadcast([128, GB, NB]), ALU.is_equal))
                this(dve, s["expd"], i)
                r4 = rows[:, :, 0:16].rearrange("p j (h e) -> p j h e", h=H)
                p4 = pay[:, :, 0:16].rearrange("p j (h e) -> p j h e", h=H)
                for j in range(GB):
                    ins = V.tensor_tensor(p4[:, j], r4[:, j], pay[:, j, 16:20].unsqueeze(2).to_broadcast([128, H, EX]), ALU.mult)
                step(ins)
                for j in range(GB):
                    ins = V.tensor_tensor(big[j].rearrange("p (t c) -> p t c", c=20),
                                          ohh[:, j, :].unsqueeze(2).to_broadcast([128, NB, 20]),
                                          pay[:, j, :].unsqueeze(1).to_broadcast([128, NB, 20]), ALU.mult)
                ins.then_inc(s["made"], 1)
                step.end()
            dve.wait_ge(s["final"], 1)
            V.tensor_copy(ALLD, total).then_inc(s["copied"], 1)
            dve.wait_ge(s["back"], 16)
            step2 = Steps(dve, s["red"])
            own = g.view(32300, NT * 20, P).rearrange("p (t c) -> p t c", c=20)
            for h in range(H):
                o = own[:, :, 4 * h:4 * h + 4]
                w = wself.rearrange("p (t h) -> p t h", h=H)[:, :, h:h + 1].to_broadcast([P, NT, EX])
                step2(V.tensor_tensor(o, T3[:, :, 4 * h:4 * h + 4], w, ALU.mult))
            step2(V.tensor_copy(own[:, :, 16:20], wself.rearrange("p (t h) -> p t h", h=H)))
            step2(V.tensor_tensor(A3, A3, own, ALU.add))

        @block.tensor
        def _(pe):
            pe.sem_inc(s["summed"], 1)
            pe.wait_ge(s["zeroed"], 1)
            nc.tensor.matmul(total, g.o[0:1, 0:128], g.o[0:1, 0:500], start=True, stop=False, skip_group_check=True)
            with pe.Fori(0, EC // GB) as i:
                this(pe, s["made"], i)
                for j in range(GB):
                    ins = nc.tensor.matmul(total, ohl[j], big[j], start=False, stop=False, skip_group_check=True)
                ins.then_inc(s["summed"], 1)
            nc.tensor.matmul(total, g.o[0:1, 0:128], g.o[0:1, 0:500], start=False, stop=True,
                             skip_group_check=True).then_inc(s["final"], 1)

        @block.sync
        def _(sp):
            sp.wait_ge(s["copied"], 1)
            sp.dma_start(d.agg.rearrange("(t p) c -> p t c", p=128), ALLD.rearrange("p (t c) -> p t c", c=20)).then_inc(s["stored"], 16)
            sp.wait_ge(s["stored"], 16)
            sp.dma_start(A3, d.agg[0:N, :].rearrange("(t p) c -> p t c", p=P)).then_inc(s["back"], 16)

    rz = small[:, 2600:2700]
    s16 = small[:, 2700:3100]
    sq = small[:, 3100:3500]
    m1, v1, r1, q1 = (small[:, 3500 + 25 * n:3525 + 25 * n] for n in range(4))
    par = small[:, 3600:3648]
    scr = small[:, 3700:3800]
    cmpb = small[:, 3800:4200]
    rk4 = small[:, 4200:4300]
    ex = small[:, 4300:4400]
    gate = small[:, 4400:4500]
    lower = small[:, 4500:4516]
    with phase(nc, g, "loaded", "lowset", "step", "var", "std", "shifted", "expd") as (block, s):
        @block.sync
        def _(sp):
            for n, b in enumerate((a["L1_ffn_b_gat"], a["L1_ffn_ln_gamma"], a["L1_ffn_ln_beta"])):
                sp.dma_start(par[:, 16 * n:16 * n + 16], b.partition_broadcast(P)).then_inc(s["loaded"], 16)

        @block.gpsimd
        def _(pool):
            nc.gpsimd.memset(lower, 0.0).then_inc(s["lowset"], 1)
            pool.wait_ge(s["lowset"], 1)
            for n in range(1, EX):
                nc.gpsimd.memset(lower[:, n * EX:n * EX + n], 1.0).then_inc(s["lowset"], 1)

        @block.scalar
        def _(act):
            act.wait_ge(s["var"], 1)
            nc.scalar.activation(q1, v1, ACT.Sqrt, bias=g.eps[0:P, :], scale=1.0 / 16).then_inc(s["std"], 1)
            act.wait_ge(s["shifted"], 1)
            nc.scalar.activation(ex, scr, ACT.Exp).then_inc(s["expd"], 1)

        @block.vector
        def _(dve):
            V = nc.vector
            step = Steps(dve, s["step"])
            step(V.tensor_scalar(rz.rearrange("p (t h) -> p t h", h=H), A3[:, :, 16:20], 1e-16, None, ALU.add))
            step(V.reciprocal(rz, rz))
            S3 = s16.rearrange("p (t c) -> p t c", c=16)
            Q3 = sq.rearrange("p (t c) -> p t c", c=16)
            w16 = [P, NT, 16]
            step(V.tensor_copy(S3, A3[:, :, 0:16]))
            s4 = s16.rearrange("p (n e) -> p n e", e=EX)
            step(V.tensor_tensor(s4, s4, rz.unsqueeze(2).to_broadcast([P, NT * H, EX]), ALU.mult))
            dve.wait_ge(s["loaded"], 48)
            step(V.tensor_tensor(S3, S3, par[:, 0:16].unsqueeze(1).to_broadcast(w16), ALU.add))
            step(V.tensor_reduce(m1, S3, AX, ALU.add))
            step(V.tensor_scalar(m1, m1, 1.0 / 16, None, ALU.mult))
            step(V.tensor_tensor(S3, S3, m1.unsqueeze(2).to_broadcast(w16), ALU.subtract))
            step(V.tensor_tensor(sq, s16, s16, ALU.mult))
            V.tensor_reduce(v1, Q3, AX, ALU.add).then_inc(s["var"], 1)
            dve.wait_ge(s["std"], 1)
            step(V.reciprocal(r1, q1))
            step(V.tensor_tensor(S3, S3, r1.unsqueeze(2).to_broadcast(w16), ALU.mult))
            step(V.tensor_tensor(S3, S3, par[:, 16:32].unsqueeze(1).to_broadcast(w16), ALU.mult))
            step(V.tensor_tensor(S3, S3, par[:, 32:48].unsqueeze(1).to_broadcast(w16), ALU.add))
            sc3 = scr.rearrange("p (t e) -> p t e", e=EX)
            step(V.tensor_tensor(sc3, S3[:, :, 0:4], S3[:, :, 4:8], ALU.add))
            step(V.tensor_tensor(sc3, sc3, S3[:, :, 8:12], ALU.add))
            step(V.tensor_tensor(sc3, sc3, S3[:, :, 12:16], ALU.add))
            step(V.tensor_scalar(scr, scr, 0.25, None, ALU.mult))
            dve.wait_ge(s["lowset"], EX)
            k3 = rk4.rearrange("p (t e) -> p t e", e=EX)
            c3 = cmpb.rearrange("p (t e) -> p t e", e=16)
            for i in range(EX):
                me = sc3[:, :, i:i + 1].to_broadcast([P, NT, EX])
                gt, eq = c3[:, :, 0:4], c3[:, :, 4:8]
                step(V.tensor_tensor(gt, sc3, me, ALU.is_gt))
                step(V.tensor_tensor(eq, sc3, me, ALU.is_equal))
                step(V.tensor_tensor(eq, eq, lower[:, i * EX:(i + 1) * EX].unsqueeze(1).to_broadcast([P, NT, EX]), ALU.mult))
                step(V.tensor_tensor(gt, gt, eq, ALU.add))
                step(V.tensor_reduce(k3[:, :, i:i + 1], gt, AX, ALU.add))
            step(V.tensor_reduce(m1, sc3, AX, ALU.max))
            V.tensor_tensor(sc3, sc3, m1.unsqueeze(2).to_broadcast([P, NT, EX]), ALU.subtract).then_inc(s["shifted"], 1)
            dve.wait_ge(s["expd"], 1)
            step(V.scalar_tensor_tensor(ex, rk4, 2.0, ex, ALU.is_lt, ALU.mult))
            e3 = ex.rearrange("p (t e) -> p t e", e=EX)
            step(V.tensor_reduce(m1, e3, AX, ALU.add))
            step(V.reciprocal(r1, m1))
            step(V.tensor_tensor(gate.rearrange("p (e t) -> p t e", e=EX), e3, r1.unsqueeze(2).to_broadcast([P, NT, EX]), ALU.mult))
    for e in range(EX):
        mlp(nc, g, xn, a["L1_ffn_W1"][e], a["L1_ffn_b1"][e], a["L1_ffn_W2"][e], a["L1_ffn_b2"][e], ACT.Gelu, x,
            gate[:, e * NT:(e + 1) * NT])


STOP = 99


def gps_program(nc, a, out):
    d = Names()

    def dram(name, shape, dt=F32):
        return nc.dram_tensor(name, shape, dt, kind="Internal").ap()

    d.key, d.w, d.keys = dram("key", [ET]), dram("w", [NV], I32), dram("keys", [NV * P + 16])
    d.q, d.k, d.v = dram("q_rows", [N, D]), dram("k_rows", [N, D]), dram("v_rows", [N, D])
    d.rowa, d.arow = dram("rowa", [N]), dram("arow", [4 * N])
    d.pen, d.tab, d.dtab, d.agg = dram("pen", [N * N]), dram("tab", [N, 20]), dram("dtab", [N, 8]), dram("agg", [25 * 128, 20])
    d.links = dram("links", [128, SEQ + 1])
    with ExitStack() as ctx:
        g = setup(nc, ctx)
        EC = E2 // 128
        g.loF, g.hiF = g.view(35300, EC), g.view(34700, EC)
        constants(nc, g)
        plan_visits(nc, g, a["src"], a["dst"], d)
        if STOP > 0:
            with phase(nc, g, "loaded") as (block, s):
                @block.sync
                def _(sp):
                    sp.dma_start(g.x.rearrange("p (t n) -> p t n", t=NT), a["x"].rearrange("(t p) n -> p t n", p=P)).then_inc(s["loaded"], 16)
                    sp.wait_ge(s["loaded"], 16)
            layernorm(nc, g, g.x, g.h, g.b2)
        if STOP == 1:
            return dump(nc, g, g.h, out)
        if STOP > 1:
            spill(nc, g, d.links, True)
            mix(nc, g, g.h, g.x, a["L0_mix_w_qkv"], a["L0_mix_bn_gamma"], a["L0_mix_bn_beta"], a["L0_mix_w_dw"], a["L0_mix_w_pw"],
                a["L0_mix_w_res"], a["L0_mix_b_res"])
            spill(nc, g, d.links, False)
        if STOP == 2:
            return dump(nc, g, g.x, out)
        for l in range(2):
            graph_attention_layer(nc, g, d, a["L0_gnn_Wq"][l], a["L0_gnn_Wk"][l], a["L0_gnn_Wv"][l], a["L0_gnn_Wo"][l],
                                  a["L0_gnn_ln_g"][l], a["L0_gnn_ln_b"][l], l == 0)
            if STOP == 3:
                return dump(nc, g, g.h, out)
        mlp(nc, g, g.h, a["L0_gnn_w1"], a["L0_gnn_b1"], a["L0_gnn_w2"], a["L0_gnn_b2"], ACT.Relu, g.x, g.unit)
        if STOP == 4:
            return dump(nc, g, g.x, out)
        routed_ffn(nc, g, a, d)
        if STOP == 5:
            return dump(nc, g, g.x, out)
        graph_convolution(nc, g, a, d)
        if STOP == 6:
            return dump(nc, g, g.x, out)
        transformer(nc, g, a)
        if STOP == 7:
            return dump(nc, g, g.x, out)
        experts(nc, g, a, d)
        dump(nc, g, g.x, out)


_NAMES = ["x", "src", "dst", "L0_gnn_Wq", "L0_gnn_Wk", "L0_gnn_Wv", "L0_gnn_Wo", "L0_gnn_ln_g", "L0_gnn_ln_b", "L0_gnn_w1",
          "L0_gnn_b1", "L0_gnn_w2", "L0_gnn_b2", "L0_mix_w_qkv", "L0_mix_bn_gamma", "L0_mix_bn_beta", "L0_mix_w_dw",
          "L0_mix_w_pw", "L0_mix_w_res", "L0_mix_b_res", "L0_ffn_wr", "L0_ffn_br", "L0_ffn_w1", "L0_ffn_b1", "L0_ffn_w2",
          "L0_ffn_b2", "L1_gnn_W", "L1_mix_Wq", "L1_mix_Wk", "L1_mix_Wv", "L1_mix_Wo", "L1_mix_bo", "L1_mix_ln1_g",
          "L1_mix_ln1_b", "L1_mix_W1", "L1_mix_b1", "L1_mix_W2", "L1_mix_b2", "L1_mix_ln2_g", "L1_mix_ln2_b",
          "L1_ffn_W_gat", "L1_ffn_att_src", "L1_ffn_att_dst", "L1_ffn_b_gat", "L1_ffn_ln_gamma", "L1_ffn_ln_beta",
          "L1_ffn_W1", "L1_ffn_b1", "L1_ffn_W2", "L1_ffn_b2", "L1_ffn_edge_index"]


def _layout(name, a):
    if name == "L0_mix_w_qkv":
        a = a.transpose(2, 1, 0)
    if name == "L0_mix_w_dw":
        a = a.reshape(MIX, 5).transpose(1, 0)
    if name == "L0_mix_w_pw":
        a = a.reshape(6, 4, 32, 32).transpose(1, 3, 0, 2)
    if name == "L0_mix_w_res":
        a = a.reshape(D, 2 * D).transpose(1, 0)
    return np.ascontiguousarray(a)


def kernel(**inputs):
    import concourse.bacc as bacc
    from concourse.bass_utils import run_bass_kernel_spmd

    nc = bacc.Bacc("TRN2", target_bir_lowering=False, num_devices=1)
    arrays, aps = {}, {}
    for name in _NAMES:
        v = _layout(name, np.asarray(inputs[name]))
        arrays["in_" + name] = v
        aps[name] = nc.dram_tensor("in_" + name, v.shape, mybir.dt.from_np(v.dtype), kind="ExternalInput").ap()
    out = nc.dram_tensor("out", (N, D), F32, kind="ExternalOutput").ap()
    gps_program(nc, aps, out)
    return run_bass_kernel_spmd(nc, [arrays], core_ids=[0]).results[0]["out"]
```

```python
from contextlib import ExitStack, contextmanager
import math

import numpy as np
import concourse.bass as bass
from concourse import mybir

F32 = mybir.dt.float32
I32 = mybir.dt.int32
ALU = mybir.AluOpType
ACT = mybir.ActivationFunctionType
AX = mybir.AxisListType.X

N, D, E = 3125, 256, 100000
P = 125
NT = N // P
ET = E // P
NV = 832
CH, CS = 16, NV // 16
HEADS, DK = 8, 32
SEQ = CS * P
G = 8
GG = 4
RG = 2 * G
BIG = 1.0e30
MIX = 768
E2 = 65536
MAXNORM = float(np.float32(1.0) - np.float32(1e-5))
ATANH_MAX = 0.5 * math.log((1.0 + MAXNORM) / (1.0 - MAXNORM))


class Names:
    pass


COUNT = [0]


@contextmanager
def phase(nc, g, *names):
    COUNT[0] += 1
    sems = [nc.alloc_semaphore(f"{n}_{COUNT[0]}") for n in names]
    with nc.Block() as block:
        yield block, dict(zip(names, sems))
    nc.clear_and_free_semaphores(sems)
    nc.all_engine_barrier()


def hold(eng, sem, value):
    eng.wait_ge(sem, value)
    if not isinstance(value, int):
        eng.sem_inc(HELD[str(eng.engine)], 1)


HELD = {}


def hold_on(eng):
    return lambda sem, value: hold(eng, sem, value)


def before(eng, sem, t, unit=1, more=0, light=False):
    (eng.wait_ge if light else hold_on(eng))(sem, (t + 1) * unit + more)


def this(eng, sem, t, unit=1, more=0, light=False):
    (eng.wait_ge if light else hold_on(eng))(sem, (t + 2) * unit + more)


def landed(eng, sem, t, unit, light=False):
    (eng.wait_ge if light else hold_on(eng))(sem, (t + 1) * unit)


class Steps:

    def __init__(self, eng, sem, t=None, per=0):
        self.eng, self.sem, self.t, self.per, self.n = eng, sem, t, per, 0

    def __call__(self, ins):
        self.n += 1
        ins.then_inc(self.sem, 1)
        hold(self.eng, self.sem, self.n if self.t is None else self.t * self.per + self.n)

    def end(self):
        assert self.t is None or self.n == self.per, (self.n, self.per)


def col(ap, t, width=1):
    return ap[:, bass.ds(t * width, width)]


def setup(nc, ctx):
    g = Names()
    arena = ctx.enter_context(nc.sbuf_tensor("arena", [128, 39104], F32))

    def view(off, size, parts=128):
        return arena[0:parts, off:off + size]

    g.view = view
    g.x = view(0, NT * D, P)
    g.h = view(6400, NT * D, P)
    g.b2 = view(12800, NT * D, P)
    g.b3 = view(19200, NT * D, P)
    g.b4 = view(25600, NT * D, P)
    g.b5 = view(32000, NT * D, P)
    g.sums = view(12800, NT * (D + 9), P)
    g.score = view(19430, NV * HEADS, P)
    g.scan = view(26088, SEQ)
    g.link = view(32592, SEQ + 1)
    g.fwd = view(12800, SEQ)

    def sb(name, shape, dt=F32):
        return ctx.enter_context(nc.sbuf_tensor(name, shape, dt))

    visit_src, visit_dst = sb("visit_src", [128, NV], I32), sb("visit_dst", [128, NV], I32)
    visit_rel = sb("visit_rel", [128, NV])
    g.srcv, g.dstv, g.relv = visit_src[0:P, :], visit_dst[0:P, :], visit_rel[0:P, :]
    EC = E2 // 128
    g.srcv_e, g.dstv_e, g.dlo = visit_src[:, 0:EC], visit_dst[:, 0:EC], visit_rel[:, 0:EC].bitcast(I32)
    g.wrow = sb("wrow", [1, NV], I32)
    g.ident = sb("ident", [128, 128])
    g.iota = sb("iota", [128, 128])
    g.ones = sb("ones", [128, 128])
    g.unit = sb("unit", [P, NT])
    g.dinv = sb("dinv", [P, NT])
    g.stat = sb("stat", [P, 8 * NT])
    g.coef = sb("coef", [P, 4 * NT])
    g.eps = sb("eps", [128, 1])
    g.zero = sb("zero", [128, 1])
    g.place_ix = sb("place_ix", [128, 16], I32)
    g.places = view(38400, E2 // 128).bitcast(I32)
    g.w1 = sb("w1", [128, 2048])
    g.w2 = sb("w2", [128, 2048])
    g.vec = sb("vec", [128, 64])
    g.brow = sb("brow", [1, 256])
    g.stage = sb("stage", [P, 512])
    g.ht = sb("ht", [128, MIX])
    g.h1 = sb("h1", [128, 2 * MIX])
    g.o = sb("o", [P, MIX])
    g.dhi = g.h1[:, 0:EC].bitcast(I32)
    g.ps = ctx.enter_context(nc.psum_tensor("ps", [128, 8, 512], F32))
    g.psT = g.ps[:, 0, 0:500]
    for e in (nc.sync, nc.scalar, nc.vector, nc.gpsimd, nc.tensor):
        HELD[str(e.engine)] = nc.alloc_semaphore("held_" + str(e.engine).split(".")[-1])
    return g


def constants(nc, g):
    with phase(nc, g, "made", "filled") as (block, s):
        it = g.view(0, 128).bitcast(I32)

        @block.gpsimd
        def _(pool):
            nc.gpsimd.iota(it, [[1, 128]], base=0, channel_multiplier=0).then_inc(s["made"], 1)
            nc.gpsimd.memset(g.ident[:, :], 0.0).then_inc(s["made"], 1)
            nc.gpsimd.memset(g.ones[:, :], 1.0).then_inc(s["made"], 1)
            nc.gpsimd.memset(g.unit[:, :], 1.0).then_inc(s["made"], 1)
            nc.gpsimd.memset(g.eps[:, :], 1e-5).then_inc(s["made"], 1)
            pool.wait_ge(s["made"], 5)
            nc.gpsimd.affine_select(out=g.ident[:, :], in_=g.ident[:, :], compare_op=ALU.not_equal, fill=1.0,
                                    base=0, pattern=[[-1, 128]], channel_multiplier=1).then_inc(s["filled"], 1)

        @block.vector
        def _(dve):
            dve.wait_ge(s["made"], 5)
            nc.vector.tensor_copy(g.iota[:, :], it).then_inc(s["filled"], 1)


def plan_visits(nc, g, src, dst, d):
    VP, VC = 104, 8
    src_rows = src.rearrange("(t e) -> t e", e=P)
    dst_rows = dst.rearrange("(t e) -> t e", e=P)
    v = g.view
    d0 = v(0, 8 * P, 100).bitcast(I32)
    last = v(1000, 8, 100)
    thr_i = v(1010, 24, 100).bitcast(I32)
    thr = v(1040, 24, 100)
    cmp = v(1070, 8 * 24, 100)
    wl = v(1270, 8, 100)
    tau_i = v(1280, 8, 100).bitcast(I32)
    tau_f = v(1290, 8, 100)
    key = v(1300, 8, 100)
    keyrow = v(1400, ET, VP)
    junk = v(2300, ET, VP)
    vi = v(3200, VC, VP).bitcast(I32)
    vf = v(3210, VC, VP)
    tau = v(3220, VC, VP)
    taui = v(3230, VC, VP).bitcast(I32)
    w = v(3240, VC, VP)
    wi = v(3250, VC, VP).bitcast(I32)
    wbase = v(3260, VC, VP)
    gs = v(4000, VC * P, VP).bitcast(I32)
    gd = v(5000, VC * P, VP).bitcast(I32)
    sf = v(6000, VC * P, VP)
    df = v(7000, VC * P, VP)
    rel = v(8000, VC * P, VP)
    inn = v(9000, VC * P, VP)
    pad = v(10000, 8, 1)
    keys = v(10100, SEQ + 2)
    with phase(nc, g, "loaded", "iotas", "step", "key_ready", "key_stored", "key_back", "tau_ready", "gathered",
               "made", "turned", "kept", "keys_stored", "keys_back", "stored", "pad_ready") as (block, s):

        @block.gpsimd
        def _(pool):
            nc.gpsimd.iota(thr_i, [[P, 24]], base=P, channel_multiplier=0).then_inc(s["iotas"], 1)
            nc.gpsimd.iota(tau_i, [[100, 8]], base=0, channel_multiplier=1).then_inc(s["iotas"], 1)
            nc.gpsimd.iota(vi, [[VP, VC]], base=0, channel_multiplier=1).then_inc(s["iotas"], 1)
            pool.wait_ge(s["tau_ready"], 1)
            for c in range(VC):
                at = bass.IndirectOffsetOnAxis(taui[:, c:c + 1], 0)
                nc.gpsimd.indirect_dma_start(gs[:, c * P:(c + 1) * P], None, src_rows, at).then_inc(s["gathered"], 16)
                nc.gpsimd.indirect_dma_start(gd[:, c * P:(c + 1) * P], None, dst_rows, at).then_inc(s["gathered"], 16)

        @block.sync
        def _(sp):
            sp.dma_start(d0.rearrange("p (k e) -> p k e", k=8),
                         dst.rearrange("(k p e) -> p k e", k=8, e=P)).then_inc(s["loaded"], 16)
            sp.wait_ge(s["key_ready"], 1)
            sp.dma_start(d.key.rearrange("(k p) -> p k", p=100), key,
                         allow_slow_non_contiguous=True).then_inc(s["key_stored"], 16)
            sp.wait_ge(s["key_stored"], 16)
            sp.dma_start(keyrow, d.key.partition_broadcast(VP)).then_inc(s["key_back"], 16)
            sp.wait_ge(s["tau_ready"], 2)
            sp.dma_start(d.w.rearrange("(c p) -> p c", p=VP), wi,
                         allow_slow_non_contiguous=True).then_inc(s["stored"], 16)
            sp.wait_ge(s["stored"], 16)
            sp.dma_start(g.wrow[:, :], d.w.rearrange("(a v) -> a v", a=1)).then_inc(s["stored"], 16)
            sp.wait_ge(s["pad_ready"], 1)
            sp.dma_start(d.keys[0:8].rearrange("(a v) -> a v", a=1), pad).then_inc(s["keys_stored"], 16)
            sp.dma_start(d.keys[8 + NV * P:16 + NV * P].rearrange("(a v) -> a v", a=1), pad).then_inc(s["keys_stored"], 16)
            sp.wait_ge(s["made"], 1)
            sp.dma_start(d.keys[8:8 + NV * P].rearrange("(c p e) -> p c e", c=VC, p=VP),
                         inn.rearrange("p (c e) -> p c e", c=VC)).then_inc(s["keys_stored"], 16)
            sp.wait_ge(s["keys_stored"], 48)
            for c in range(CH):
                sp.dma_start(keys[HEADS * c:HEADS * c + HEADS, :],
                             d.keys[7 + c * SEQ:9 + (c + 1) * SEQ].partition_broadcast(HEADS)).then_inc(s["keys_back"], 16)
            sp.wait_ge(s["stored"], 32)

        @block.vector
        def _(dve):
            step = Steps(dve, s["step"])
            V = nc.vector
            V.memset(pad, -5.0).then_inc(s["pad_ready"], 1)
            dve.wait_ge(s["iotas"], 3)
            dve.wait_ge(s["loaded"], 16)
            step(V.tensor_copy(last, d0[:, P - 1:8 * P:P]))
            step(V.tensor_copy(thr, thr_i))
            step(V.tensor_copy(tau_f, tau_i))
            step(V.tensor_copy(vf, vi))
            c3 = cmp.rearrange("p (k t) -> p k t", t=24)
            step(V.tensor_tensor(c3, last.unsqueeze(2).to_broadcast([100, 8, 24]),
                                 thr.unsqueeze(1).to_broadcast([100, 8, 24]), ALU.is_ge))
            step(V.tensor_reduce(wl, c3, AX, ALU.add))
            V.tensor_tensor(key, wl, tau_f, ALU.add).then_inc(s["key_ready"], 1)
            dve.wait_ge(s["key_back"], 16)
            for c in range(VC):
                step(V.tensor_scalar(junk[:, 0:ET - 1], keyrow[:, 0:ET - 1], vf[:, c:c + 1], 0.0, ALU.is_lt, ALU.add,
                                     accum_out=tau[:, c:c + 1]))
            V.tensor_copy(taui, tau).then_inc(s["tau_ready"], 1)
            step(V.tensor_tensor(w, vf, tau, ALU.subtract))
            step(V.tensor_scalar(wbase, w, float(P), None, ALU.mult))
            step(V.tensor_scalar(w, w, float(NT - 1), None, ALU.min))
            V.tensor_copy(wi, w).then_inc(s["tau_ready"], 1)
            dve.wait_ge(s["gathered"], 32 * VC)
            step(V.tensor_copy(sf, gs))
            step(V.tensor_copy(df, gd))
            for c in range(VC):
                a, b = c * P, (c + 1) * P
                step(V.tensor_scalar(rel[:, a:b], df[:, a:b], wbase[:, c:c + 1], None, ALU.subtract))
            step(V.tensor_scalar(inn, rel, 0.0, None, ALU.is_ge))
            step(V.scalar_tensor_tensor(inn, rel, float(P), inn, ALU.is_lt, ALU.mult))
            V.scalar_tensor_tensor(inn, df, 1.0, inn, ALU.add, ALU.mult).then_inc(s["made"], 1)
            for c in range(VC):
                dve.wait_ge(s["turned"], c + 1)
                out = slice(c * VP, (c + 1) * VP)
                b = g.ps[0:P, 2 * (c % 2), 0:512]
                V.tensor_copy(g.srcv[:, out], b[:, 0:VP])
                V.tensor_copy(g.dstv[:, out], b[:, 128:128 + VP])
                V.tensor_copy(g.relv[:, out], b[:, 256:256 + VP]).then_inc(s["kept"], 1)
            dve.wait_ge(s["keys_back"], 16 * CH)
            dve.wait_ge(s["kept"], VC)
            step(V.tensor_tensor(g.link, keys[:, 1:SEQ + 2], keys[:, 0:SEQ + 1], ALU.not_equal))
            V.tensor_scalar(g.link, g.link, -BIG, None, ALU.mult)

        @block.tensor
        def _(pe):
            pe.wait_ge(s["made"], 1)
            for c in range(VC):
                if c >= 2:
                    pe.wait_ge(s["kept"], c - 1)
                a, b = c * P, (c + 1) * P
                bank = g.ps[0:P, 2 * (c % 2), 0:512]
                nc.tensor.transpose(bank[:, 0:VP], sf[:, a:b], g.ident[0:VP, 0:VP])
                nc.tensor.transpose(bank[:, 128:128 + VP], df[:, a:b], g.ident[0:VP, 0:VP])
                nc.tensor.transpose(bank[:, 256:256 + VP], rel[:, a:b], g.ident[0:VP, 0:VP]).then_inc(s["turned"], 1)


def spill(nc, g, links, out):
    with phase(nc, g, "moved") as (block, s):
        @block.sync
        def _(sp):
            sp.dma_start(links if out else g.link, g.link if out else links).then_inc(s["moved"], 16)
            sp.wait_ge(s["moved"], 16)


def dump(nc, g, ap, out):
    with phase(nc, g, "written") as (block, s):
        @block.sync
        def _(sp):
            sp.dma_start(out.rearrange("(t p) n -> p t n", p=P),
                         ap.rearrange("p (t n) -> p t n", t=NT)).then_inc(s["written"], 16)
            sp.wait_ge(s["written"], 16)


def layernorm(nc, g, x, out, scratch, gamma=None, beta=None):
    X3, O3, S3 = (a.rearrange("p (t n) -> p t n", t=NT) for a in (x, out, scratch))
    mean, var, std, rstd = (g.stat[:, k * NT:(k + 1) * NT] for k in range(4))
    wide = [P, NT, D]
    with phase(nc, g, "step", "centred", "squared", "var_ready", "std_ready", "loaded") as (block, s):
        if gamma is not None:
            @block.sync
            def _(sp):
                sp.dma_start(g.w1[0:P, 0:D], gamma.partition_broadcast(P)).then_inc(s["loaded"], 16)
                sp.dma_start(g.w1[0:P, D:2 * D], beta.partition_broadcast(P)).then_inc(s["loaded"], 16)

        @block.vector
        def _(dve):
            step = Steps(dve, s["step"])
            V = nc.vector
            step(V.tensor_reduce(mean, X3, AX, ALU.add))
            step(V.tensor_scalar(mean, mean, 1.0 / D, None, ALU.mult))
            V.tensor_tensor(O3, X3, mean.unsqueeze(2).to_broadcast(wide), ALU.subtract).then_inc(s["centred"], 1)
            dve.wait_ge(s["squared"], 1)
            V.tensor_reduce(var, S3, AX, ALU.add).then_inc(s["var_ready"], 1)
            dve.wait_ge(s["std_ready"], 1)
            step(V.reciprocal(rstd, std))
            dve.wait_ge(s["centred"], 1)
            step(V.tensor_tensor(O3, O3, rstd.unsqueeze(2).to_broadcast(wide), ALU.mult))
            if gamma is not None:
                dve.wait_ge(s["loaded"], 32)
                step(V.tensor_tensor(O3, O3, g.w1[0:P, 0:D].unsqueeze(1).to_broadcast(wide), ALU.mult))
                step(V.tensor_tensor(O3, O3, g.w1[0:P, D:2 * D].unsqueeze(1).to_broadcast(wide), ALU.add))

        @block.scalar
        def _(act):
            act.wait_ge(s["centred"], 1)
            nc.scalar.activation(scratch, out, ACT.Square).then_inc(s["squared"], 1)
            act.wait_ge(s["var_ready"], 1)
            nc.scalar.activation(std, var, ACT.Sqrt, bias=g.eps[0:P, :], scale=1.0 / D).then_inc(s["std_ready"], 1)


def tile_pass(nc, g, src, nk, outs, loads, finish, scale=None, affine=None, hidden=None, bias=False, tables=None, row=None, side=None):
    C = nk * 128
    nj = hidden[0] // 128 if hidden else 0
    half = nj // 2
    hT = g.ht[:, 0:nk * P].rearrange("p (k r) -> p k r", r=P)
    psT = g.psT[:, 0:nk * P].rearrange("p (k r) -> p k r", r=P)
    h1 = g.h1[:, 0:8 * P].rearrange("p (j r) -> p j r", r=P)

    def up(j):
        return g.ps[:, 2 + j // half, (j % half) * P:(j % half + 1) * P]

    with phase(nc, g, "loaded", "staged", "turned", "fetched", "up_a", "up_b", "act_a", "act_b", "down",
               "stored", "written", "step", "side_a", "side_b") as (block, s):
        if side:
            side(block, s)

        @block.sync
        def _(sp):
            for dst, dram in loads:
                sp.dma_start(dst, dram, allow_slow_non_contiguous=True).then_inc(s["loaded"], 16)
            if tables:
                n = 16 * len(tables)
                sp.sem_inc(s["written"], n)
                with sp.Fori(0, NT) as t:
                    this(sp, s["stored"], t)
                    for dram, ap in tables:
                        sp.dma_start(dram[bass.ds(t * P, P), :], ap).then_inc(s["written"], 16)
                this(sp, s["written"], NT - 1, n)

        @block.scalar
        def _(act):
            act.sem_inc(s["staged"], 1)
            act.sem_inc(s["act_a"], 1)
            act.sem_inc(s["act_b"], 1)
            if hidden:
                act.wait_ge(s["loaded"], 16 * len(loads))

            def stage(t):
                kw = {} if scale is None else {"scale": col(scale, t)}
                nc.scalar.activation(g.stage[:, 0:C], src[:, bass.ds(t * (row or C), C)], ACT.Copy, **kw).then_inc(s["staged"], 1)

            def round_(t, last):
                if not last:
                    this(act, s["turned"], t)
                    stage(t + 1)
                if hidden:
                    for j in range(nj):
                        if j % half == 0:
                            this(act, s["up_b"] if j else s["up_a"], t)
                            if not j:
                                before(act, s["down"], t)
                        ins = nc.scalar.activation(h1[:, j, :], up(j), hidden[1], bias=g.vec[:, j:j + 1])
                        if j % half == half - 1:
                            ins.then_inc(s["act_b"] if j == nj - 1 else s["act_a"], 1)

            stage(0)
            with act.Fori(0, NT - 1) as t:
                round_(t, False)
            round_(NT - 1, True)

        @block.tensor
        def _(pe):
            pe.sem_inc(s["turned"], 1)
            pe.sem_inc(s["up_a"], 1)
            pe.sem_inc(s["up_b"], 1)
            pe.sem_inc(s["down"], 1)

            def turn(t):
                this(pe, s["staged"], t)
                for k in range(nk):
                    ins = nc.tensor.transpose(psT[:, k, :], g.stage[:, k * 128:(k + 1) * 128], g.ident[0:P, 0:P])
                ins.then_inc(s["turned"], 1)

            def round_(t, last):
                this(pe, s["fetched"], t)
                if hidden:
                    for j in range(nj):
                        for k in range(nk):
                            ins = nc.tensor.matmul(up(j), g.w1[:, k * hidden[0] + j * 128:k * hidden[0] + (j + 1) * 128],
                                                   hT[:, k, :], start=(k == 0), stop=(k == nk - 1))
                        if j % half == half - 1:
                            ins.then_inc(s["up_b"] if j == nj - 1 else s["up_a"], 1)
                if not last:
                    turn(t + 1)
                before(pe, s["stored"], t)
                lhs = [h1[:, j, :] for j in range(nj)] if hidden else [hT[:, k, :] for k in range(nk)]
                for m, left in enumerate(lhs):
                    if hidden and m % half == 0:
                        this(pe, s["act_b"] if m else s["act_a"], t)
                    for wt, ps in outs:
                        ins = nc.tensor.matmul(ps, left, wt(m), start=(m == 0), stop=(m == len(lhs) - 1 and not bias))
                if bias:
                    for wt, ps in outs:
                        ins = nc.tensor.matmul(ps, g.ones[0:1, 0:P], g.brow[0:1, :], start=False, stop=True)
                ins.then_inc(s["down"], 1)

            pe.wait_ge(s["loaded"], 16 * len(loads))
            turn(0)
            with pe.Fori(0, NT - 1) as t:
                round_(t, False)
            round_(NT - 1, True)

        @block.vector
        def _(dve):
            dve.sem_inc(s["fetched"], 1)
            dve.sem_inc(s["stored"], 1)
            dve.wait_ge(s["loaded"], 16 * len(loads))

            def fetch(t):
                this(dve, s["turned"], t)
                if affine is None:
                    ins = nc.vector.tensor_copy(hT, psT)
                else:
                    for k in range(nk):
                        ins = nc.vector.tensor_scalar(hT[:, k, :], psT[:, k, :], affine[0][:, k:k + 1],
                                                      affine[1][:, k:k + 1], ALU.mult, ALU.add)
                ins.then_inc(s["fetched"], 1)

            def round_(t, last):
                if hidden and not last:
                    this(dve, s["up_b"], t)
                    fetch(t + 1)
                this(dve, s["down"], t)
                if not hidden and not last:
                    fetch(t + 1)
                if tables:
                    before(dve, s["written"], t, 16 * len(tables))
                finish(nc.vector, t, lambda per: Steps(dve, s["step"], t, per)).then_inc(s["stored"], 1)

            fetch(0)
            with dve.Fori(0, NT - 1) as t:
                round_(t, False)
            round_(NT - 1, True)


def penalty_indices(nc, g, a):
    EC = E2 // 128
    sI, dI = g.view(19200, EC).bitcast(I32), g.view(19800, EC).bitcast(I32)
    sF, dF = g.view(20400, EC), g.view(21000, EC)
    ei = a["L1_ffn_edge_index"]
    with phase(nc, g, "loaded", "step") as (block, s):
        @block.sync
        def _(sp):
            sp.dma_start(sI, ei[0].rearrange("(p c) -> p c", p=128)).then_inc(s["loaded"], 16)
            sp.dma_start(dI, ei[1].rearrange("(p c) -> p c", p=128)).then_inc(s["loaded"], 16)

        @block.vector
        def _(dve):
            V = nc.vector
            step = Steps(dve, s["step"])
            dve.wait_ge(s["loaded"], 32)
            step(V.memset(g.zero[:, :], 0.0))
            step(V.tensor_copy(sF, sI))
            step(V.tensor_copy(dF, dI))
            step(V.tensor_scalar(sF, sF, float(N - 1), None, ALU.min))
            step(V.scalar_tensor_tensor(dF, dF, float(N), sF, ALU.mult, ALU.add))
            step(V.tensor_copy(g.places, dF))


def fill_penalties(nc, g, d):
    def side(block, s):
        fill = g.view(19200, N, P)

        @block.gpsimd
        def _(pool):
            nc.gpsimd.memset(fill, -BIG).then_inc(s["side_a"], 1)
            pool.wait_ge(s["side_a"], 1)
            for t in range(NT):
                nc.gpsimd.dma_start(d.pen[t * P * N:(t + 1) * P * N].rearrange("(p n) -> p n", p=P),
                                    fill).then_inc(s["side_b"], 16)
            pool.wait_ge(s["side_b"], 16 * NT)
    return side


def lift_penalties(nc, g, d, start, count):
    GS = 16

    def side(block, s):
        @block.gpsimd
        def _(pool):
            pool.sem_inc(s["side_a"], 1)
            with pool.Fori(0, count // GS) as i:
                nc.gpsimd.tensor_copy(g.place_ix[:, :], g.places[:, bass.ds(i * GS + start, GS)]).then_inc(s["side_a"], 1)
                this(pool, s["side_a"], i)
                for j in range(GS):
                    nc.gpsimd.indirect_dma_start(d.pen.rearrange("(n o) -> n o", o=1),
                                                 bass.IndirectOffsetOnAxis(g.place_ix[:, j:j + 1], 0), g.zero[:, :], None,
                                                 bounds_check=N * N - 1, oob_is_err=False).then_inc(s["side_b"], 16)
                    hold(pool, s["side_b"], i * (16 * GS) + 16 * (j + 1))
    return side


def add_into(ps, dst, coef, width=D):
    def finish(V, t, steps):
        return V.scalar_tensor_tensor(col(dst, t, width), ps, col(coef, t), col(dst, t, width), ALU.mult, ALU.add)
    return finish


def mm_weights(buf, n):
    return lambda k: buf[:, k * n:(k + 1) * n]


def split_k(dram, nk):
    return dram.rearrange("(k p) n -> p k n", k=nk)


def w3(buf, nk, n):
    return buf[:, 0:nk * n].rearrange("p (k n) -> p k n", k=nk)


def mlp(nc, g, src, w1, b1, w2, b2, func, dst, coef, affine=None, scale=None, extra=(), side=None):
    H = w1.shape[1]
    nj = H // 128
    down = g.ps[0:P, 4, 0:D]
    loads = [(w3(g.w1, 2, H), split_k(w1, 2)), (w3(g.w2, nj, D), split_k(w2, nj)),
             (g.vec[:, 0:nj], b1.rearrange("(j p) -> p j", p=128)),
             (g.brow[:, :], b2.rearrange("(a n) -> a n", a=1))] + list(extra)
    tile_pass(nc, g, src, 2, [(mm_weights(g.w2, D), down)], loads, add_into(down, dst, coef),
              scale=scale, hidden=(H, func), bias=True, affine=affine, side=side)



def edge_scores(nc, g, q, k_table):
    kb = [g.scan[0:P, j * D:(j + 1) * D] for j in range(RG)]
    oh = [g.w1[0:P, j * P:(j + 1) * P] for j in range(G)]
    ohT = [g.w2[0:P, (G + j) * P:(G + j + 1) * P] for j in range(G)]
    pr = [g.h1[0:P, j * D:(j + 1) * D] for j in range(GG)]
    ix = g.ht[0:P, 0:RG].bitcast(I32)
    psQ = [g.ps[0:P, j, 0:D] for j in range(G)]
    psT = [g.ps[0:P, j, D:D + P] for j in range(G)]
    names = [f"got{j}" for j in range(RG)] + [f"{n}{j}" for n in ("hot", "turned", "kept", "picked", "used") for j in range(G)]
    with phase(nc, g, "indexed", "reduced", *names) as (block, s):
        got = [s[f"got{j}"] for j in range(RG)]
        hot, turned, kept, picked, used = ([s[f"{n}{j}"] for j in range(G)] for n in ("hot", "turned", "kept", "picked", "used"))

        @block.gpsimd
        def _(pool):
            with pool.Fori(0, NV // RG) as i:
                for a in range(0, RG, GG):
                    last = a + GG - 1
                    hold(pool, used[last % G], i * 2 + last // G + 1)
                    nc.gpsimd.tensor_copy(ix[:, a:a + GG], g.srcv[:, bass.ds(i * RG + a, GG)]).then_inc(s["indexed"], 1)
                    hold(pool, s["indexed"], i * (RG // GG) + a // GG + 1)
                    for j in range(a, a + GG):
                        nc.gpsimd.indirect_dma_start(kb[j], None, k_table,
                                                     bass.IndirectOffsetOnAxis(ix[:, j:j + 1], 0)).then_inc(got[j], 16)

        @block.scalar
        def _(act):
            for q_ in kept:
                act.sem_inc(q_, 1)
            with act.Fori(0, NV // G) as i:
                for j in range(G):
                    this(act, turned[j], i, light=True)
                    nc.scalar.copy(ohT[j], psT[j]).then_inc(kept[j], 1)

        @block.tensor
        def _(pe):
            for q_ in turned + picked:
                pe.sem_inc(q_, 1)

            def turn(i, j):
                this(pe, hot[j], i, light=True)
                nc.tensor.transpose(psT[j], oh[j], g.ident[0:P, 0:P]).then_inc(turned[j], 1)

            def pick(i, j):
                tile = pe.value_load(g.wrow[0:1, bass.ds(i * G + j, 1)], min_val=0, max_val=NT - 1)
                this(pe, kept[j], i, light=True)
                before(pe, used[j], i, more=1, light=True)
                nc.tensor.matmul(psQ[j], ohT[j], q[:, bass.ds(tile * D, D)], start=True, stop=True).then_inc(picked[j], 1)

            with pe.Fori(0, NV // G) as i:
                turn(i, 0)
                turn(i, 1)
                for j in range(G):
                    if j + 2 < G:
                        turn(i, j + 2)
                    pick(i, j)

        @block.vector
        def _(dve):
            for q_ in used + hot + [s["reduced"]]:
                dve.sem_inc(q_, 1)

            def one_hot(i, j):
                nc.vector.tensor_scalar(oh[j], g.iota[0:P, 0:P], g.relv[:, bass.ds(i * G + j, 1)], None,
                                        ALU.is_equal).then_inc(hot[j], 1)

            def dots(i, half, u, a):
                hold(dve, s["reduced"], i * 2 + 1 + a // GG)
                for j in range(a, a + GG):
                    landed(dve, got[u * G + j], half, 16, light=True)
                    this(dve, picked[j], i, light=True)
                    nc.vector.tensor_tensor(pr[j - a], kb[u * G + j], psQ[j], ALU.mult).then_inc(used[j], 1)
                this(dve, used[a + GG - 1], i, more=1)
                for j in range(a, a + GG):
                    ins = nc.vector.tensor_reduce(g.score[:, bass.ds(i * (G * HEADS) + j * HEADS, HEADS)],
                                                  pr[j - a].rearrange("p (h d) -> p h d", h=HEADS), AX, ALU.add)
                ins.then_inc(s["reduced"], 1)

            def round_(i, half, u, last):
                for a in range(0, G, GG):
                    for j in range(a, a + GG):
                        if a == 0:
                            one_hot(i, j + GG)
                        elif not last:
                            one_hot(i + 1, j - GG)
                    dots(i, half, u, a)

            for q_ in used:
                dve.sem_inc(q_, 1)
            for j in range(GG):
                one_hot(0, j)
            with dve.Fori(0, NV // RG - 1) as half:
                round_(half * 2, half, 0, False)
                round_(half * 2 + 1, half, 1, False)
            round_(NV // G - 2, NV // RG - 1, 0, False)
            round_(NV // G - 1, NV // RG - 1, 1, True)


def segment_softmax(nc, g):
    sc4 = g.score.rearrange("p (c s h) -> p c s h", c=CH, s=CS)
    with ExitStack() as ctx:
        def sb(name, shape):
            return ctx.enter_context(nc.sbuf_tensor(name, shape, F32))
        st = g.o[0:P, 0:128]
        st2 = g.h1[:, 0:P]
        fwd = g.fwd
        ends = g.w1[:, 0:2]
        rows = g.w2[0:1, 0:4 * 128]
        init = g.w1[:, 4:5]
        psA = g.ps[:, 0, 0:P]
        with phase(nc, g, "staged", "turned", "kept") as (block, s):
            @block.vector
            def _(dve):
                dve.sem_inc(s["staged"], 1)
                with dve.Fori(0, CS) as i:
                    before(dve, s["turned"], i)
                    nc.vector.tensor_copy(st.rearrange("p (c h) -> p c h", c=CH),
                                          sc4[:, :, bass.ds(i, 1), :].rearrange("p c s h -> p c (s h)")).then_inc(s["staged"], 1)

            @block.tensor
            def _(pe):
                pe.sem_inc(s["turned"], 1)
                with pe.Fori(0, CS) as i:
                    this(pe, s["staged"], i)
                    before(pe, s["kept"], i)
                    nc.tensor.transpose(psA, st, g.ident[0:P, 0:P]).then_inc(s["turned"], 1)

            @block.scalar
            def _(act):
                act.sem_inc(s["kept"], 1)
                with act.Fori(0, CS) as i:
                    this(act, s["turned"], i)
                    nc.scalar.copy(col(g.scan, i, P), psA).then_inc(s["kept"], 1)

        with phase(nc, g, "step", "put", "rowed", "carried", "turned_back") as (block, s):
            psR = g.ps[0:1, 1, 0:256]
            psC = g.ps[:, 2, 0:1]

            @block.vector
            def _(dve):
                V = nc.vector
                step = Steps(dve, s["step"])
                for n in range(2):
                    if n == 0:
                        dst, data, link = fwd, g.scan, g.link[:, 0:SEQ]
                        end = SEQ - 1
                    else:
                        dst, data, link = g.scan[:, ::-1], fwd[:, ::-1], g.link[:, 1:SEQ + 1][:, ::-1]
                        end = 0
                    step(V.tensor_reduce(ends[:, 0:1], g.link[:, n:SEQ + n], AX, ALU.min))
                    step(V.tensor_tensor_scan(dst, link, data, -BIG, ALU.add, ALU.max))
                    tail = fwd[:, end:end + 1] if n == 0 else g.scan[:, end:end + 1]
                    V.tensor_copy(ends[:, 1:2], tail).then_inc(s["put"], 1)
                    dve.wait_ge(s["rowed"], n + 1)
                    step(V.tensor_copy(rows[:, 0:256], psR))
                    step(V.memset(rows[:, 384:512], -BIG))
                    for h in range(HEADS):
                        a = rows[0:1, h:128:HEADS]
                        b = rows[0:1, 128 + h:256:HEADS]
                        o = rows[0:1, 256 + h:384:HEADS]
                        if n:
                            a, b, o = a[:, ::-1], b[:, ::-1], o[:, ::-1]
                        step(V.tensor_tensor_scan(o, a, b, -BIG, ALU.add, ALU.max))
                    if n == 0:
                        V.tensor_copy(rows[:, 384 + HEADS:512], rows[:, 256:384 - HEADS]).then_inc(s["carried"], 1)
                    else:
                        V.tensor_copy(rows[:, 384:512 - HEADS], rows[:, 256 + HEADS:384]).then_inc(s["carried"], 1)
                    dve.wait_ge(s["turned_back"], n + 1)
                    step(V.tensor_copy(init[:, :], psC))
                    if n == 0:
                        step(V.tensor_tensor_scan(fwd, link, data, init[:, :], ALU.add, ALU.max))
                    else:
                        step(V.tensor_tensor_scan(dst, link, data, init[:, :], ALU.add, ALU.max))

            @block.tensor
            def _(pe):
                for n in range(2):
                    pe.wait_ge(s["put"], n + 1)
                    nc.tensor.transpose(psR[:, 0:128], ends[:, 0:1], g.ident[:, :])
                    nc.tensor.transpose(psR[:, 128:256], ends[:, 1:2], g.ident[:, :]).then_inc(s["rowed"], 1)
                    pe.wait_ge(s["carried"], n + 1)
                    nc.tensor.matmul(psC, rows[0:1, 384:512], g.ones[0:1, 0:1], start=True, stop=True).then_inc(s["turned_back"], 1)

        with phase(nc, g, "staged", "turned", "kept", "maxed") as (block, s):
            psB = g.ps[0:P, 0, 0:128]
            psM = g.ps[0:P, 1, 0:128]
            @block.scalar
            def _(act):
                act.sem_inc(s["staged"], 1)
                with act.Fori(0, CS) as i:
                    before(act, s["turned"], i)
                    nc.scalar.copy(st2, col(g.scan, i, P)).then_inc(s["staged"], 1)

            @block.tensor
            def _(pe):
                pe.sem_inc(s["turned"], 1)
                with pe.Fori(0, CS) as i:
                    this(pe, s["staged"], i)
                    before(pe, s["kept"], i)
                    nc.tensor.transpose(psB, st2, g.ident[:, :]).then_inc(s["turned"], 1)

            @block.vector
            def _(dve):
                dve.sem_inc(s["kept"], 1)
                with dve.Fori(0, CS) as i:
                    this(dve, s["turned"], i)
                    sl = sc4[:, :, bass.ds(i, 1), :].rearrange("p c s h -> p c (s h)")
                    nc.vector.tensor_tensor(sl, sl, psB.rearrange("p (c h) -> p c h", c=CH), ALU.subtract).then_inc(s["kept"], 1)

        with phase(nc, g, "done") as (block, s):
            @block.scalar
            def _(act):
                nc.scalar.activation(g.score, g.score, ACT.Exp, scale=1.0 / math.sqrt(DK)).then_inc(s["done"], 1)
                act.wait_ge(s["done"], 1)


def edge_sums(nc, g, table, acc, weighted):
    ncol = D + 9 if weighted else D
    ring = g.scan if weighted else g.score
    vb = [ring[0:P, j * D:(j + 1) * D] for j in range(RG)]
    ms = [g.w1[0:P, j * (D + 9):(j + 1) * (D + 9)] if j < 7 else g.h1[0:P, 0:D + 9] for j in range(G)]
    oh = [g.w2[0:P, j * P:(j + 1) * P] for j in range(G)]
    ix = g.ht[0:P, 0:RG].bitcast(I32)
    names = [f"got{j}" for j in range(RG)] + [f"{n}{j}" for n in ("hot", "weighed", "summed", "added") for j in range(G)]
    with phase(nc, g, "indexed", "zeroed", "side", *names) as (block, s):
        got = [s[f"got{j}"] for j in range(RG)]
        hot, weighed, summed, added = ([s[f"{n}{j}"] for j in range(G)] for n in ("hot", "weighed", "summed", "added"))
        freed = weighed if weighted else summed
        sm = 0 if weighted else 1

        @block.gpsimd
        def _(pool):
            with pool.Fori(0, NV // RG) as i:
                for a in range(0, RG, GG):
                    last = a + GG - 1
                    hold(pool, freed[last % G], i * 2 + last // G + 1)
                    nc.gpsimd.tensor_copy(ix[:, a:a + GG], g.srcv[:, bass.ds(i * RG + a, GG)]).then_inc(s["indexed"], 1)
                    hold(pool, s["indexed"], i * (RG // GG) + a // GG + 1)
                    for j in range(a, a + GG):
                        nc.gpsimd.indirect_dma_start(vb[j], None, table,
                                                     bass.IndirectOffsetOnAxis(ix[:, j:j + 1], 0)).then_inc(got[j], 16)

        @block.scalar
        def _(act):
            if weighted:
                act.sem_inc(s["side"], G)
                act.wait_ge(s["zeroed"], 2)
                with act.Fori(0, NV // G) as i:
                    for j in range(G):
                        before(act, summed[j], i, more=sm)
                        nc.scalar.copy(ms[j][:, D:D + HEADS],
                                       g.score[:, bass.ds(i * (G * HEADS) + j * HEADS, HEADS)]).then_inc(s["side"], 1)

        @block.vector
        def _(dve):
            V = nc.vector
            V.memset(acc, 0.0).then_inc(s["zeroed"], 1)
            for j in range(G if weighted else 0):
                ins = V.memset(ms[j][:, D:D + 9], 1.0)
            if weighted:
                ins.then_inc(s["zeroed"], 1)
            dve.wait_ge(s["zeroed"], 2 if weighted else 1)
            for q in hot + weighed + weighed + added:
                dve.sem_inc(q, 1)

            def weigh(i, half, u, j):
                V.tensor_scalar(oh[j], g.iota[0:P, 0:P], g.relv[:, bass.ds(i * G + j, 1)], None,
                                ALU.is_equal).then_inc(hot[j], 1)
                if weighted:
                    landed(dve, got[u * G + j], half, 16, light=True)
                    V.tensor_tensor(ms[j][:, 0:D].rearrange("p (h d) -> p h d", h=HEADS),
                                    vb[u * G + j].rearrange("p (h d) -> p h d", h=HEADS),
                                    g.score[:, bass.ds(i * (G * HEADS) + j * HEADS, HEADS)].unsqueeze(2)
                                    .to_broadcast([P, HEADS, DK]), ALU.mult).then_inc(weighed[j], 1)

            def add(i, j):
                tile = dve.value_load(g.wrow[0:1, bass.ds(i * G + j, 1)], min_val=0, max_val=NT - 1)
                this(dve, summed[j], i, more=sm, light=True)
                if j:
                    this(dve, added[j - 1], i, light=True)
                else:
                    before(dve, added[G - 1], i, light=True)
                V.tensor_tensor(acc[:, bass.ds(tile * ncol, ncol)], acc[:, bass.ds(tile * ncol, ncol)],
                                g.ps[0:P, j, 0:ncol], ALU.add).then_inc(added[j], 1)

            def round_(i, half, u, first):
                for j in range(G):
                    weigh(i, half, u, j)
                    if j >= GG:
                        add(i, j - GG)
                    elif not first:
                        add(i - 1, j + GG)

            R = NV // G
            round_(0, 0, 0, True)
            with dve.Fori(0, R // 2 - 1) as h:
                round_(h * 2 + 1, h, 1, False)
                round_(h * 2 + 2, h + 1, 0, False)
            round_(R - 1, R // 2 - 1, 1, False)
            for j in range(GG, G):
                add(R - 1, j)

        @block.tensor
        def _(pe):
            for q in summed:
                pe.sem_inc(q, 1 + sm)
            with pe.Fori(0, NV // RG) as half:
                for u in range(2):
                    i = half * 2 + u
                    for j in range(G):
                        if weighted:
                            this(pe, weighed[j], i, more=1, light=True)
                            pe.wait_ge(s["side"], i * G + (G + j + 1))
                        else:
                            this(pe, hot[j], i, light=True)
                            landed(pe, got[u * G + j], half, 16, light=True)
                        rows = ms[j][:, 0:ncol] if weighted else vb[u * G + j]
                        nc.tensor.matmul(g.ps[0:P, j, 0:ncol], oh[j], rows, start=True, stop=True).then_inc(summed[j], 1)



def norm_factor(V, step, out, sumsq_root, limit):
    step(V.tensor_scalar(sumsq_root, sumsq_root, 1e-15, None, ALU.max))
    step(V.reciprocal(out, sumsq_root))
    step(V.tensor_scalar(out, out, limit, 1.0, ALU.mult, ALU.min))


def mix(nc, g, xn, x, w_qkv, gamma, beta, w_dw, w_pw, w_res, b_res):
    nq, n2 = g.stat[:, 0:NT], g.stat[:, NT:2 * NT]
    za, zb = g.stat[:, 2 * NT:3 * NT], g.stat[:, 3 * NT:4 * NT]
    s1 = g.coef[:, 0:NT]
    XN3 = xn.rearrange("p (t n) -> p t n", t=NT)
    S3 = g.b2.rearrange("p (t n) -> p t n", t=NT)
    with phase(nc, g, "step", "squared", "summed", "rooted", "ready", "logged") as (block, s):
        @block.scalar
        def _(act):
            nc.scalar.activation(g.b2, xn, ACT.Square).then_inc(s["squared"], 1)
            act.wait_ge(s["summed"], 1)
            nc.scalar.activation(nq, n2, ACT.Sqrt).then_inc(s["rooted"], 1)
            act.wait_ge(s["ready"], 1)
            nc.scalar.activation(za, n2, ACT.Ln, bias=1.0, scale=1.0)
            nc.scalar.activation(zb, n2, ACT.Ln, bias=1.0, scale=-1.0).then_inc(s["logged"], 1)

        @block.vector
        def _(dve):
            V = nc.vector
            step = Steps(dve, s["step"])
            dve.wait_ge(s["squared"], 1)
            V.tensor_reduce(n2, S3, AX, ALU.add).then_inc(s["summed"], 1)
            dve.wait_ge(s["rooted"], 1)
            step(V.tensor_scalar(nq, nq, 1e-15, None, ALU.max))
            step(V.reciprocal(s1, nq))
            V.tensor_scalar(n2, nq, MAXNORM, None, ALU.min).then_inc(s["ready"], 1)
            dve.wait_ge(s["logged"], 1)
            step(V.tensor_tensor(za, za, zb, ALU.subtract))
            step(V.scalar_tensor_tensor(s1, za, 0.5, s1, ALU.mult, ALU.mult))

    H1T = g.view(19200, 6 * N)
    H3 = H1T.rearrange("p (j n) -> p j n", j=6)
    psA = g.ps[:, 2, 0:4 * P].rearrange("p (j r) -> p j r", r=P)
    psB = g.ps[:, 3, 0:2 * P].rearrange("p (j r) -> p j r", r=P)
    psT = g.psT[:, 0:2 * P].rearrange("p (k r) -> p k r", r=P)
    hT = g.ht[:, 0:2 * P].rearrange("p (k r) -> p k r", r=P)
    with phase(nc, g, "loaded", "staged", "turned", "fetched", "made", "kept") as (block, s):
        @block.sync
        def _(sp):
            sp.dma_start(w3(g.w1, 2, MIX), split_k(w_qkv[2], 2)).then_inc(s["loaded"], 16)

        @block.scalar
        def _(act):
            act.sem_inc(s["staged"], 1)
            with act.Fori(0, NT) as t:
                before(act, s["turned"], t)
                nc.scalar.activation(g.stage[:, 0:D], col(xn, t, D), ACT.Copy, scale=col(s1, t)).then_inc(s["staged"], 1)

        @block.tensor
        def _(pe):
            pe.sem_inc(s["turned"], 1)
            pe.sem_inc(s["made"], 1)
            pe.wait_ge(s["loaded"], 16)
            with pe.Fori(0, NT) as t:
                this(pe, s["staged"], t)
                for k in range(2):
                    ins = nc.tensor.transpose(psT[:, k, :], g.stage[:, k * 128:(k + 1) * 128], g.ident[0:P, 0:P])
                ins.then_inc(s["turned"], 1)
                this(pe, s["fetched"], t)
                before(pe, s["kept"], t)
                for j in range(6):
                    ps = psA[:, j, :] if j < 4 else psB[:, j - 4, :]
                    for k in range(2):
                        ins = nc.tensor.matmul(ps, g.w1[:, k * MIX + j * 128:k * MIX + (j + 1) * 128], hT[:, k, :],
                                               start=(k == 0), stop=(k == 1))
                ins.then_inc(s["made"], 1)

        @block.vector
        def _(dve):
            dve.sem_inc(s["fetched"], 1)
            dve.sem_inc(s["kept"], 1)
            with dve.Fori(0, NT) as t:
                this(dve, s["turned"], t)
                before(dve, s["made"], t)
                nc.vector.tensor_copy(hT, psT).then_inc(s["fetched"], 1)
                this(dve, s["made"], t)
                nc.vector.tensor_copy(H3[:, 0:4, bass.ds(t * P, P)], psA)
                nc.vector.tensor_copy(H3[:, 4:6, bass.ds(t * P, P)], psB).then_inc(s["kept"], 1)

    mean, nmean, var, sc, sh = (g.vec[:, 6 * k:6 * k + 6] for k in range(5))
    gb, bb, dw = (g.vec[:, 6 * k:6 * k + 6] for k in range(5, 8))
    BD = g.w1[:, 0:MIX].rearrange("p (j o) -> p j o", j=6)
    brw = g.w1[0:P, MIX:MIX + D]
    with phase(nc, g, "loaded", "zeroed", "placed", "step", "means", "squares", "rooted", "ready", "done") as (block, s):
        @block.sync
        def _(sp):
            for a, b in ((gb, gamma), (bb, beta), (dw, w_dw[2])):
                sp.dma_start(a, b.rearrange("(j p) -> p j", p=128), allow_slow_non_contiguous=True).then_inc(s["loaded"], 16)
            sp.dma_start(brw, b_res.partition_broadcast(P)).then_inc(s["loaded"], 16)
            sp.dma_start(w3(g.w2, 4, D), split_k(w_res, 4)).then_inc(s["loaded"], 16)
            sp.wait_ge(s["zeroed"], 1)
            for q in range(4):
                sp.dma_start(BD[32 * q:32 * q + 32, :, 32 * q:32 * q + 32], w_pw[q]).then_inc(s["placed"], 16)

        @block.scalar
        def _(act):
            act.wait_ge(s["means"], 1)
            for j in range(6):
                ins = nc.scalar.activation(g.view(12800, N), H3[:, j, :], ACT.Square, bias=nmean[:, j:j + 1],
                                           accum_out=var[:, j:j + 1])
                ins.then_inc(s["squares"], 1)
                act.wait_ge(s["squares"], j + 1)
            nc.scalar.activation(sc, var, ACT.Sqrt, bias=g.eps[:, :], scale=1.0 / N).then_inc(s["rooted"], 1)
            act.wait_ge(s["ready"], 1)
            for j in range(6):
                ins = nc.scalar.activation(H3[:, j, :], H3[:, j, :], ACT.Relu, bias=sh[:, j:j + 1], scale=sc[:, j:j + 1])
            ins.then_inc(s["done"], 1)
            act.wait_ge(s["done"], 1)

        @block.vector
        def _(dve):
            V = nc.vector
            step = Steps(dve, s["step"])
            V.memset(g.w1[:, 0:MIX], 0.0).then_inc(s["zeroed"], 1)
            step(V.tensor_reduce(mean, H3, AX, ALU.add))
            step(V.tensor_scalar(mean, mean, 1.0 / N, None, ALU.mult))
            V.tensor_scalar(nmean, mean, -1.0, None, ALU.mult).then_inc(s["means"], 1)
            dve.wait_ge(s["loaded"], 16 * 5)
            dve.wait_ge(s["placed"], 64)
            for j in range(6):
                V.tensor_scalar(BD[:, j, :], BD[:, j, :], dw[:, j:j + 1], None, ALU.mult)
            dve.wait_ge(s["rooted"], 1)
            step(V.reciprocal(sc, sc))
            step(V.tensor_tensor(sc, sc, gb, ALU.mult))
            step(V.tensor_tensor(sh, mean, sc, ALU.mult))
            V.tensor_tensor(sh, bb, sh, ALU.subtract).then_inc(s["ready"], 1)

    FT = g.b2
    psR = g.ps[0:P, 0:2, 0:384]
    psS = g.ps[0:P, 2:4, 0:384]
    psO = g.ps[:, 4, 0:4 * P].rearrange("p (k r) -> p k r", r=P)
    psF = g.ps[0:P, 5, 0:D]
    with ExitStack() as ctx:
        def sb(name, shape):
            return ctx.enter_context(nc.sbuf_tensor(name, shape, F32))
        cat = sb("cat", [P, 2 * MIX])
        nn = sb("nn", [P, 8])
        ks = sb("ks", [P, 16])
        junk = g.h1[0:P, :]
        num = g.stage[:, 0:512]
        den = g.o[:, 0:512]
        hjT = g.ht[:, 0:6 * P].rearrange("p (j r) -> p j r", r=P)
        oT = g.h1[:, 0:4 * P].rearrange("p (k r) -> p k r", r=P)
        PER = 15
        with phase(nc, g, "taken", "turned", "sq1", "nn1", "sq2", "nn2", "cat_ready", "sq3", "nn3", "out_ready",
                   "oturned", "ofetched", "made", "kept", "step") as (block, s):
            @block.tensor
            def _(pe):
                for q in (s["turned"], s["oturned"], s["made"]):
                    pe.sem_inc(q, 1)
                with pe.Fori(0, NT) as t:
                    this(pe, s["taken"], t)
                    before(pe, s["cat_ready"], t)
                    for j in range(6):
                        nc.tensor.transpose(psR[:, j // 3, (j % 3) * 128:(j % 3 + 1) * 128], hjT[:, j, :], g.ident[:, :])
                    for j in range(6):
                        ins = nc.tensor.matmul(psS[:, j // 3, (j % 3) * 128:(j % 3 + 1) * 128], hjT[:, j, :], BD[:, j, :],
                                               start=True, stop=True)
                    ins.then_inc(s["turned"], 1)
                    this(pe, s["out_ready"], t)
                    for k in range(4):
                        ins = nc.tensor.transpose(psO[:, k, :], num[:, k * 128:(k + 1) * 128], g.ident[0:P, 0:P])
                    ins.then_inc(s["oturned"], 1)
                    this(pe, s["ofetched"], t)
                    before(pe, s["kept"], t)
                    for k in range(4):
                        ins = nc.tensor.matmul(psF, oT[:, k, :], g.w2[:, k * D:(k + 1) * D], start=(k == 0), stop=(k == 3))
                    ins.then_inc(s["made"], 1)

            @block.scalar
            def _(act):
                for q in (s["sq1"], s["nn1"], s["sq2"], s["nn2"], s["sq3"], s["nn3"], s["ofetched"]):
                    act.sem_inc(q, 1)
                with act.Fori(0, NT) as t:
                    this(act, s["turned"], t)
                    nc.scalar.activation(junk[:, 0:MIX].rearrange("p (a b) -> p a b", a=2), psR, ACT.Square, accum_out=nn[:, 0:1]).then_inc(s["sq1"], 1)
                    this(act, s["sq1"], t)
                    nc.scalar.activation(nn[:, 1:2], nn[:, 0:1], ACT.Sqrt).then_inc(s["nn1"], 1)
                    this(act, s["cat_ready"], t)
                    nc.scalar.activation(junk, cat[:, :], ACT.Square, accum_out=nn[:, 2:3]).then_inc(s["sq2"], 1)
                    this(act, s["sq2"], t)
                    nc.scalar.activation(nn[:, 3:4], nn[:, 2:3], ACT.Sqrt).then_inc(s["nn2"], 1)
                    this(act, s["out_ready"], t)
                    nc.scalar.activation(junk[:, 0:512], num, ACT.Square, accum_out=nn[:, 5:6]).then_inc(s["sq3"], 1)
                    this(act, s["sq3"], t)
                    nc.scalar.activation(nn[:, 6:7], nn[:, 5:6], ACT.Sqrt).then_inc(s["nn3"], 1)
                    this(act, s["oturned"], t)
                    this(act, s["nn3"], t)
                    nc.scalar.copy(oT, psO).then_inc(s["ofetched"], 1)

            @block.vector
            def _(dve):
                V = nc.vector
                for q in (s["taken"], s["cat_ready"], s["out_ready"], s["kept"]):
                    dve.sem_inc(q, 1)
                with dve.Fori(0, NT) as t:
                    step = Steps(dve, s["step"], t, PER)
                    before(dve, s["made"], t)
                    V.tensor_copy(hjT, H3[:, :, bass.ds(t * P, P)]).then_inc(s["taken"], 1)
                    this(dve, s["nn1"], t)
                    norm_factor(V, step, nn[:, 7:8], nn[:, 1:2], ATANH_MAX)
                    step(V.tensor_scalar(cat[:, 0:MIX].rearrange("p (a b) -> p a b", a=2), psR, nn[:, 7:8], None, ALU.mult))
                    V.tensor_scalar(cat[:, MIX:2 * MIX].rearrange("p (a b) -> p a b", a=2), psS, nn[:, 7:8], None,
                                    ALU.mult).then_inc(s["cat_ready"], 1)
                    this(dve, s["nn2"], t)
                    norm_factor(V, step, nn[:, 4:5], nn[:, 3:4], ATANH_MAX)
                    c3 = cat[:, :].rearrange("p (g c) -> p g c", g=16)
                    q, k, v = (c3[:, :, c * 32:(c + 1) * 32] for c in range(3))
                    n3 = num.rearrange("p (g d) -> p g d", g=16)
                    d3 = den.rearrange("p (g d) -> p g d", g=16)
                    V.tensor_scalar(c3[:, :, 0:64], c3[:, :, 0:64], nn[:, 4:5], 0.0, ALU.mult, ALU.max)
                    step(V.tensor_scalar(v, v, nn[:, 4:5], None, ALU.mult))
                    V.tensor_reduce(ks[:, :], k, AX, ALU.add)
                    step(V.tensor_scalar(d3, v, 1e-15, None, ALU.add))
                    step(V.reciprocal(den, den))
                    step(V.tensor_tensor(n3, q, v, ALU.mult))
                    step(V.tensor_tensor(n3, n3, ks[:, :].unsqueeze(2).to_broadcast([P, 16, 32]), ALU.mult))
                    V.tensor_tensor(num, num, den, ALU.mult).then_inc(s["out_ready"], 1)
                    this(dve, s["nn3"], t)
                    norm_factor(V, step, nn[:, 7:8], nn[:, 6:7], ATANH_MAX)
                    this(dve, s["made"], t)
                    V.scalar_tensor_tensor(col(FT, t, D), psF, nn[:, 7:8], brw, ALU.mult, ALU.add).then_inc(s["kept"], 1)
                    step.end()

    F3 = FT.rearrange("p (t n) -> p t n", t=NT)
    sq = g.b3
    with phase(nc, g, "squared", "summed", "rooted", "tanhed", "step") as (block, s):
        @block.scalar
        def _(act):
            nc.scalar.activation(sq, FT, ACT.Square).then_inc(s["squared"], 1)
            act.wait_ge(s["summed"], 1)
            nc.scalar.activation(nq, n2, ACT.Sqrt).then_inc(s["rooted"], 1)
            act.wait_ge(s["rooted"], 1)
            nc.scalar.activation(za, nq, ACT.Tanh).then_inc(s["tanhed"], 1)

        @block.vector
        def _(dve):
            V = nc.vector
            step = Steps(dve, s["step"])
            dve.wait_ge(s["squared"], 1)
            V.tensor_reduce(n2, sq.rearrange("p (t n) -> p t n", t=NT), AX, ALU.add).then_inc(s["summed"], 1)
            dve.wait_ge(s["tanhed"], 1)
            step(V.tensor_scalar(za, za, MAXNORM, None, ALU.min))
            step(V.tensor_scalar(nq, nq, 1e-15, None, ALU.max))
            step(V.reciprocal(zb, nq))
            step(V.tensor_tensor(za, za, zb, ALU.mult))
            step(V.tensor_tensor(F3, F3, za.unsqueeze(2).to_broadcast([P, NT, D]), ALU.mult))
            step(V.tensor_tensor(x, x, FT, ALU.add))



def vector_phase(nc, g, program):
    with phase(nc, g, "step") as (block, s):
        @block.vector
        def _(dve):
            program(nc.vector, Steps(dve, s["step"]))


def graph_attention_layer(nc, g, d, Wq, Wk, Wv, Wo, gam, bet, first):
    ps = [g.ps[0:P, 4, 0:D], g.ps[0:P, 5, 0:D], g.ps[0:P, 6, 0:D]]
    wts = [g.w1[:, 0:512], g.w1[:, 512:1024], g.w1[:, 1024:1536]]

    def split(V, t, steps):
        V.tensor_copy(col(g.b2, t, D), ps[0])
        for m in (1, 2):
            ins = V.tensor_copy(g.o[:, m * D:(m + 1) * D], ps[m])
        return ins

    tile_pass(nc, g, g.h, 2, [(mm_weights(wts[m], D), ps[m]) for m in range(3)],
              [(w3(wts[m], 2, D), split_k(w, 2)) for m, w in enumerate((Wq, Wk, Wv))], split,
              tables=[(tb, g.o[:, m * D:(m + 1) * D]) for m, tb in ((1, d.k), (2, d.v))])
    edge_scores(nc, g, g.b2, d.k)
    segment_softmax(nc, g)
    edge_sums(nc, g, d.v, g.sums, True)

    S3 = g.sums.rearrange("p (t c) -> p t c", c=D + 9)
    Z3 = S3[:, :, D:D + 9]

    def normalise(V, step):
        if first:
            step(V.tensor_scalar(g.coef[:, 0:NT], Z3[:, :, 8], 0.0, None, ALU.is_gt))
            step(V.tensor_scalar(g.coef[:, NT:2 * NT], Z3[:, :, 8], 1.0, None, ALU.max))
        z = g.ht[0:P, 0:NT * HEADS]
        step(V.tensor_scalar(z.rearrange("p (t h) -> p t h", h=HEADS), Z3[:, :, 0:8], 1e-9, None, ALU.add))
        step(V.reciprocal(z, z))
        z3 = z.rearrange("p (t h) -> p t h", h=HEADS)
        for h in range(HEADS):
            A = S3[:, :, h * DK:(h + 1) * DK]
            V.tensor_tensor(A, A, z3[:, :, h:h + 1].to_broadcast([P, NT, DK]), ALU.mult)

    vector_phase(nc, g, normalise)
    if first:
        with phase(nc, g, "rooted", "step") as (block, s):
            @block.scalar
            def _(act):
                nc.scalar.activation(g.coef[:, 2 * NT:3 * NT], g.coef[:, NT:2 * NT], ACT.Sqrt).then_inc(s["rooted"], 1)

            @block.vector
            def _(dve):
                step = Steps(dve, s["step"])
                dve.wait_ge(s["rooted"], 1)
                step(nc.vector.reciprocal(g.dinv[:, :], g.coef[:, 2 * NT:3 * NT]))
                step(nc.vector.tensor_tensor(g.dinv[:, :], g.dinv[:, :], g.coef[:, 0:NT], ALU.mult))
    down = g.ps[0:P, 4, 0:D]
    tile_pass(nc, g, g.sums, 2, [(mm_weights(g.w2, D), down)], [(w3(g.w2, 2, D), split_k(Wo, 2))],
              add_into(down, g.h, g.unit), row=D + 9)
    layernorm(nc, g, g.h, g.h, g.b2, gam, bet)


def routed_ffn(nc, g, a, d):
    xn, x = g.h, g.x
    layernorm(nc, g, x, xn, g.b2)
    K1 = max(1, int(0.5 * N))
    K1 = K1 - 1 if K1 > 1 else 1
    wr = g.w1[0:P, 0:D]
    br = g.vec[0:P, 0:1]
    wt, rank = g.stat[:, 0:NT], g.stat[:, NT:2 * NT]
    later = g.stat[:, 2 * NT:3 * NT]
    part = g.stat[:, 3 * NT:4 * NT]
    wrow = g.view(19200, N, P)
    junk = g.view(22400, N, P)
    tri = g.view(25600, P, P)
    tri2 = g.view(25800, P, P)
    X3 = lambda b: b.rearrange("p (t n) -> p t n", t=NT)
    with phase(nc, g, "loaded", "step", "turned", "rowed", "stored", "back", "tri") as (block, s):
        @block.sync
        def _(sp):
            sp.dma_start(wr, a["L0_ffn_wr"].rearrange("n o -> (n o)").partition_broadcast(P)).then_inc(s["loaded"], 16)
            sp.dma_start(br, a["L0_ffn_br"].partition_broadcast(P)).then_inc(s["loaded"], 16)
            sp.wait_ge(s["rowed"], 1)
            sp.dma_start(d.rowa.rearrange("(t p) -> t p", p=P), g.o[0:NT, 0:P]).then_inc(s["stored"], 16)
            sp.wait_ge(s["stored"], 16)
            sp.dma_start(wrow, d.rowa.partition_broadcast(P)).then_inc(s["back"], 16)

        @block.gpsimd
        def _(pool):
            nc.gpsimd.memset(tri, 1.0).then_inc(s["tri"], 1)
            pool.wait_ge(s["tri"], 1)
            nc.gpsimd.affine_select(out=tri, in_=tri, compare_op=ALU.is_gt, fill=0.0, base=0, pattern=[[-1, P]],
                                    channel_multiplier=1).then_inc(s["tri"], 1)

        @block.tensor
        def _(pe):
            pe.wait_ge(s["turned"], 1)
            nc.tensor.transpose(g.ps[0:NT, 0, 0:P], wt, g.ident[0:P, 0:P]).then_inc(s["turned"], 1)

        @block.vector
        def _(dve):
            V = nc.vector
            step = Steps(dve, s["step"])
            dve.wait_ge(s["loaded"], 32)
            step(V.tensor_tensor(X3(g.b2), X3(xn), wr.unsqueeze(1).to_broadcast([P, NT, D]), ALU.mult))
            step(V.tensor_reduce(wt, X3(g.b2), AX, ALU.add))
            V.tensor_scalar(wt, wt, br, None, ALU.add).then_inc(s["turned"], 1)
            dve.wait_ge(s["turned"], 2)
            V.tensor_copy(g.o[0:NT, 0:P], g.ps[0:NT, 0, 0:P]).then_inc(s["rowed"], 1)
            dve.wait_ge(s["back"], 16)
            dve.wait_ge(s["tri"], 2)
            step(V.memset(g.stat[:, NT:2 * NT], 0.0))
            step(V.memset(later, 0.0))
            for t in range(NT):
                me = wt[:, t:t + 1]
                a0, a1 = t * P, (t + 1) * P
                if t:
                    step(V.tensor_scalar(junk[:, 0:a0], wrow[:, 0:a0], me, 0.0, ALU.is_ge, ALU.add, accum_out=rank[:, t:t + 1]))
                step(V.tensor_scalar(junk[:, a0:N], wrow[:, a0:N], me, 0.0, ALU.is_gt, ALU.add, accum_out=later[:, t:t + 1]))
                step(V.scalar_tensor_tensor(tri2, wrow[:, a0:a1], me, tri, ALU.is_equal, ALU.mult))
                step(V.tensor_reduce(part[:, t:t + 1], tri2, AX, ALU.add))
            step(V.tensor_tensor(rank, rank, later, ALU.add))
            step(V.tensor_tensor(rank, rank, part, ALU.add))
            step(V.scalar_tensor_tensor(g.coef[:, 0:NT], rank, float(K1), wt, ALU.is_lt, ALU.mult))
            step(V.tensor_tensor(x, x, xn, ALU.add))
    mlp(nc, g, xn, a["L0_ffn_w1"], a["L0_ffn_b1"], a["L0_ffn_w2"], a["L0_ffn_b2"], ACT.Gelu_apprx_tanh, x, g.coef[:, 0:NT],
        side=fill_penalties(nc, g, d))


def graph_convolution(nc, g, a, d):
    layernorm(nc, g, g.x, g.h, g.b2)
    ps = g.ps[0:P, 4, 0:D]

    def to_table(V, t, steps):
        return V.tensor_scalar(g.o[:, 0:D], ps, col(g.dinv, t), None, ALU.mult)

    tile_pass(nc, g, g.h, 2, [(mm_weights(g.w1, D), ps)], [(w3(g.w1, 2, D), split_k(a["L1_gnn_W"], 2))], to_table,
              tables=[(d.q, g.o[:, 0:D])])
    edge_sums(nc, g, d.q, g.b2, False)

    def add(V, step):
        A3 = g.b2.rearrange("p (t n) -> p t n", t=NT)
        step(V.tensor_tensor(A3, A3, g.dinv[:, :].unsqueeze(2).to_broadcast([P, NT, D]), ALU.mult))
        step(V.tensor_tensor(g.x, g.x, g.b2, ALU.add))
    vector_phase(nc, g, add)


def linear_attention(nc, g, a, d, l):
    y, xh = g.h, g.b5
    q, k, v = g.b2, g.b3, g.b4
    layernorm(nc, g, y, xh, q)
    ps = [g.ps[0:P, 4, 0:D], g.ps[0:P, 5, 0:D], g.ps[0:P, 6, 0:D]]
    wts = [g.w1[:, 0:512], g.w1[:, 512:1024], g.w1[:, 1024:1536]]
    aff = (g.vec[:, 32:34], g.vec[:, 34:36])

    def keep(V, t, steps):
        for m, b in enumerate((q, k, v)):
            ins = V.tensor_copy(col(b, t, D), ps[m])
        return ins

    tile_pass(nc, g, xh, 2, [(mm_weights(wts[m], D), ps[m]) for m in range(3)],
              [(w3(wts[m], 2, D), split_k(w[l], 2)) for m, w in enumerate((a["L1_mix_Wq"], a["L1_mix_Wk"], a["L1_mix_Wv"]))]
              + [(aff[0], a["L1_mix_ln1_g"][l].rearrange("(k p) -> p k", p=128)),
                 (aff[1], a["L1_mix_ln1_b"][l].rearrange("(k p) -> p k", p=128))], keep, affine=aff,
              side=lift_penalties(nc, g, d, 128 * l, 48))

    S = float(DK) ** -0.25
    Q4 = q.rearrange("p (n d) -> p n d", d=DK)
    K3 = k.rearrange("p (t n) -> p t n", t=NT)
    KT = k.rearrange("p (t n) -> p n t", t=NT)
    qm = g.ht[0:P, 0:NT * HEADS]
    kcol = g.o[:, 0:D]
    kmT = g.vec[:, 0:2]
    bd = g.h1[:, 0:256].rearrange("p (k n) -> p k n", k=2)
    with phase(nc, g, "step", "kcol", "kturn", "kmax", "krow", "ksub", "qsub", "kexp", "qexp") as (block, s):
        @block.vector
        def _(dve):
            V = nc.vector
            step = Steps(dve, s["step"])
            V.tensor_reduce(kcol, KT, AX, ALU.max).then_inc(s["kcol"], 1)
            step(V.tensor_reduce(qm, Q4, AX, ALU.max))
            V.tensor_tensor(Q4, Q4, qm.unsqueeze(2).to_broadcast([P, NT * HEADS, DK]), ALU.subtract).then_inc(s["qsub"], 1)
            dve.wait_ge(s["kturn"], 1)
            step(V.tensor_reduce(kmT, g.ps[:, 0, 0:2 * P].rearrange("p (k r) -> p k r", r=P), AX, ALU.max))
            for c in range(2):
                ins = V.tensor_scalar(bd[:, c, :], g.ident[:, :], kmT[:, c:c + 1], None, ALU.mult)
            ins.then_inc(s["kmax"], 1)
            dve.wait_ge(s["krow"], 1)
            step(V.tensor_copy(kcol, g.ps[0:P, 1, 0:D]))
            V.tensor_tensor(K3, K3, kcol.unsqueeze(1).to_broadcast([P, NT, D]), ALU.subtract).then_inc(s["ksub"], 1)
            dve.wait_ge(s["qexp"], 1)
            step(V.tensor_reduce(qm, Q4, AX, ALU.add))
            step(V.reciprocal(qm, qm))
            step(V.tensor_tensor(Q4, Q4, qm.unsqueeze(2).to_broadcast([P, NT * HEADS, DK]), ALU.mult))

        @block.tensor
        def _(pe):
            pe.wait_ge(s["kcol"], 1)
            for c in range(2):
                ins = nc.tensor.transpose(g.ps[:, 0, c * P:(c + 1) * P], kcol[:, c * 128:(c + 1) * 128], g.ident[0:P, 0:P])
            ins.then_inc(s["kturn"], 1)
            pe.wait_ge(s["kmax"], 1)
            for c in range(2):
                ins = nc.tensor.matmul(g.ps[0:P, 1, c * 128:(c + 1) * 128], g.ones[:, 0:P], bd[:, c, :], start=True, stop=True)
            ins.then_inc(s["krow"], 1)

        @block.scalar
        def _(act):
            act.wait_ge(s["qsub"], 1)
            nc.scalar.activation(q, q, ACT.Exp, scale=S).then_inc(s["qexp"], 1)
            act.wait_ge(s["ksub"], 1)
            nc.scalar.activation(k, k, ACT.Exp, scale=S).then_inc(s["kexp"], 1)
            act.wait_ge(s["kexp"], 1)

    ctxT = g.h1[:, 0:256].rearrange("p (c n) -> p c n", c=2)
    rk = g.h1[:, 256:512].rearrange("p (c n) -> p c n", c=2)
    wctx = g.w1[:, 0:512]
    hd = g.h1[:, 512:640]
    TS = 5
    vst = g.w1[0:P, 0:TS * D]
    with phase(nc, g, "masked", "zeroed", "made", "step", "ready", "loaded", "fused", "staged", "read") as (block, s):
        @block.sync
        def _(sp):
            sp.dma_start(w3(g.w2, 2, D), split_k(a["L1_mix_Wo"][l], 2)).then_inc(s["loaded"], 16)

        @block.gpsimd
        def _(pool):
            nc.gpsimd.memset(hd, 0.0).then_inc(s["masked"], 1)
            pool.wait_ge(s["masked"], 1)
            for b in range(4):
                nc.gpsimd.memset(hd[32 * b:32 * b + 32, 32 * b:32 * b + 32], 1.0).then_inc(s["masked"], 1)

        @block.scalar
        def _(act):
            act.sem_inc(s["staged"], 1)
            with act.Fori(0, NT // TS) as t:
                before(act, s["read"], t)
                nc.scalar.copy(vst, col(v, t, TS * D)).then_inc(s["staged"], 1)

        @block.tensor
        def _(pe):
            pe.sem_inc(s["read"], 1)
            pe.wait_ge(s["zeroed"], 1)
            z = g.o[0:1, 0:128]
            for c in range(2):
                nc.tensor.matmul(g.ps[:, 2 + c, 0:128], z, z, start=True, stop=False, skip_group_check=True)
                nc.tensor.matmul(g.ps[:, 4 + c, 0:128], z, z, start=True, stop=False, skip_group_check=True)
            with pe.Fori(0, NT // TS) as t:
                this(pe, s["staged"], t)
                for n in range(TS):
                    for c in range(2):
                        kt = k[:, bass.ds(t * (TS * D) + n * D + c * 128, 128)]
                        nc.tensor.matmul(g.ps[:, 2 + c, 0:128], vst[:, n * D + c * 128:n * D + (c + 1) * 128], kt,
                                         start=False, stop=False, skip_group_check=True)
                        ins = nc.tensor.matmul(g.ps[:, 4 + c, 0:128], g.ones[0:P, :], kt, start=False, stop=False,
                                               skip_group_check=True)
                ins.then_inc(s["read"], 1)
            for c in range(2):
                nc.tensor.matmul(g.ps[:, 2 + c, 0:128], z, z, start=False, stop=True, skip_group_check=True)
                ins = nc.tensor.matmul(g.ps[:, 4 + c, 0:128], z, z, start=False, stop=True, skip_group_check=True)
            ins.then_inc(s["made"], 1)
            pe.wait_ge(s["ready"], 1)
            pe.wait_ge(s["loaded"], 16)
            for c in range(2):
                ins = nc.tensor.matmul(g.ps[:, 6 + c, 0:D], ctxT[:, c, :], g.w2[:, c * D:(c + 1) * D], start=True, stop=True)
            ins.then_inc(s["fused"], 1)

        @block.vector
        def _(dve):
            V = nc.vector
            step = Steps(dve, s["step"])
            V.memset(g.o[0:1, 0:128], 0.0).then_inc(s["zeroed"], 1)
            dve.wait_ge(s["masked"], 5)
            dve.wait_ge(s["made"], 1)
            step(V.reciprocal(rk, g.ps[:, 4:6, 0:128]))
            for c in range(2):
                step(V.tensor_tensor(rk[:, c, :], rk[:, c, :], hd, ALU.mult))
            V.tensor_tensor(ctxT, g.ps[:, 2:4, 0:128], rk, ALU.mult).then_inc(s["ready"], 1)
            dve.wait_ge(s["fused"], 1)
            step(V.tensor_copy(wctx.rearrange("p (c n) -> p c n", c=2), g.ps[:, 6:8, 0:D]))

    down = g.ps[0:P, 4, 0:D]
    tile_pass(nc, g, q, 2, [(mm_weights(wctx, D), down)],
              [(g.brow[:, :], a["L1_mix_bo"][l].rearrange("(a n) -> a n", a=1))], add_into(down, y, g.unit), bias=True,
              side=lift_penalties(nc, g, d, 128 * l + 48, 16))


def transformer(nc, g, a, d):
    y = g.h
    for l in range(4):
        linear_attention(nc, g, a, d, l)
        layernorm(nc, g, y, g.b5, g.b2)
        aff = (g.vec[:, 32:34], g.vec[:, 34:36])
        mlp(nc, g, g.b5, a["L1_mix_W1"][l], a["L1_mix_b1"][l], a["L1_mix_W2"][l], a["L1_mix_b2"][l], ACT.Gelu, y, g.unit, affine=aff,
            side=lift_penalties(nc, g, d, 128 * l + 64, 64),
            extra=[(aff[0], a["L1_mix_ln2_g"][l].rearrange("(k p) -> p k", p=128)),
                   (aff[1], a["L1_mix_ln2_b"][l].rearrange("(k p) -> p k", p=128))])

    def add(V, step):
        step(V.tensor_tensor(g.x, g.x, y, ALU.add))
    vector_phase(nc, g, add)


def experts(nc, g, a, d):
    xn, x = g.h, g.x
    layernorm(nc, g, x, xn, g.b2)
    H, EX = 4, 4
    small = g.view(12800, 6400, P)
    hg = small[:, 0:NT * 16]
    tab = small[:, 400:400 + NT * 20]
    dtab = small[:, 900:900 + NT * 8]
    ps = g.ps[0:P, 4, 0:16]

    def keep(V, t, steps):
        return V.tensor_copy(col(hg, t, 16), ps)

    tile_pass(nc, g, xn, 2, [(lambda k: g.w1[:, k * 16:(k + 1) * 16], ps)],
              [(w3(g.w1, 2, 16), split_k(a["L1_ffn_W_gat"], 2))], keep)

    T3 = tab.rearrange("p (t c) -> p t c", c=20)
    D3 = dtab.rearrange("p (t c) -> p t c", c=8)
    H4 = hg.rearrange("p (n e) -> p n e", e=EX)
    tmp = small[:, 1100:1500]
    aS, aD = small[:, 1500:1516], small[:, 1516:1532]
    sc = small[:, 1600:1700]
    arow = g.view(19200, 4 * N, P)
    pen = [g.view(31700 + 3200 * b, N, P) for b in range(2)]
    with phase(nc, g, "loaded", "step", "table", "stored") as (block, s):
        @block.sync
        def _(sp):
            sp.dma_start(aS, a["L1_ffn_att_src"].rearrange("h e -> (h e)").partition_broadcast(P)).then_inc(s["loaded"], 16)
            sp.dma_start(aD, a["L1_ffn_att_dst"].rearrange("h e -> (h e)").partition_broadcast(P)).then_inc(s["loaded"], 16)
            sp.wait_ge(s["table"], 1)
            sp.dma_start(d.tab.rearrange("(t p) c -> p t c", p=P), T3).then_inc(s["stored"], 16)
            for h in range(H):
                sp.dma_start(d.arow[h * N:(h + 1) * N].rearrange("(t p) -> p t", p=P), T3[:, :, 16 + h],
                             allow_slow_non_contiguous=True).then_inc(s["stored"], 16)
            sp.wait_ge(s["stored"], 16 * 5)

        @block.vector
        def _(dve):
            V = nc.vector
            step = Steps(dve, s["step"])
            dve.wait_ge(s["loaded"], 32)
            t4 = tmp.rearrange("p (t c) -> p t c", c=16)
            h3 = hg.rearrange("p (t c) -> p t c", c=16)
            for n, w in enumerate((aD, aS)):
                step(V.tensor_tensor(t4, h3, w.unsqueeze(1).to_broadcast([P, NT, 16]), ALU.mult))
                step(V.tensor_reduce(sc, tmp.rearrange("p (n e) -> p n e", e=EX), AX, ALU.add))
                out = (D3[:, :, 0:4], T3[:, :, 16:20])[n]
                step(V.tensor_copy(out, sc.rearrange("p (t h) -> p t h", h=H)))
            V.tensor_copy(T3[:, :, 0:16], h3).then_inc(s["table"], 1)

    EC = E2 // 128
    sI = g.view(31700, EC).bitcast(I32)
    dI = g.view(32300, EC).bitcast(I32)
    sF, dF = g.view(32900, EC), g.view(33500, EC)
    srcI, dstI = g.srcv_e, g.dstv_e
    ei = a["L1_ffn_edge_index"]
    with phase(nc, g, "loaded", "step") as (block, s):
        @block.sync
        def _(sp):
            sp.dma_start(sI, ei[0].rearrange("(p c) -> p c", p=128)).then_inc(s["loaded"], 16)
            sp.dma_start(dI, ei[1].rearrange("(p c) -> p c", p=128)).then_inc(s["loaded"], 16)

        @block.vector
        def _(dve):
            V = nc.vector
            step = Steps(dve, s["step"])
            dve.wait_ge(s["loaded"], 32)
            step(V.tensor_copy(sF, sI))
            step(V.tensor_copy(dF, dI))
            step(V.tensor_scalar(sF, sF, float(N - 1), None, ALU.min))
            step(V.tensor_copy(srcI, sF))
            step(V.tensor_scalar(dF, dF, float(N - 1), None, ALU.min))
            step(V.tensor_copy(dstI, dF))
            step(V.tensor_scalar(g.dlo, dI, 127, None, ALU.bitwise_and))
            step(V.tensor_scalar(g.dhi, dI, 7, None, ALU.logical_shift_right))

    mx = small[:, 1700:1700 + NT * H]
    sums = g.ps[0:P, :, :].rearrange("p b c -> p (b c)")[:, 0:N]
    with phase(nc, g, "loaded", "pen0", "pen1", "used0", "used1") as (block, s):
        lp, us = [s["pen0"], s["pen1"]], [s["used0"], s["used1"]]

        @block.sync
        def _(sp):
            for h in range(H):
                sp.dma_start(arow[:, h * N:(h + 1) * N], d.arow[h * N:(h + 1) * N].partition_broadcast(P)).then_inc(s["loaded"], 16)
            for t in range(NT):
                if t >= 2:
                    sp.wait_ge(us[t % 2], H * (t // 2))
                sp.dma_start(pen[t % 2], d.pen[t * P * N:(t + 1) * P * N].rearrange("(p n) -> p n", p=P)).then_inc(lp[t % 2], 16)

        @block.vector
        def _(dve):
            dve.wait_ge(s["loaded"], 64)
            for t in range(NT):
                dve.wait_ge(lp[t % 2], 16 * (t // 2 + 1))
                for h in range(H):
                    if t or h:
                        before_ = (t, h - 1) if h else (t - 1, H - 1)
                        dve.wait_ge(us[before_[0] % 2], H * (before_[0] // 2) + before_[1] + 1)
                    nc.vector.tensor_tensor_reduce(sums, pen[t % 2],
                                                   arow[:, h * N:(h + 1) * N], 1.0, -BIG, ALU.add, ALU.max,
                                                   mx[:, t * H + h:t * H + h + 1]).then_inc(us[t % 2], 1)

    lk = small[:, 1800:1900]
    wself = small[:, 1900:2000]
    agg = small[:, 2100:2600]
    A3 = agg.rearrange("p (t c) -> p t c", c=20)
    with phase(nc, g, "step", "shifted", "expd", "table", "stored") as (block, s):
        @block.vector
        def _(dve):
            V = nc.vector
            step = Steps(dve, s["step"])
            m3 = mx.rearrange("p (t h) -> p t h", h=H)
            l3 = lk.rearrange("p (t h) -> p t h", h=H)
            step(V.tensor_tensor(m3, m3, T3[:, :, 16:20], ALU.max))
            step(V.tensor_tensor(m3, m3, D3[:, :, 0:4], ALU.add))
            step(V.tensor_copy(l3, m3))
            V.scalar_tensor_tensor(D3[:, :, 4:8], l3, 0.2, m3, ALU.mult, ALU.max).then_inc(s["table"], 1)
            dve.wait_ge(s["table"], 1)
            step(V.tensor_tensor(m3, T3[:, :, 16:20], D3[:, :, 0:4], ALU.add))
            step(V.tensor_copy(l3, m3))
            step(V.scalar_tensor_tensor(l3, l3, 0.2, m3, ALU.mult, ALU.max))
            V.tensor_tensor(l3, l3, D3[:, :, 4:8], ALU.subtract).then_inc(s["shifted"], 1)

        @block.scalar
        def _(act):
            act.wait_ge(s["shifted"], 1)
            nc.scalar.activation(wself, lk, ACT.Exp).then_inc(s["expd"], 1)
            act.wait_ge(s["expd"], 1)

        @block.sync
        def _(sp):
            sp.wait_ge(s["table"], 1)
            sp.dma_start(d.dtab.rearrange("(t p) c -> p t c", p=P), D3).then_inc(s["stored"], 16)
            sp.wait_ge(s["stored"], 16)

    GB, NB = 8, 25

    def buffers(u):
        v = lambda off, n: g.view(19200 + 6000 * u + off, n)
        b = Names()
        b.rows = v(0, GB * 20).rearrange("p (j c) -> p j c", c=20)
        b.drows = v(160, GB * 8).rearrange("p (j c) -> p j c", c=8)
        b.ee = v(224, GB * 4).rearrange("p (j c) -> p j c", c=4)
        b.e2 = v(256, GB * 4).rearrange("p (j c) -> p j c", c=4)
        b.pay = v(288, GB * 20).rearrange("p (j c) -> p j c", c=20)
        b.ohh = v(448, GB * NB).rearrange("p (j t) -> p j t", t=NB)
        b.ohl = [v(656 + 128 * j, 128) for j in range(GB)]
        b.big = [v(1680 + 500 * j, 500) for j in range(GB)]
        b.ix = g.ht[:, 2 * GB * u:2 * GB * (u + 1)].bitcast(I32)
        return b

    bufs = [buffers(0), buffers(1)]
    loF, hiF = g.loF, g.hiF
    total = g.ps[:, 3, 0:NB * 20]
    ALLD = g.view(31700, NB * 20)
    sets = [f"{n}{u}" for n in ("gathered", "raw", "expd", "made", "summed", "step") for u in range(2)]
    names = ["zeroed", "indexed", "final", "copied", "stored", "back", "red"] + sets
    with phase(nc, g, *names) as (block, s):
        gathered, raw, expd, made, summed, stepped = ([s[f"{n}{u}"] for u in range(2)]
                                                      for n in ("gathered", "raw", "expd", "made", "summed", "step"))

        @block.gpsimd
        def _(pool):
            with pool.Fori(0, EC // (2 * GB)) as i:
                for u, b in enumerate(bufs):
                    before(pool, made[u], i)
                    c = i * (2 * GB) + u * GB
                    nc.gpsimd.tensor_copy(b.ix[:, 0:GB], srcI[:, bass.ds(c, GB)]).then_inc(s["indexed"], 1)
                    nc.gpsimd.tensor_copy(b.ix[:, GB:2 * GB], dstI[:, bass.ds(c, GB)]).then_inc(s["indexed"], 1)
                    hold(pool, s["indexed"], i * 4 + 2 * (u + 1))
                    for j in range(GB):
                        nc.gpsimd.indirect_dma_start(b.rows[:, j, :], None, d.tab,
                                                     bass.IndirectOffsetOnAxis(b.ix[:, j:j + 1], 0)).then_inc(gathered[u], 16)
                        nc.gpsimd.indirect_dma_start(b.drows[:, j, :], None, d.dtab,
                                                     bass.IndirectOffsetOnAxis(b.ix[:, GB + j:GB + j + 1], 0)).then_inc(gathered[u], 16)

        @block.scalar
        def _(act):
            for q in expd:
                act.sem_inc(q, 1)
            with act.Fori(0, EC // (2 * GB)) as i:
                for u, b in enumerate(bufs):
                    this(act, raw[u], i)
                    nc.scalar.activation(b.pay[:, :, 16:20], b.ee, ACT.Exp).then_inc(expd[u], 1)

        @block.vector
        def _(dve):
            V = nc.vector
            V.memset(g.o[0:1, 0:500], 0.0).then_inc(s["zeroed"], 1)
            V.tensor_copy(loF, g.dlo)
            V.tensor_copy(hiF, g.dhi).then_inc(s["zeroed"], 1)
            dve.wait_ge(s["zeroed"], 2)
            for q in raw + made:
                dve.sem_inc(q, 1)
            with dve.Fori(0, EC // (2 * GB)) as i:
                for u, b in enumerate(bufs):
                    step = Steps(dve, stepped[u], i, 4)
                    c = i * (2 * GB) + u * GB
                    landed(dve, gathered[u], i, 32 * GB)
                    step(V.tensor_tensor(b.ee, b.rows[:, :, 16:20], b.drows[:, :, 0:4], ALU.add))
                    step(V.scalar_tensor_tensor(b.e2, b.ee, 0.2, b.ee, ALU.mult, ALU.max))
                    before(dve, summed[u], i)
                    V.tensor_tensor(b.ee, b.e2, b.drows[:, :, 4:8], ALU.subtract).then_inc(raw[u], 1)
                    for j in range(GB):
                        V.tensor_scalar(b.ohl[j], g.iota[:, :], loF[:, bass.ds(c + j, 1)], None, ALU.is_equal)
                    step(V.tensor_tensor(b.ohh, g.iota[:, 0:NB].unsqueeze(1).to_broadcast([128, GB, NB]),
                                         hiF[:, bass.ds(c, GB)].unsqueeze(2).to_broadcast([128, GB, NB]), ALU.is_equal))
                    this(dve, expd[u], i)
                    r4 = b.rows[:, :, 0:16].rearrange("p j (h e) -> p j h e", h=H)
                    p4 = b.pay[:, :, 0:16].rearrange("p j (h e) -> p j h e", h=H)
                    for j in range(GB):
                        ins = V.tensor_tensor(p4[:, j], r4[:, j], b.pay[:, j, 16:20].unsqueeze(2).to_broadcast([128, H, EX]),
                                              ALU.mult)
                    step(ins)
                    for j in range(GB):
                        ins = V.tensor_tensor(b.big[j].rearrange("p (t c) -> p t c", c=20),
                                              b.ohh[:, j, :].unsqueeze(2).to_broadcast([128, NB, 20]),
                                              b.pay[:, j, :].unsqueeze(1).to_broadcast([128, NB, 20]), ALU.mult)
                    ins.then_inc(made[u], 1)
                    step.end()
            dve.wait_ge(s["final"], 1)
            V.tensor_copy(ALLD, total).then_inc(s["copied"], 1)
            dve.wait_ge(s["back"], 16)
            step2 = Steps(dve, s["red"])
            own = g.view(32300, NT * 20, P).rearrange("p (t c) -> p t c", c=20)
            for h in range(H):
                o = own[:, :, 4 * h:4 * h + 4]
                w = wself.rearrange("p (t h) -> p t h", h=H)[:, :, h:h + 1].to_broadcast([P, NT, EX])
                step2(V.tensor_tensor(o, T3[:, :, 4 * h:4 * h + 4], w, ALU.mult))
            step2(V.tensor_copy(own[:, :, 16:20], wself.rearrange("p (t h) -> p t h", h=H)))
            step2(V.tensor_tensor(A3, A3, own, ALU.add))

        @block.tensor
        def _(pe):
            for q in summed:
                pe.sem_inc(q, 1)
            pe.wait_ge(s["zeroed"], 1)
            nc.tensor.matmul(total, g.o[0:1, 0:128], g.o[0:1, 0:500], start=True, stop=False, skip_group_check=True)
            with pe.Fori(0, EC // (2 * GB)) as i:
                for u, b in enumerate(bufs):
                    this(pe, made[u], i)
                    for j in range(GB):
                        ins = nc.tensor.matmul(total, b.ohl[j], b.big[j], start=False, stop=False, skip_group_check=True)
                    ins.then_inc(summed[u], 1)
            nc.tensor.matmul(total, g.o[0:1, 0:128], g.o[0:1, 0:500], start=False, stop=True,
                             skip_group_check=True).then_inc(s["final"], 1)

        @block.sync
        def _(sp):
            sp.wait_ge(s["copied"], 1)
            sp.dma_start(d.agg.rearrange("(t p) c -> p t c", p=128), ALLD.rearrange("p (t c) -> p t c", c=20)).then_inc(s["stored"], 16)
            sp.wait_ge(s["stored"], 16)
            sp.dma_start(A3, d.agg[0:N, :].rearrange("(t p) c -> p t c", p=P)).then_inc(s["back"], 16)

    rz = small[:, 2600:2700]
    s16 = small[:, 2700:3100]
    sq = small[:, 3100:3500]
    m1, v1, r1, q1 = (small[:, 3500 + 25 * n:3525 + 25 * n] for n in range(4))
    par = small[:, 3600:3648]
    scr = small[:, 3700:3800]
    cmpb = small[:, 3800:4200]
    rk4 = small[:, 4200:4300]
    ex = small[:, 4300:4400]
    gate = small[:, 4400:4500]
    lower = small[:, 4500:4516]
    with phase(nc, g, "loaded", "lowset", "step", "var", "std", "shifted", "expd") as (block, s):
        @block.sync
        def _(sp):
            for n, b in enumerate((a["L1_ffn_b_gat"], a["L1_ffn_ln_gamma"], a["L1_ffn_ln_beta"])):
                sp.dma_start(par[:, 16 * n:16 * n + 16], b.partition_broadcast(P)).then_inc(s["loaded"], 16)

        @block.gpsimd
        def _(pool):
            nc.gpsimd.memset(lower, 0.0).then_inc(s["lowset"], 1)
            pool.wait_ge(s["lowset"], 1)
            for n in range(1, EX):
                nc.gpsimd.memset(lower[:, n * EX:n * EX + n], 1.0).then_inc(s["lowset"], 1)

        @block.scalar
        def _(act):
            act.wait_ge(s["var"], 1)
            nc.scalar.activation(q1, v1, ACT.Sqrt, bias=g.eps[0:P, :], scale=1.0 / 16).then_inc(s["std"], 1)
            act.wait_ge(s["shifted"], 1)
            nc.scalar.activation(ex, scr, ACT.Exp).then_inc(s["expd"], 1)

        @block.vector
        def _(dve):
            V = nc.vector
            step = Steps(dve, s["step"])
            step(V.tensor_scalar(rz.rearrange("p (t h) -> p t h", h=H), A3[:, :, 16:20], 1e-16, None, ALU.add))
            step(V.reciprocal(rz, rz))
            S3 = s16.rearrange("p (t c) -> p t c", c=16)
            Q3 = sq.rearrange("p (t c) -> p t c", c=16)
            w16 = [P, NT, 16]
            step(V.tensor_copy(S3, A3[:, :, 0:16]))
            s4 = s16.rearrange("p (n e) -> p n e", e=EX)
            step(V.tensor_tensor(s4, s4, rz.unsqueeze(2).to_broadcast([P, NT * H, EX]), ALU.mult))
            dve.wait_ge(s["loaded"], 48)
            step(V.tensor_tensor(S3, S3, par[:, 0:16].unsqueeze(1).to_broadcast(w16), ALU.add))
            step(V.tensor_reduce(m1, S3, AX, ALU.add))
            step(V.tensor_scalar(m1, m1, 1.0 / 16, None, ALU.mult))
            step(V.tensor_tensor(S3, S3, m1.unsqueeze(2).to_broadcast(w16), ALU.subtract))
            step(V.tensor_tensor(sq, s16, s16, ALU.mult))
            V.tensor_reduce(v1, Q3, AX, ALU.add).then_inc(s["var"], 1)
            dve.wait_ge(s["std"], 1)
            step(V.reciprocal(r1, q1))
            step(V.tensor_tensor(S3, S3, r1.unsqueeze(2).to_broadcast(w16), ALU.mult))
            step(V.tensor_tensor(S3, S3, par[:, 16:32].unsqueeze(1).to_broadcast(w16), ALU.mult))
            step(V.tensor_tensor(S3, S3, par[:, 32:48].unsqueeze(1).to_broadcast(w16), ALU.add))
            sc3 = scr.rearrange("p (t e) -> p t e", e=EX)
            step(V.tensor_tensor(sc3, S3[:, :, 0:4], S3[:, :, 4:8], ALU.add))
            step(V.tensor_tensor(sc3, sc3, S3[:, :, 8:12], ALU.add))
            step(V.tensor_tensor(sc3, sc3, S3[:, :, 12:16], ALU.add))
            step(V.tensor_scalar(scr, scr, 0.25, None, ALU.mult))
            dve.wait_ge(s["lowset"], EX)
            k3 = rk4.rearrange("p (t e) -> p t e", e=EX)
            c3 = cmpb.rearrange("p (t e) -> p t e", e=16)
            for i in range(EX):
                me = sc3[:, :, i:i + 1].to_broadcast([P, NT, EX])
                gt, eq = c3[:, :, 0:4], c3[:, :, 4:8]
                step(V.tensor_tensor(gt, sc3, me, ALU.is_gt))
                step(V.tensor_tensor(eq, sc3, me, ALU.is_equal))
                step(V.tensor_tensor(eq, eq, lower[:, i * EX:(i + 1) * EX].unsqueeze(1).to_broadcast([P, NT, EX]), ALU.mult))
                step(V.tensor_tensor(gt, gt, eq, ALU.add))
                step(V.tensor_reduce(k3[:, :, i:i + 1], gt, AX, ALU.add))
            step(V.tensor_reduce(m1, sc3, AX, ALU.max))
            V.tensor_tensor(sc3, sc3, m1.unsqueeze(2).to_broadcast([P, NT, EX]), ALU.subtract).then_inc(s["shifted"], 1)
            dve.wait_ge(s["expd"], 1)
            step(V.scalar_tensor_tensor(ex, rk4, 2.0, ex, ALU.is_lt, ALU.mult))
            e3 = ex.rearrange("p (t e) -> p t e", e=EX)
            step(V.tensor_reduce(m1, e3, AX, ALU.add))
            step(V.reciprocal(r1, m1))
            step(V.tensor_tensor(gate.rearrange("p (e t) -> p t e", e=EX), e3, r1.unsqueeze(2).to_broadcast([P, NT, EX]), ALU.mult))
    for e in range(EX):
        mlp(nc, g, xn, a["L1_ffn_W1"][e], a["L1_ffn_b1"][e], a["L1_ffn_W2"][e], a["L1_ffn_b2"][e], ACT.Gelu, x,
            gate[:, e * NT:(e + 1) * NT])


STOP = 99


def gps_program(nc, a, out):
    d = Names()

    def dram(name, shape, dt=F32):
        return nc.dram_tensor(name, shape, dt, kind="Internal").ap()

    d.key, d.w, d.keys = dram("key", [ET]), dram("w", [NV], I32), dram("keys", [NV * P + 16])
    d.q, d.k, d.v = dram("q_rows", [N, D]), dram("k_rows", [N, D]), dram("v_rows", [N, D])
    d.rowa, d.arow = dram("rowa", [N]), dram("arow", [4 * N])
    d.pen, d.tab, d.dtab, d.agg = dram("pen", [N * N]), dram("tab", [N, 20]), dram("dtab", [N, 8]), dram("agg", [25 * 128, 20])
    d.links = dram("links", [128, SEQ + 1])
    with ExitStack() as ctx:
        g = setup(nc, ctx)
        EC = E2 // 128
        g.loF, g.hiF = g.view(35300, EC), g.view(34700, EC)
        constants(nc, g)
        plan_visits(nc, g, a["src"], a["dst"], d)
        if STOP > 0:
            with phase(nc, g, "loaded") as (block, s):
                @block.sync
                def _(sp):
                    sp.dma_start(g.x.rearrange("p (t n) -> p t n", t=NT), a["x"].rearrange("(t p) n -> p t n", p=P)).then_inc(s["loaded"], 16)
                    sp.wait_ge(s["loaded"], 16)
            layernorm(nc, g, g.x, g.h, g.b2)
        if STOP == 1:
            return dump(nc, g, g.h, out)
        if STOP > 1:
            spill(nc, g, d.links, True)
            mix(nc, g, g.h, g.x, a["L0_mix_w_qkv"], a["L0_mix_bn_gamma"], a["L0_mix_bn_beta"], a["L0_mix_w_dw"], a["L0_mix_w_pw"],
                a["L0_mix_w_res"], a["L0_mix_b_res"])
            spill(nc, g, d.links, False)
        if STOP == 2:
            return dump(nc, g, g.x, out)
        for l in range(2):
            graph_attention_layer(nc, g, d, a["L0_gnn_Wq"][l], a["L0_gnn_Wk"][l], a["L0_gnn_Wv"][l], a["L0_gnn_Wo"][l],
                                  a["L0_gnn_ln_g"][l], a["L0_gnn_ln_b"][l], l == 0)
            if STOP == 3:
                return dump(nc, g, g.h, out)
        mlp(nc, g, g.h, a["L0_gnn_w1"], a["L0_gnn_b1"], a["L0_gnn_w2"], a["L0_gnn_b2"], ACT.Relu, g.x, g.unit)
        if STOP == 4:
            return dump(nc, g, g.x, out)
        routed_ffn(nc, g, a, d)
        if STOP == 5:
            return dump(nc, g, g.x, out)
        graph_convolution(nc, g, a, d)
        if STOP == 6:
            return dump(nc, g, g.x, out)
        penalty_indices(nc, g, a)
        transformer(nc, g, a, d)
        if STOP == 7:
            return dump(nc, g, g.x, out)
        experts(nc, g, a, d)
        dump(nc, g, g.x, out)


_NAMES = ["x", "src", "dst", "L0_gnn_Wq", "L0_gnn_Wk", "L0_gnn_Wv", "L0_gnn_Wo", "L0_gnn_ln_g", "L0_gnn_ln_b", "L0_gnn_w1",
          "L0_gnn_b1", "L0_gnn_w2", "L0_gnn_b2", "L0_mix_w_qkv", "L0_mix_bn_gamma", "L0_mix_bn_beta", "L0_mix_w_dw",
          "L0_mix_w_pw", "L0_mix_w_res", "L0_mix_b_res", "L0_ffn_wr", "L0_ffn_br", "L0_ffn_w1", "L0_ffn_b1", "L0_ffn_w2",
          "L0_ffn_b2", "L1_gnn_W", "L1_mix_Wq", "L1_mix_Wk", "L1_mix_Wv", "L1_mix_Wo", "L1_mix_bo", "L1_mix_ln1_g",
          "L1_mix_ln1_b", "L1_mix_W1", "L1_mix_b1", "L1_mix_W2", "L1_mix_b2", "L1_mix_ln2_g", "L1_mix_ln2_b",
          "L1_ffn_W_gat", "L1_ffn_att_src", "L1_ffn_att_dst", "L1_ffn_b_gat", "L1_ffn_ln_gamma", "L1_ffn_ln_beta",
          "L1_ffn_W1", "L1_ffn_b1", "L1_ffn_W2", "L1_ffn_b2", "L1_ffn_edge_index"]


def _layout(name, a):
    if name == "L0_mix_w_qkv":
        a = a.transpose(2, 1, 0)
    if name == "L0_mix_w_dw":
        a = a.reshape(MIX, 5).transpose(1, 0)
    if name == "L0_mix_w_pw":
        a = a.reshape(6, 4, 32, 32).transpose(1, 3, 0, 2)
    if name == "L0_mix_w_res":
        a = a.reshape(D, 2 * D).transpose(1, 0)
    return np.ascontiguousarray(a)


def kernel(**inputs):
    import concourse.bacc as bacc
    from concourse.bass_utils import run_bass_kernel_spmd

    nc = bacc.Bacc("TRN2", target_bir_lowering=False, num_devices=1)
    arrays, aps = {}, {}
    for name in _NAMES:
        v = _layout(name, np.asarray(inputs[name]))
        arrays["in_" + name] = v
        aps[name] = nc.dram_tensor("in_" + name, v.shape, mybir.dt.from_np(v.dtype), kind="ExternalInput").ap()
    out = nc.dram_tensor("out", (N, D), F32, kind="ExternalOutput").ap()
    gps_program(nc, aps, out)
    return run_bass_kernel_spmd(nc, [arrays], core_ids=[0]).results[0]["out"]
```

```python
from contextlib import ExitStack, contextmanager
import math

import numpy as np
import concourse.bass as bass
from concourse import mybir

F32 = mybir.dt.float32
I32 = mybir.dt.int32
ALU = mybir.AluOpType
ACT = mybir.ActivationFunctionType
AX = mybir.AxisListType.X

N, D, E = 3125, 256, 100000
P = 125
NT = N // P
ET = E // P
NV = 832
CH, CS = 16, NV // 16
HEADS, DK = 8, 32
SEQ = CS * P
GG = 4
GROUPS = NV // GG
RC = 4
BIG = 1.0e30
MIX = 768
E2 = 65536
MAXNORM = float(np.float32(1.0) - np.float32(1e-5))
ATANH_MAX = 0.5 * math.log((1.0 + MAXNORM) / (1.0 - MAXNORM))


class Names:
    pass


COUNT = [0]


@contextmanager
def phase(nc, g, *names):
    COUNT[0] += 1
    sems = [nc.alloc_semaphore(f"{n}_{COUNT[0]}") for n in names]
    with nc.Block() as block:
        yield block, dict(zip(names, sems))
    nc.clear_and_free_semaphores(sems)
    nc.all_engine_barrier()


def hold(eng, sem, value):
    eng.wait_ge(sem, value)
    if not isinstance(value, int):
        eng.sem_inc(HELD[str(eng.engine)], 1)


HELD = {}


def hold_on(eng):
    return lambda sem, value: hold(eng, sem, value)


def before(eng, sem, t, unit=1, more=0, light=False):
    (eng.wait_ge if light else hold_on(eng))(sem, (t + 1) * unit + more)


def this(eng, sem, t, unit=1, more=0, light=False):
    (eng.wait_ge if light else hold_on(eng))(sem, (t + 2) * unit + more)


def landed(eng, sem, t, unit, light=False):
    (eng.wait_ge if light else hold_on(eng))(sem, (t + 1) * unit)


class Steps:

    def __init__(self, eng, sem, t=None, per=0):
        self.eng, self.sem, self.t, self.per, self.n = eng, sem, t, per, 0

    def __call__(self, ins):
        self.n += 1
        ins.then_inc(self.sem, 1)
        hold(self.eng, self.sem, self.n if self.t is None else self.t * self.per + self.n)

    def end(self):
        assert self.t is None or self.n == self.per, (self.n, self.per)


def col(ap, t, width=1):
    return ap[:, bass.ds(t * width, width)]


def setup(nc, ctx):
    g = Names()
    arena = ctx.enter_context(nc.sbuf_tensor("arena", [128, 39104], F32))

    def view(off, size, parts=128):
        return arena[0:parts, off:off + size]

    g.view = view
    g.x = view(0, NT * D, P)
    g.h = view(6400, NT * D, P)
    g.b2 = view(12800, NT * D, P)
    g.b3 = view(19200, NT * D, P)
    g.b4 = view(25600, NT * D, P)
    g.b5 = view(32000, NT * D, P)
    g.sums = view(12800, NT * (D + 9), P)
    g.score = view(19430, NV * HEADS, P)
    g.scan = view(26088, SEQ)
    g.link = view(32592, SEQ + 1)
    g.fwd = view(12800, SEQ)
    g.acc2 = view(30184, NT * (D + 9), P)

    def sb(name, shape, dt=F32):
        return ctx.enter_context(nc.sbuf_tensor(name, shape, dt))

    visit_src, visit_dst = sb("visit_src", [128, NV], I32), sb("visit_dst", [128, NV], I32)
    visit_rel = sb("visit_rel", [128, NV])
    g.srcv, g.dstv, g.relv = visit_src[0:P, :], visit_dst[0:P, :], visit_rel[0:P, :]
    EC = E2 // 128
    g.srcv_e, g.dstv_e, g.dlo = visit_src[:, 0:EC], visit_dst[:, 0:EC], visit_rel[:, 0:EC].bitcast(I32)
    g.wrow = sb("wrow", [1, NV], I32)
    g.ident = sb("ident", [128, 128])
    g.iota = sb("iota", [128, 128])
    g.ones = sb("ones", [128, 128])
    g.unit = sb("unit", [P, NT])
    g.dinv = sb("dinv", [P, NT])
    g.stat = sb("stat", [P, 8 * NT])
    g.coef = sb("coef", [P, 4 * NT])
    g.eps = sb("eps", [128, 1])
    g.zero = sb("zero", [128, 1])
    g.place_ix = sb("place_ix", [128, 8], I32)
    g.places = view(38400, E2 // 128).bitcast(I32)
    g.w1 = sb("w1", [128, 2048])
    g.w2 = sb("w2", [128, 2048])
    g.vec = sb("vec", [128, 64])
    g.brow = sb("brow", [1, 256])
    g.stage = sb("stage", [P, 512])
    g.ht = sb("ht", [128, MIX])
    g.h1 = sb("h1", [128, 2 * MIX])
    g.o = sb("o", [P, MIX])
    g.dhi = g.h1[:, 0:EC].bitcast(I32)
    g.ps = ctx.enter_context(nc.psum_tensor("ps", [128, 8, 512], F32))
    g.psT = g.ps[:, 0, 0:500]
    for e in (nc.sync, nc.scalar, nc.vector, nc.gpsimd, nc.tensor):
        HELD[str(e.engine)] = nc.alloc_semaphore("held_" + str(e.engine).split(".")[-1])
    return g


def constants(nc, g):
    with phase(nc, g, "made", "filled") as (block, s):
        it = g.view(0, 128).bitcast(I32)

        @block.gpsimd
        def _(pool):
            nc.gpsimd.iota(it, [[1, 128]], base=0, channel_multiplier=0).then_inc(s["made"], 1)
            nc.gpsimd.memset(g.ident[:, :], 0.0).then_inc(s["made"], 1)
            nc.gpsimd.memset(g.ones[:, :], 1.0).then_inc(s["made"], 1)
            nc.gpsimd.memset(g.unit[:, :], 1.0).then_inc(s["made"], 1)
            nc.gpsimd.memset(g.eps[:, :], 1e-5).then_inc(s["made"], 1)
            pool.wait_ge(s["made"], 5)
            nc.gpsimd.affine_select(out=g.ident[:, :], in_=g.ident[:, :], compare_op=ALU.not_equal, fill=1.0,
                                    base=0, pattern=[[-1, 128]], channel_multiplier=1).then_inc(s["filled"], 1)

        @block.vector
        def _(dve):
            dve.wait_ge(s["made"], 5)
            nc.vector.tensor_copy(g.iota[:, :], it).then_inc(s["filled"], 1)


def plan_visits(nc, g, src, dst, d):
    VP, VC = 104, 8
    src_rows = src.rearrange("(t e) -> t e", e=P)
    dst_rows = dst.rearrange("(t e) -> t e", e=P)
    v = g.view
    d0 = v(0, 8 * P, 100).bitcast(I32)
    last = v(1000, 8, 100)
    thr_i = v(1010, 24, 100).bitcast(I32)
    thr = v(1040, 24, 100)
    cmp = v(1070, 8 * 24, 100)
    wl = v(1270, 8, 100)
    tau_i = v(1280, 8, 100).bitcast(I32)
    tau_f = v(1290, 8, 100)
    key = v(1300, 8, 100)
    keyrow = v(1400, ET, VP)
    junk = v(2300, ET, VP)
    vi = v(3200, VC, VP).bitcast(I32)
    vf = v(3210, VC, VP)
    tau = v(3220, VC, VP)
    taui = v(3230, VC, VP).bitcast(I32)
    w = v(3240, VC, VP)
    wi = v(3250, VC, VP).bitcast(I32)
    wbase = v(3260, VC, VP)
    gs = v(4000, VC * P, VP).bitcast(I32)
    gd = v(5000, VC * P, VP).bitcast(I32)
    sf = v(6000, VC * P, VP)
    df = v(7000, VC * P, VP)
    rel = v(8000, VC * P, VP)
    inn = v(9000, VC * P, VP)
    pad = v(10000, 8, 1)
    keys = v(10100, SEQ + 2)
    with phase(nc, g, "loaded", "iotas", "step", "key_ready", "key_stored", "key_back", "tau_ready", "gathered",
               "made", "turned", "kept", "keys_stored", "keys_back", "stored", "pad_ready") as (block, s):

        @block.gpsimd
        def _(pool):
            nc.gpsimd.iota(thr_i, [[P, 24]], base=P, channel_multiplier=0).then_inc(s["iotas"], 1)
            nc.gpsimd.iota(tau_i, [[100, 8]], base=0, channel_multiplier=1).then_inc(s["iotas"], 1)
            nc.gpsimd.iota(vi, [[VP, VC]], base=0, channel_multiplier=1).then_inc(s["iotas"], 1)
            pool.wait_ge(s["tau_ready"], 1)
            for c in range(VC):
                at = bass.IndirectOffsetOnAxis(taui[:, c:c + 1], 0)
                nc.gpsimd.indirect_dma_start(gs[:, c * P:(c + 1) * P], None, src_rows, at).then_inc(s["gathered"], 16)
                nc.gpsimd.indirect_dma_start(gd[:, c * P:(c + 1) * P], None, dst_rows, at).then_inc(s["gathered"], 16)

        @block.sync
        def _(sp):
            sp.dma_start(d0.rearrange("p (k e) -> p k e", k=8),
                         dst.rearrange("(k p e) -> p k e", k=8, e=P)).then_inc(s["loaded"], 16)
            sp.wait_ge(s["key_ready"], 1)
            sp.dma_start(d.key.rearrange("(k p) -> p k", p=100), key,
                         allow_slow_non_contiguous=True).then_inc(s["key_stored"], 16)
            sp.wait_ge(s["key_stored"], 16)
            sp.dma_start(keyrow, d.key.partition_broadcast(VP)).then_inc(s["key_back"], 16)
            sp.wait_ge(s["tau_ready"], 2)
            sp.dma_start(d.w.rearrange("(c p) -> p c", p=VP), wi,
                         allow_slow_non_contiguous=True).then_inc(s["stored"], 16)
            sp.wait_ge(s["stored"], 16)
            sp.dma_start(g.wrow[:, :], d.w.rearrange("(a v) -> a v", a=1)).then_inc(s["stored"], 16)
            sp.wait_ge(s["pad_ready"], 1)
            sp.dma_start(d.keys[0:8].rearrange("(a v) -> a v", a=1), pad).then_inc(s["keys_stored"], 16)
            sp.dma_start(d.keys[8 + NV * P:16 + NV * P].rearrange("(a v) -> a v", a=1), pad).then_inc(s["keys_stored"], 16)
            sp.wait_ge(s["made"], 1)
            sp.dma_start(d.keys[8:8 + NV * P].rearrange("(c p e) -> p c e", c=VC, p=VP),
                         inn.rearrange("p (c e) -> p c e", c=VC)).then_inc(s["keys_stored"], 16)
            sp.wait_ge(s["keys_stored"], 48)
            for c in range(CH):
                sp.dma_start(keys[HEADS * c:HEADS * c + HEADS, :],
                             d.keys[7 + c * SEQ:9 + (c + 1) * SEQ].partition_broadcast(HEADS)).then_inc(s["keys_back"], 16)
            sp.wait_ge(s["stored"], 32)

        @block.vector
        def _(dve):
            step = Steps(dve, s["step"])
            V = nc.vector
            V.memset(pad, -5.0).then_inc(s["pad_ready"], 1)
            dve.wait_ge(s["iotas"], 3)
            dve.wait_ge(s["loaded"], 16)
            step(V.tensor_copy(last, d0[:, P - 1:8 * P:P]))
            step(V.tensor_copy(thr, thr_i))
            step(V.tensor_copy(tau_f, tau_i))
            step(V.tensor_copy(vf, vi))
            c3 = cmp.rearrange("p (k t) -> p k t", t=24)
            step(V.tensor_tensor(c3, last.unsqueeze(2).to_broadcast([100, 8, 24]),
                                 thr.unsqueeze(1).to_broadcast([100, 8, 24]), ALU.is_ge))
            step(V.tensor_reduce(wl, c3, AX, ALU.add))
            V.tensor_tensor(key, wl, tau_f, ALU.add).then_inc(s["key_ready"], 1)
            dve.wait_ge(s["key_back"], 16)
            for c in range(VC):
                step(V.tensor_scalar(junk[:, 0:ET - 1], keyrow[:, 0:ET - 1], vf[:, c:c + 1], 0.0, ALU.is_lt, ALU.add,
                                     accum_out=tau[:, c:c + 1]))
            V.tensor_copy(taui, tau).then_inc(s["tau_ready"], 1)
            step(V.tensor_tensor(w, vf, tau, ALU.subtract))
            step(V.tensor_scalar(wbase, w, float(P), None, ALU.mult))
            step(V.tensor_scalar(w, w, float(NT - 1), None, ALU.min))
            V.tensor_copy(wi, w).then_inc(s["tau_ready"], 1)
            dve.wait_ge(s["gathered"], 32 * VC)
            step(V.tensor_copy(sf, gs))
            step(V.tensor_copy(df, gd))
            for c in range(VC):
                a, b = c * P, (c + 1) * P
                step(V.tensor_scalar(rel[:, a:b], df[:, a:b], wbase[:, c:c + 1], None, ALU.subtract))
            step(V.tensor_scalar(inn, rel, 0.0, None, ALU.is_ge))
            step(V.scalar_tensor_tensor(inn, rel, float(P), inn, ALU.is_lt, ALU.mult))
            V.scalar_tensor_tensor(inn, df, 1.0, inn, ALU.add, ALU.mult).then_inc(s["made"], 1)
            for c in range(VC):
                dve.wait_ge(s["turned"], c + 1)
                out = slice(c * VP, (c + 1) * VP)
                b = g.ps[0:P, 2 * (c % 2), 0:512]
                V.tensor_copy(g.srcv[:, out], b[:, 0:VP])
                V.tensor_copy(g.dstv[:, out], b[:, 128:128 + VP])
                V.tensor_copy(g.relv[:, out], b[:, 256:256 + VP]).then_inc(s["kept"], 1)
            dve.wait_ge(s["keys_back"], 16 * CH)
            dve.wait_ge(s["kept"], VC)
            step(V.tensor_tensor(g.link, keys[:, 1:SEQ + 2], keys[:, 0:SEQ + 1], ALU.not_equal))
            V.tensor_scalar(g.link, g.link, -BIG, None, ALU.mult)

        @block.tensor
        def _(pe):
            pe.wait_ge(s["made"], 1)
            for c in range(VC):
                if c >= 2:
                    pe.wait_ge(s["kept"], c - 1)
                a, b = c * P, (c + 1) * P
                bank = g.ps[0:P, 2 * (c % 2), 0:512]
                nc.tensor.transpose(bank[:, 0:VP], sf[:, a:b], g.ident[0:VP, 0:VP])
                nc.tensor.transpose(bank[:, 128:128 + VP], df[:, a:b], g.ident[0:VP, 0:VP])
                nc.tensor.transpose(bank[:, 256:256 + VP], rel[:, a:b], g.ident[0:VP, 0:VP]).then_inc(s["turned"], 1)


def spill(nc, g, links):
    with phase(nc, g, "moved") as (block, s):
        @block.sync
        def _(sp):
            sp.dma_start(links, g.link).then_inc(s["moved"], 16)
            sp.wait_ge(s["moved"], 16)


def store(nc, g, ap, out):
    with phase(nc, g, "written") as (block, s):
        @block.sync
        def _(sp):
            sp.dma_start(out.rearrange("(t p) n -> p t n", p=P),
                         ap.rearrange("p (t n) -> p t n", t=NT)).then_inc(s["written"], 16)
            sp.wait_ge(s["written"], 16)


def layernorm(nc, g, x, out, gamma=None, beta=None):
    O3 = out.rearrange("p (t n) -> p t n", t=NT)
    mean, var, rstd, shift = (g.stat[:, k * NT:(k + 1) * NT] for k in range(4))
    std = g.stat[:, 4 * NT:5 * NT]
    parts = g.ht[0:P, 0:6 * NT]
    P3 = parts.rearrange("p (t c) -> p t c", c=6)
    wide = [P, NT, D]
    half = 15
    with phase(nc, g, "step", "counted", "var_ready", "std_ready", "ready", "scaled", "loaded") as (block, s):
        if gamma is not None:
            @block.sync
            def _(sp):
                sp.dma_start(g.w1[0:P, 0:D], gamma.partition_broadcast(P)).then_inc(s["loaded"], 16)
                sp.dma_start(g.w1[0:P, D:2 * D], beta.partition_broadcast(P)).then_inc(s["loaded"], 16)

        @block.vector
        def _(dve):
            step = Steps(dve, s["step"])
            V = nc.vector
            with dve.Fori(0, NT // 5) as i:
                for n in range(5):
                    V.bn_stats(col(parts, i * 5 + n, 6), col(x, i * 5 + n, D)).then_inc(s["counted"], 1)
            dve.wait_ge(s["counted"], NT)
            step(V.tensor_tensor(mean, P3[:, :, 1], P3[:, :, 4], ALU.add))
            step(V.tensor_tensor(shift, P3[:, :, 1], P3[:, :, 4], ALU.subtract))
            step(V.tensor_scalar(mean, mean, 0.5, None, ALU.mult))
            step(V.tensor_tensor(var, P3[:, :, 2], P3[:, :, 5], ALU.add))
            step(V.tensor_tensor(shift, shift, shift, ALU.mult))
            V.scalar_tensor_tensor(var, shift, D / 4.0, var, ALU.mult, ALU.add).then_inc(s["var_ready"], 1)
            dve.wait_ge(s["std_ready"], 1)
            step(V.reciprocal(rstd, std))
            V.scalar_tensor_tensor(shift, mean, -1.0, rstd, ALU.mult, ALU.mult).then_inc(s["ready"], 1)
            dve.wait_ge(s["ready"], 1)
            with dve.Fori(0, half // 5) as i:
                for n in range(5):
                    t = i * 5 + n
                    V.tensor_scalar(col(out, t, D), col(x, t, D), col(rstd, t), col(shift, t), ALU.mult,
                                    ALU.add).then_inc(s["scaled"], 1)
            if gamma is not None:
                dve.wait_ge(s["scaled"], NT)
                dve.wait_ge(s["loaded"], 32)
                step(V.tensor_tensor(O3, O3, g.w1[0:P, 0:D].unsqueeze(1).to_broadcast(wide), ALU.mult))
                step(V.tensor_tensor(O3, O3, g.w1[0:P, D:2 * D].unsqueeze(1).to_broadcast(wide), ALU.add))

        @block.scalar
        def _(act):
            act.wait_ge(s["var_ready"], 1)
            nc.scalar.activation(std, var, ACT.Sqrt, bias=g.eps[0:P, :], scale=1.0 / D).then_inc(s["std_ready"], 1)
            act.wait_ge(s["ready"], 1)
            with act.Fori(0, (NT - half) // 5) as i:
                for n in range(5):
                    t = i * 5 + (half + n)
                    nc.scalar.activation(col(out, t, D), col(x, t, D), ACT.Identity, bias=col(shift, t),
                                         scale=col(rstd, t)).then_inc(s["scaled"], 1)


def tile_pass(nc, g, src, nk, outs, loads, finish, scale=None, affine=None, hidden=None, bias=False, tables=None, row=None, side=None):
    C = nk * 128
    nj = hidden[0] // 128 if hidden else 0
    half = nj // 2
    stage_ = [g.stage[:, u * C:(u + 1) * C] for u in range(2)]
    hT_ = [g.ht[:, u * nk * P:(u + 1) * nk * P].rearrange("p (k r) -> p k r", r=P) for u in range(2)]
    psT_ = [g.ps[:, u, 0:nk * P].rearrange("p (k r) -> p k r", r=P) for u in range(2)]
    h1 = g.h1[:, 0:8 * P].rearrange("p (j r) -> p j r", r=P)

    def up(j):
        return g.ps[:, 2 + j // half, (j % half) * P:(j % half + 1) * P]

    with phase(nc, g, "loaded", "staged", "turned", "fetched", "up_a", "up_b", "act_a", "act_b", "down",
               "stored", "written", "side_a", "side_b") as (block, s):
        if side:
            side(block, s)

        @block.sync
        def _(sp):
            for dst, dram in loads:
                sp.dma_start(dst, dram, allow_slow_non_contiguous=True).then_inc(s["loaded"], 16)
            if tables:
                n = 16 * len(tables)
                sp.sem_inc(s["written"], n)
                with sp.Fori(0, NT) as t:
                    this(sp, s["stored"], t)
                    for dram, ap in tables:
                        sp.dma_start(dram[bass.ds(t * P, P), :], ap).then_inc(s["written"], 16)
                this(sp, s["written"], NT - 1, n)

        @block.scalar
        def _(act):
            act.sem_inc(s["staged"], 1)
            act.sem_inc(s["act_a"], 1)
            act.sem_inc(s["act_b"], 1)
            if hidden:
                act.wait_ge(s["loaded"], 16 * len(loads))

            def stage(t, u):
                kw = {} if scale is None else {"scale": col(scale, t)}
                nc.scalar.activation(stage_[u], src[:, bass.ds(t * (row or C), C)], ACT.Copy, **kw).then_inc(s["staged"], 1)

            def round_(t, u, ahead):
                if ahead:
                    this(act, s["turned"], t)
                    stage(t + 2, u)
                if hidden:
                    for j in range(nj):
                        if j % half == 0:
                            this(act, s["up_b"] if j else s["up_a"], t)
                            if not j:
                                before(act, s["down"], t)
                        ins = nc.scalar.activation(h1[:, j, :], up(j), hidden[1], bias=g.vec[:, j:j + 1])
                        if j % half == half - 1:
                            ins.then_inc(s["act_b"] if j == nj - 1 else s["act_a"], 1)

            stage(0, 0)
            stage(1, 1)
            with act.Fori(0, NT // 2 - 1) as i:
                round_(i * 2, 0, True)
                round_(i * 2 + 1, 1, True)
            round_(NT - 3, 0, True)
            round_(NT - 2, 1, False)
            round_(NT - 1, 0, False)

        @block.tensor
        def _(pe):
            pe.sem_inc(s["turned"], 1)
            pe.sem_inc(s["up_a"], 1)
            pe.sem_inc(s["up_b"], 1)
            pe.sem_inc(s["down"], 1)

            def turn(t, u):
                this(pe, s["staged"], t)
                for k in range(nk):
                    ins = nc.tensor.transpose(psT_[u][:, k, :], stage_[u][:, k * 128:(k + 1) * 128], g.ident[0:P, 0:P])
                ins.then_inc(s["turned"], 1)

            def round_(t, u, last):
                hT = hT_[u]
                this(pe, s["fetched"], t)
                if hidden:
                    for j in range(nj):
                        for k in range(nk):
                            ins = nc.tensor.matmul(up(j), g.w1[:, k * hidden[0] + j * 128:k * hidden[0] + (j + 1) * 128],
                                                   hT[:, k, :], start=(k == 0), stop=(k == nk - 1))
                        if j % half == half - 1:
                            ins.then_inc(s["up_b"] if j == nj - 1 else s["up_a"], 1)
                if not last:
                    turn(t + 1, 1 - u)
                lhs = [h1[:, j, :] for j in range(nj)] if hidden else [hT[:, k, :] for k in range(nk)]
                for m, left in enumerate(lhs):
                    if hidden and m % half == 0:
                        this(pe, s["act_b"] if m else s["act_a"], t)
                    for wt, ps in outs:
                        ins = nc.tensor.matmul(ps[u], left, wt(m), start=(m == 0), stop=(m == len(lhs) - 1 and not bias))
                if bias:
                    for wt, ps in outs:
                        ins = nc.tensor.matmul(ps[u], g.ones[0:1, 0:P], g.brow[0:1, :], start=False, stop=True)
                ins.then_inc(s["down"], 1)

            pe.wait_ge(s["loaded"], 16 * len(loads))
            turn(0, 0)
            with pe.Fori(0, NT // 2) as i:
                round_(i * 2, 0, False)
                round_(i * 2 + 1, 1, False)
            round_(NT - 1, 0, True)

        @block.vector
        def _(dve):
            dve.sem_inc(s["fetched"], 1)
            dve.sem_inc(s["stored"], 1)
            dve.wait_ge(s["loaded"], 16 * len(loads))

            def fetch(t, u):
                this(dve, s["turned"], t)
                if affine is None:
                    ins = nc.vector.tensor_copy(hT_[u], psT_[u])
                else:
                    for k in range(nk):
                        ins = nc.vector.tensor_scalar(hT_[u][:, k, :], psT_[u][:, k, :], affine[0][:, k:k + 1],
                                                      affine[1][:, k:k + 1], ALU.mult, ALU.add)
                ins.then_inc(s["fetched"], 1)

            def round_(t, u, last):
                if not last:
                    fetch(t + 1, 1 - u)
                this(dve, s["down"], t)
                if tables:
                    before(dve, s["written"], t, 16 * len(tables))
                finish(nc.vector, t, u).then_inc(s["stored"], 1)

            fetch(0, 0)
            with dve.Fori(0, NT // 2) as i:
                round_(i * 2, 0, False)
                round_(i * 2 + 1, 1, False)
            round_(NT - 1, 0, True)


def penalty_indices(nc, g, a):
    EC = E2 // 128
    sI, dI = g.view(19200, EC).bitcast(I32), g.view(19800, EC).bitcast(I32)
    sF, dF = g.view(20400, EC), g.view(21000, EC)
    ei = a["L1_ffn_edge_index"]
    with phase(nc, g, "loaded", "step") as (block, s):
        @block.sync
        def _(sp):
            sp.dma_start(sI, ei[0].rearrange("(p c) -> p c", p=128)).then_inc(s["loaded"], 16)
            sp.dma_start(dI, ei[1].rearrange("(p c) -> p c", p=128)).then_inc(s["loaded"], 16)

        @block.vector
        def _(dve):
            V = nc.vector
            step = Steps(dve, s["step"])
            dve.wait_ge(s["loaded"], 32)
            step(V.memset(g.zero[:, :], 0.0))
            step(V.tensor_copy(sF, sI))
            step(V.tensor_copy(dF, dI))
            step(V.tensor_scalar(sF, sF, float(N - 1), None, ALU.min))
            step(V.scalar_tensor_tensor(dF, dF, float(N), sF, ALU.mult, ALU.add))
            step(V.tensor_copy(g.places, dF))


def fill_penalties(nc, g, d):
    def side(block, s):
        fill = g.view(19200, N, P)

        @block.gpsimd
        def _(pool):
            nc.gpsimd.memset(fill, -BIG).then_inc(s["side_a"], 1)
            pool.wait_ge(s["side_a"], 1)
            for t in range(NT):
                nc.gpsimd.dma_start(d.pen[t * P * N:(t + 1) * P * N].rearrange("(p n) -> p n", p=P),
                                    fill).then_inc(s["side_b"], 16)
            pool.wait_ge(s["side_b"], 16 * NT)
    return side


def lift_penalties(nc, g, d, start, count):
    GS = 8

    def side(block, s):
        @block.gpsimd
        def _(pool):
            pool.sem_inc(s["side_a"], 1)
            with pool.Fori(0, count // GS) as i:
                nc.gpsimd.tensor_copy(g.place_ix[:, :], g.places[:, bass.ds(i * GS + start, GS)]).then_inc(s["side_a"], 1)
                this(pool, s["side_a"], i)
                for j in range(GS):
                    nc.gpsimd.indirect_dma_start(d.pen.rearrange("(n o) -> n o", o=1),
                                                 bass.IndirectOffsetOnAxis(g.place_ix[:, j:j + 1], 0), g.zero[:, :], None,
                                                 bounds_check=N * N - 1, oob_is_err=False).then_inc(s["side_b"], 16)
                    hold(pool, s["side_b"], i * (16 * GS) + 16 * (j + 1))
    return side


def add_into(ps, dst, coef, width=D):
    def finish(V, t, u):
        return V.scalar_tensor_tensor(col(dst, t, width), ps[u], col(coef, t), col(dst, t, width), ALU.mult, ALU.add)
    return finish


def mm_weights(buf, n):
    return lambda k: buf[:, k * n:(k + 1) * n]


def split_k(dram, nk):
    return dram.rearrange("(k p) n -> p k n", k=nk)


def w3(buf, nk, n):
    return buf[:, 0:nk * n].rearrange("p (k n) -> p k n", k=nk)


def mlp(nc, g, src, w1, b1, w2, b2, func, dst, coef, affine=None, scale=None, extra=(), side=None):
    H = w1.shape[1]
    nj = H // 128
    down = [g.ps[0:P, 4 + u, 0:D] for u in range(2)]
    loads = [(w3(g.w1, 2, H), split_k(w1, 2)), (w3(g.w2, nj, D), split_k(w2, nj)),
             (g.vec[:, 0:nj], b1.rearrange("(j p) -> p j", p=128)),
             (g.brow[:, :], b2.rearrange("(a n) -> a n", a=1))] + list(extra)
    tile_pass(nc, g, src, 2, [(mm_weights(g.w2, D), down)], loads, add_into(down, dst, coef),
              scale=scale, hidden=(H, func), bias=True, affine=affine, side=side)



def groups(i, c):
    return i * RC + c, i * 2 + c // 2, c % 2


def one_hots(nc, g, oh, k):
    wide = [P, GG, P]
    return nc.vector.tensor_tensor(oh.rearrange("p (j n) -> p j n", j=GG), g.iota[0:P, 0:P].unsqueeze(1).to_broadcast(wide),
                                   g.relv[:, bass.ds(k * GG, GG)].unsqueeze(2).to_broadcast(wide), ALU.is_equal)


def edge_scores(nc, g, q, k_table, links):
    ring = g.scan[0:P, 0:RC * GG * D]
    oh = [g.w1[0:P, u * GG * P:(u + 1) * GG * P] for u in range(2)]
    ohT = [g.w1[0:P, (2 + u) * GG * P:(3 + u) * GG * P] for u in range(2)]
    pr = [g.h1[0:P, 0:GG * D], g.w2[0:P, 0:GG * D]]
    ix = g.ht[0:P, 0:RC * GG].bitcast(I32)
    psQ = [g.ps[0:P, 2 * u:2 * u + 2, :].rearrange("p b (j n) -> p (b j) n", j=2) for u in range(2)]
    psT = [g.ps[0:P, 4 + u, 0:GG * P].rearrange("p (j n) -> p j n", j=GG) for u in range(2)]
    names = [f"got{c}" for c in range(RC)] + [f"{n}{u}" for n in ("hot", "turned", "kept", "picked", "used") for u in range(2)]
    with phase(nc, g, "indexed", "reduced", "linked", *names) as (block, s):
        got = [s[f"got{c}"] for c in range(RC)]
        hot, turned, kept, picked, used = ([s[f"{n}{u}"] for u in range(2)] for n in ("hot", "turned", "kept", "picked", "used"))

        @block.gpsimd
        def _(pool):
            with pool.Fori(0, GROUPS // RC) as i:
                for c in range(RC):
                    hold(pool, used[c % 2], i * 2 + c // 2 + 1)
                    nc.gpsimd.tensor_copy(ix[:, c * GG:(c + 1) * GG],
                                          g.srcv[:, bass.ds(i * (RC * GG) + c * GG, GG)]).then_inc(s["indexed"], 1)
                    hold(pool, s["indexed"], i * RC + c + 1)
                    for j in range(c * GG, (c + 1) * GG):
                        nc.gpsimd.indirect_dma_start(ring[:, j * D:(j + 1) * D], None, k_table,
                                                     bass.IndirectOffsetOnAxis(ix[:, j:j + 1], 0)).then_inc(got[c], 16)

        @block.sync
        def _(sp):
            sp.dma_start(g.link, links).then_inc(s["linked"], 16)
            sp.wait_ge(s["linked"], 16)

        @block.scalar
        def _(act):
            for q_ in kept:
                act.sem_inc(q_, 1)
            with act.Fori(0, GROUPS // RC) as i:
                for c in range(RC):
                    k, r, u = groups(i, c)
                    this(act, turned[u], r, light=True)
                    nc.scalar.copy(ohT[u].rearrange("p (j n) -> p j n", j=GG), psT[u]).then_inc(kept[u], 1)

        @block.tensor
        def _(pe):
            for q_ in turned + picked:
                pe.sem_inc(q_, 1)

            def turn(r, u):
                this(pe, hot[u], r, light=True)
                for j in range(GG):
                    ins = nc.tensor.transpose(psT[u][:, j, :], oh[u][:, j * P:(j + 1) * P], g.ident[0:P, 0:P])
                ins.then_inc(turned[u], 1)

            def pick(k, r, u):
                this(pe, kept[u], r)
                before(pe, used[u], r, more=1)
                for j in range(GG):
                    tile = pe.value_load(g.wrow[0:1, bass.ds(k * GG + j, 1)], min_val=0, max_val=NT - 1)
                    ins = nc.tensor.matmul(psQ[u][:, j, :], ohT[u][:, j * P:(j + 1) * P], q[:, bass.ds(tile * D, D)],
                                           start=True, stop=True)
                ins.then_inc(picked[u], 1)

            def round_(i, c, last):
                k, r, u = groups(i, c)
                if not last:
                    turn(r + u, 1 - u)
                pick(k, r, u)

            turn(0, 0)
            with pe.Fori(0, GROUPS // RC - 1) as i:
                for c in range(RC):
                    round_(i, c, False)
            for c in range(RC):
                round_(GROUPS // RC - 1, c, c == RC - 1)

        @block.vector
        def _(dve):
            for q_ in used + used + hot + [s["reduced"]]:
                dve.sem_inc(q_, 1)

            def round_(i, c, last):
                k, r, u = groups(i, c)
                if not last:
                    this(dve, turned[u], r, light=True)
                    one_hots(nc, g, oh[u], k + 2).then_inc(hot[u], 1)
                landed(dve, got[c], i, 16 * GG, light=True)
                this(dve, picked[u], r, light=True)
                hold(dve, s["reduced"], k + 1)
                nc.vector.tensor_tensor(pr[u].rearrange("p (j n) -> p j n", j=GG),
                                        ring[:, c * GG * D:(c + 1) * GG * D].rearrange("p (j n) -> p j n", j=GG),
                                        psQ[u], ALU.mult).then_inc(used[u], 1)
                this(dve, used[u], r, more=1)
                nc.vector.tensor_reduce(g.score[:, bass.ds(k * (GG * HEADS), GG * HEADS)],
                                        pr[u].rearrange("p (m d) -> p m d", d=DK), AX, ALU.add).then_inc(s["reduced"], 1)

            for k in range(2):
                one_hots(nc, g, oh[k], k).then_inc(hot[k], 1)
            with dve.Fori(0, GROUPS // RC - 1) as i:
                for c in range(RC):
                    round_(i, c, False)
            for c in range(RC):
                round_(GROUPS // RC - 1, c, c >= RC - 2)


def segment_softmax(nc, g):
    sc4 = g.score.rearrange("p (c s h) -> p c s h", c=CH, s=CS)
    TB = 2
    turns = CS // TB
    st = [g.o[0:P, 256 * u:256 * u + 256] for u in range(2)]
    st2 = [g.h1[:, 256 * u:256 * u + TB * P] for u in range(2)]
    fwd = g.fwd
    ends = g.w1[:, 0:2]
    rows = g.w2[0:1, 0:4 * 128]
    init = g.w1[:, 4:5]
    psA = [g.ps[:, u, 0:TB * P] for u in range(2)]
    pairs = [f"{n}{u}" for n in ("staged", "turned", "kept") for u in range(2)]
    with phase(nc, g, *pairs) as (block, s):
        staged, turned, kept = ([s[f"{n}{u}"] for u in range(2)] for n in ("staged", "turned", "kept"))

        @block.vector
        def _(dve):
            for q in staged:
                dve.sem_inc(q, 1)
            with dve.Fori(0, turns // 2) as i:
                for u in range(2):
                    before(dve, turned[u], i)
                    nc.vector.tensor_copy(st[u].rearrange("p (s c h) -> p c s h", s=TB, c=CH),
                                          sc4[:, :, bass.ds(i * (2 * TB) + TB * u, TB), :]).then_inc(staged[u], 1)

        @block.tensor
        def _(pe):
            for q in turned:
                pe.sem_inc(q, 1)
            with pe.Fori(0, turns // 2) as i:
                for u in range(2):
                    this(pe, staged[u], i)
                    before(pe, kept[u], i)
                    for n in range(TB):
                        ins = nc.tensor.transpose(psA[u][:, n * P:(n + 1) * P], st[u][:, n * 128:(n + 1) * 128],
                                                  g.ident[0:P, 0:P])
                    ins.then_inc(turned[u], 1)

        @block.scalar
        def _(act):
            for q in kept:
                act.sem_inc(q, 1)
            with act.Fori(0, turns // 2) as i:
                for u in range(2):
                    this(act, turned[u], i)
                    nc.scalar.copy(col(g.scan, i * 2 + u, TB * P), psA[u]).then_inc(kept[u], 1)

    with phase(nc, g, "step", "put", "rowed", "carried", "turned_back") as (block, s):
        psR = g.ps[0:1, 1, 0:256]
        psC = g.ps[:, 2, 0:1]

        @block.vector
        def _(dve):
            V = nc.vector
            step = Steps(dve, s["step"])
            for n in range(2):
                if n == 0:
                    dst, data, link = fwd, g.scan, g.link[:, 0:SEQ]
                    end = SEQ - 1
                else:
                    dst, data, link = g.scan[:, ::-1], fwd[:, ::-1], g.link[:, 1:SEQ + 1][:, ::-1]
                    end = 0
                step(V.tensor_reduce(ends[:, 0:1], g.link[:, n:SEQ + n], AX, ALU.min))
                step(V.tensor_tensor_scan(dst, link, data, -BIG, ALU.add, ALU.max))
                tail = fwd[:, end:end + 1] if n == 0 else g.scan[:, end:end + 1]
                V.tensor_copy(ends[:, 1:2], tail).then_inc(s["put"], 1)
                dve.wait_ge(s["rowed"], n + 1)
                step(V.tensor_copy(rows[:, 0:256], psR))
                step(V.memset(rows[:, 384:512], -BIG))
                for h in range(HEADS):
                    a = rows[0:1, h:128:HEADS]
                    b = rows[0:1, 128 + h:256:HEADS]
                    o = rows[0:1, 256 + h:384:HEADS]
                    if n:
                        a, b, o = a[:, ::-1], b[:, ::-1], o[:, ::-1]
                    step(V.tensor_tensor_scan(o, a, b, -BIG, ALU.add, ALU.max))
                if n == 0:
                    V.tensor_copy(rows[:, 384 + HEADS:512], rows[:, 256:384 - HEADS]).then_inc(s["carried"], 1)
                else:
                    V.tensor_copy(rows[:, 384:512 - HEADS], rows[:, 256 + HEADS:384]).then_inc(s["carried"], 1)
                dve.wait_ge(s["turned_back"], n + 1)
                step(V.tensor_copy(init[:, :], psC))
                if n == 0:
                    step(V.tensor_tensor_scan(fwd, link, data, init[:, :], ALU.add, ALU.max))
                else:
                    step(V.tensor_tensor_scan(dst, link, data, init[:, :], ALU.add, ALU.max))

        @block.tensor
        def _(pe):
            for n in range(2):
                pe.wait_ge(s["put"], n + 1)
                nc.tensor.transpose(psR[:, 0:128], ends[:, 0:1], g.ident[:, :])
                nc.tensor.transpose(psR[:, 128:256], ends[:, 1:2], g.ident[:, :]).then_inc(s["rowed"], 1)
                pe.wait_ge(s["carried"], n + 1)
                nc.tensor.matmul(psC, rows[0:1, 384:512], g.ones[0:1, 0:1], start=True, stop=True).then_inc(s["turned_back"], 1)

    with phase(nc, g, *pairs) as (block, s):
        staged, turned, kept = ([s[f"{n}{u}"] for u in range(2)] for n in ("staged", "turned", "kept"))
        psB = [g.ps[0:P, u, 0:TB * 128] for u in range(2)]

        @block.scalar
        def _(act):
            for q in staged:
                act.sem_inc(q, 1)
            with act.Fori(0, turns // 2) as i:
                for u in range(2):
                    before(act, turned[u], i)
                    nc.scalar.copy(st2[u], col(g.scan, i * 2 + u, TB * P)).then_inc(staged[u], 1)

        @block.tensor
        def _(pe):
            for q in turned:
                pe.sem_inc(q, 1)
            with pe.Fori(0, turns // 2) as i:
                for u in range(2):
                    this(pe, staged[u], i)
                    before(pe, kept[u], i)
                    for n in range(TB):
                        ins = nc.tensor.transpose(psB[u][:, n * 128:(n + 1) * 128], st2[u][:, n * P:(n + 1) * P], g.ident[:, :])
                    ins.then_inc(turned[u], 1)

        @block.vector
        def _(dve):
            for q in kept:
                dve.sem_inc(q, 1)
            with dve.Fori(0, turns // 2) as i:
                for u in range(2):
                    this(dve, turned[u], i)
                    sl = sc4[:, :, bass.ds(i * (2 * TB) + TB * u, TB), :]
                    nc.vector.tensor_tensor(sl, sl, psB[u].rearrange("p (s c h) -> p c s h", s=TB, c=CH),
                                            ALU.subtract).then_inc(kept[u], 1)

    with phase(nc, g, "done") as (block, s):
        @block.scalar
        def _(act):
            nc.scalar.activation(g.score, g.score, ACT.Exp, scale=1.0 / math.sqrt(DK)).then_inc(s["done"], 1)
            act.wait_ge(s["done"], 1)


def edge_sums(nc, g, table, acc, weighted):
    ncol = D + 9 if weighted else D
    accs = [acc, g.acc2[:, 0:NT * ncol]]
    W = GG * (D + 9)
    ring = (g.scan if weighted else g.score)[0:P, 0:RC * GG * D]
    ms = [w[0:P, 0:W].rearrange("p (j n) -> p j n", j=GG) for w in (g.w1, g.w2)]
    oh = [w[0:P, W:W + GG * P] for w in (g.w1, g.w2)]
    ix = g.ht[0:P, 0:RC * GG].bitcast(I32)
    apart = [g.stage[:, 0:GG * P], g.o[:, 0:GG * P]]
    names = [f"got{c}" for c in range(RC)] + [f"{n}{u}" for n in ("hot", "made", "summed") for u in range(2)]
    with phase(nc, g, "indexed", "zeroed", "squared", "added", *names) as (block, s):
        got = [s[f"got{c}"] for c in range(RC)]
        hot, made, summed = ([s[f"{n}{u}"] for u in range(2)] for n in ("hot", "made", "summed"))
        freed = made if weighted else summed
        s2 = 0 if weighted else 1
        credit = GG + 1

        @block.gpsimd
        def _(pool):
            with pool.Fori(0, GROUPS // RC) as i:
                for c in range(RC):
                    hold(pool, freed[c % 2], i * 2 + c // 2 + 1)
                    nc.gpsimd.tensor_copy(ix[:, c * GG:(c + 1) * GG],
                                          g.srcv[:, bass.ds(i * (RC * GG) + c * GG, GG)]).then_inc(s["indexed"], 1)
                    hold(pool, s["indexed"], i * RC + c + 1)
                    for j in range(c * GG, (c + 1) * GG):
                        nc.gpsimd.indirect_dma_start(ring[:, j * D:(j + 1) * D], None, table,
                                                     bass.IndirectOffsetOnAxis(ix[:, j:j + 1], 0)).then_inc(got[c], 16)

        @block.scalar
        def _(act):
            for q in hot:
                act.sem_inc(q, 1)
            if weighted:
                act.wait_ge(s["zeroed"], 2)
            with act.Fori(0, GROUPS // RC) as i:
                for c in range(RC):
                    k, r, u = groups(i, c)
                    before(act, summed[u], r, more=s2)
                    for j in range(GG):
                        ins = nc.scalar.activation(apart[u][:, j * P:(j + 1) * P], g.iota[0:P, 0:P], ACT.Square, scale=-1.0,
                                                   bias=g.relv[:, bass.ds(k * GG + j, 1)])
                    ins.then_inc(s["squared"], 1)
                    if weighted:
                        nc.scalar.copy(ms[u][:, :, D:D + HEADS],
                                       g.score[:, bass.ds(k * (GG * HEADS), GG * HEADS)].rearrange("p (j h) -> p j h", j=GG))
                    hold(act, s["squared"], k + 1)
                    nc.scalar.activation(oh[u], apart[u], ACT.Relu, scale=-1.0, bias=1.0).then_inc(hot[u], 1)

        @block.vector
        def _(dve):
            V = nc.vector
            V.memset(accs[0], 0.0)
            V.memset(accs[1], 0.0).then_inc(s["zeroed"], 1)
            if weighted:
                for u in range(2):
                    ins = V.memset(ms[u][:, :, D:D + 9], 1.0)
                ins.then_inc(s["zeroed"], 1)
            dve.wait_ge(s["zeroed"], 2 if weighted else 1)
            for q in made + made:
                dve.sem_inc(q, 1)
            dve.sem_inc(s["added"], credit)

            def weigh(i, c):
                k, r, u = groups(i, c)
                landed(dve, got[c], i, 16 * GG, light=True)
                wide = [P, GG, HEADS, DK]
                V.tensor_tensor(ms[u][:, :, 0:D].rearrange("p j (h d) -> p j h d", h=HEADS),
                                ring[:, c * GG * D:(c + 1) * GG * D].rearrange("p (j h d) -> p j h d", j=GG, h=HEADS),
                                g.score[:, bass.ds(k * (GG * HEADS), GG * HEADS)]
                                .rearrange("p (j h) -> p j h", j=GG).unsqueeze(3).to_broadcast(wide), ALU.mult).then_inc(made[u], 1)

            def add(k, r, u):
                tiles = [dve.value_load(g.wrow[0:1, bass.ds(k * GG + j, 1)], min_val=0, max_val=NT - 1) for j in range(GG)]
                this(dve, summed[u], r, more=s2, light=True)
                for j, tile in enumerate(tiles):
                    dve.wait_ge(s["added"], k * GG + (j - 1 + credit))
                    at = accs[j % 2][:, bass.ds(tile * ncol, ncol)]
                    V.tensor_tensor(at, at,
                                    g.ps[0:P, GG * u + j, 0:ncol], ALU.add).then_inc(s["added"], 1)

            def round_(i, c, first):
                if weighted:
                    weigh(i, c)
                if not first:
                    k, r, u = groups(i, c)
                    add(k - 1, r - 1 + u, 1 - u)

            R = GROUPS // RC
            for c in range(RC):
                round_(0, c, c == 0)
            with dve.Fori(1, R) as i:
                for c in range(RC):
                    round_(i, c, False)
            add(GROUPS - 1, GROUPS // 2 - 1, 1)
            dve.wait_ge(s["added"], NV + credit)
            V.tensor_tensor(acc, acc, accs[1], ALU.add)

        @block.tensor
        def _(pe):
            for q in summed:
                pe.sem_inc(q, 1 + s2)
            with pe.Fori(0, GROUPS // RC) as i:
                for c in range(RC):
                    k, r, u = groups(i, c)
                    this(pe, hot[u], r)
                    if weighted:
                        this(pe, made[u], r, more=1, light=True)
                    else:
                        hold(pe, s["added"], (k - 1) * GG + credit)
                        landed(pe, got[c], i, 16 * GG, light=True)
                    for j in range(GG):
                        rows = ms[u][:, j, 0:ncol] if weighted else ring[:, (c * GG + j) * D:(c * GG + j + 1) * D]
                        ins = nc.tensor.matmul(g.ps[0:P, GG * u + j, 0:ncol], oh[u][:, j * P:(j + 1) * P], rows,
                                               start=True, stop=True)
                    ins.then_inc(summed[u], 1)



def norm_factor(V, step, out, sumsq_root, limit):
    step(V.tensor_scalar(sumsq_root, sumsq_root, 1e-15, None, ALU.max))
    step(V.reciprocal(out, sumsq_root))
    step(V.tensor_scalar(out, out, limit, 1.0, ALU.mult, ALU.min))


def mix(nc, g, xn, x, w_qkv, gamma, beta, w_dw, w_pw, w_res, b_res):
    nq, n2 = g.stat[:, 0:NT], g.stat[:, NT:2 * NT]
    za, zb = g.stat[:, 2 * NT:3 * NT], g.stat[:, 3 * NT:4 * NT]
    s1 = g.coef[:, 0:NT]
    XN3 = xn.rearrange("p (t n) -> p t n", t=NT)
    S3 = g.b2.rearrange("p (t n) -> p t n", t=NT)
    with phase(nc, g, "step", "squared", "summed", "rooted", "ready", "logged") as (block, s):
        @block.scalar
        def _(act):
            nc.scalar.activation(g.b2, xn, ACT.Square).then_inc(s["squared"], 1)
            act.wait_ge(s["summed"], 1)
            nc.scalar.activation(nq, n2, ACT.Sqrt).then_inc(s["rooted"], 1)
            act.wait_ge(s["ready"], 1)
            nc.scalar.activation(za, n2, ACT.Ln, bias=1.0, scale=1.0)
            nc.scalar.activation(zb, n2, ACT.Ln, bias=1.0, scale=-1.0).then_inc(s["logged"], 1)

        @block.vector
        def _(dve):
            V = nc.vector
            step = Steps(dve, s["step"])
            dve.wait_ge(s["squared"], 1)
            V.tensor_reduce(n2, S3, AX, ALU.add).then_inc(s["summed"], 1)
            dve.wait_ge(s["rooted"], 1)
            step(V.tensor_scalar(nq, nq, 1e-15, None, ALU.max))
            step(V.reciprocal(s1, nq))
            V.tensor_scalar(n2, nq, MAXNORM, None, ALU.min).then_inc(s["ready"], 1)
            dve.wait_ge(s["logged"], 1)
            step(V.tensor_tensor(za, za, zb, ALU.subtract))
            step(V.scalar_tensor_tensor(s1, za, 0.5, s1, ALU.mult, ALU.mult))

    H1T = g.view(19200, 6 * N)
    H3 = H1T.rearrange("p (j n) -> p j n", j=6)
    psA = g.ps[:, 2, 0:4 * P].rearrange("p (j r) -> p j r", r=P)
    psB = g.ps[:, 3, 0:2 * P].rearrange("p (j r) -> p j r", r=P)
    psT = g.psT[:, 0:2 * P].rearrange("p (k r) -> p k r", r=P)
    hT = g.ht[:, 0:2 * P].rearrange("p (k r) -> p k r", r=P)
    with phase(nc, g, "loaded", "staged", "turned", "fetched", "made", "kept") as (block, s):
        @block.sync
        def _(sp):
            sp.dma_start(w3(g.w1, 2, MIX), split_k(w_qkv[2], 2)).then_inc(s["loaded"], 16)

        @block.scalar
        def _(act):
            act.sem_inc(s["staged"], 1)
            with act.Fori(0, NT) as t:
                before(act, s["turned"], t)
                nc.scalar.activation(g.stage[:, 0:D], col(xn, t, D), ACT.Copy, scale=col(s1, t)).then_inc(s["staged"], 1)

        @block.tensor
        def _(pe):
            pe.sem_inc(s["turned"], 1)
            pe.sem_inc(s["made"], 1)
            pe.wait_ge(s["loaded"], 16)
            with pe.Fori(0, NT) as t:
                this(pe, s["staged"], t)
                for k in range(2):
                    ins = nc.tensor.transpose(psT[:, k, :], g.stage[:, k * 128:(k + 1) * 128], g.ident[0:P, 0:P])
                ins.then_inc(s["turned"], 1)
                this(pe, s["fetched"], t)
                before(pe, s["kept"], t)
                for j in range(6):
                    ps = psA[:, j, :] if j < 4 else psB[:, j - 4, :]
                    for k in range(2):
                        ins = nc.tensor.matmul(ps, g.w1[:, k * MIX + j * 128:k * MIX + (j + 1) * 128], hT[:, k, :],
                                               start=(k == 0), stop=(k == 1))
                ins.then_inc(s["made"], 1)

        @block.vector
        def _(dve):
            dve.sem_inc(s["fetched"], 1)
            dve.sem_inc(s["kept"], 1)
            with dve.Fori(0, NT) as t:
                this(dve, s["turned"], t)
                before(dve, s["made"], t)
                nc.vector.tensor_copy(hT, psT).then_inc(s["fetched"], 1)
                this(dve, s["made"], t)
                nc.vector.tensor_copy(H3[:, 0:4, bass.ds(t * P, P)], psA)
                nc.vector.tensor_copy(H3[:, 4:6, bass.ds(t * P, P)], psB).then_inc(s["kept"], 1)

    mean, nmean, var, sc, sh = (g.vec[:, 6 * k:6 * k + 6] for k in range(5))
    gb, bb, dw = (g.vec[:, 6 * k:6 * k + 6] for k in range(5, 8))
    BD = g.w1[:, 0:MIX].rearrange("p (j o) -> p j o", j=6)
    brw = g.w1[0:P, MIX:MIX + D]
    with phase(nc, g, "loaded", "zeroed", "placed", "step", "means", "squares", "rooted", "ready", "done") as (block, s):
        @block.sync
        def _(sp):
            for a, b in ((gb, gamma), (bb, beta), (dw, w_dw[2])):
                sp.dma_start(a, b.rearrange("(j p) -> p j", p=128), allow_slow_non_contiguous=True).then_inc(s["loaded"], 16)
            sp.dma_start(brw, b_res.partition_broadcast(P)).then_inc(s["loaded"], 16)
            sp.dma_start(w3(g.w2, 4, D), split_k(w_res, 4)).then_inc(s["loaded"], 16)
            sp.wait_ge(s["zeroed"], 1)
            for q in range(4):
                sp.dma_start(BD[32 * q:32 * q + 32, :, 32 * q:32 * q + 32], w_pw[q]).then_inc(s["placed"], 16)

        @block.scalar
        def _(act):
            act.wait_ge(s["means"], 1)
            for j in range(6):
                ins = nc.scalar.activation(g.view(12800, N), H3[:, j, :], ACT.Square, bias=nmean[:, j:j + 1],
                                           accum_out=var[:, j:j + 1])
                ins.then_inc(s["squares"], 1)
                act.wait_ge(s["squares"], j + 1)
            nc.scalar.activation(sc, var, ACT.Sqrt, bias=g.eps[:, :], scale=1.0 / N).then_inc(s["rooted"], 1)
            act.wait_ge(s["ready"], 1)
            for j in range(6):
                ins = nc.scalar.activation(H3[:, j, :], H3[:, j, :], ACT.Relu, bias=sh[:, j:j + 1], scale=sc[:, j:j + 1])
            ins.then_inc(s["done"], 1)
            act.wait_ge(s["done"], 1)

        @block.vector
        def _(dve):
            V = nc.vector
            step = Steps(dve, s["step"])
            V.memset(g.w1[:, 0:MIX], 0.0).then_inc(s["zeroed"], 1)
            step(V.tensor_reduce(mean, H3, AX, ALU.add))
            step(V.tensor_scalar(mean, mean, 1.0 / N, None, ALU.mult))
            V.tensor_scalar(nmean, mean, -1.0, None, ALU.mult).then_inc(s["means"], 1)
            dve.wait_ge(s["loaded"], 16 * 5)
            dve.wait_ge(s["placed"], 64)
            for j in range(6):
                V.tensor_scalar(BD[:, j, :], BD[:, j, :], dw[:, j:j + 1], None, ALU.mult)
            dve.wait_ge(s["rooted"], 1)
            step(V.reciprocal(sc, sc))
            step(V.tensor_tensor(sc, sc, gb, ALU.mult))
            step(V.tensor_tensor(sh, mean, sc, ALU.mult))
            V.tensor_tensor(sh, bb, sh, ALU.subtract).then_inc(s["ready"], 1)

    FT = g.b2
    psC = [g.ps[0:P, 4 * u:4 * u + 3, :].rearrange("p b n -> p (b n)") for u in range(2)]
    psO = [g.ps[:, 4 * u + 3, 0:4 * P].rearrange("p (k r) -> p k r", r=P) for u in range(2)]
    psF = [g.ps[0:P, 4 * u + 3, 0:D] for u in range(2)]
    with ExitStack() as ctx:
        cat0 = ctx.enter_context(nc.sbuf_tensor("cat", [P, 2 * MIX], F32))
        small = ctx.enter_context(nc.sbuf_tensor("small", [P, 64], F32))
        cat = [cat0[:, :], g.h1[0:P, :]]
        nn = [small[:, 32 * u:32 * u + 12] for u in range(2)]
        ks = [small[:, 32 * u + 16:32 * u + 32] for u in range(2)]
        num = [g.stage[:, 0:512], g.w2[0:P, 1024:1536]]
        spare = [g.view(37950, 512), g.w2[:, 1536:2048]]
        den = [w[0:P, :] for w in spare]
        hjT = [w.rearrange("p (j r) -> p j r", r=P) for w in (g.ht[:, 0:6 * P], g.w1[:, 1024:1024 + 6 * P])]
        oT = [w[:, 0:4 * P].rearrange("p (k r) -> p k r", r=P) for w in spare]
        with phase(nc, g, "taken", "turned", "sq1", "nn1", "sq2", "nn2", "cat_ready", "sq3", "nn3", "out_ready",
                   "oturned", "ofetched", "made", "kept", "step1", "step2", "step3") as (block, s):

            def two_before(eng, sem, t):
                if not isinstance(t, int) or t >= 2:
                    this(eng, sem, t - 2)

            def slots(eng, slot):
                slot(0, 0, False, True, True)
                with eng.Fori(0, (NT - 3) // 2) as i:
                    slot(i * 2 + 1, 1, True, True, True)
                    slot(i * 2 + 2, 0, True, True, True)
                slot(NT - 2, 1, True, True, False)
                slot(NT - 1, 0, True, False, False)

            @block.tensor
            def _(pe):
                for q in (s["turned"], s["oturned"], s["made"]):
                    pe.sem_inc(q, 1)

                def turn(t, u):
                    this(pe, s["taken"], t)
                    two_before(pe, s["nn2"], t)
                    for j in range(6):
                        nc.tensor.transpose(psC[u][:, j * 128:(j + 1) * 128], hjT[u][:, j, :], g.ident[:, :])
                    for j in range(6, 12):
                        ins = nc.tensor.matmul(psC[u][:, j * 128:(j + 1) * 128], hjT[u][:, j - 6, :], BD[:, j - 6, :],
                                               start=True, stop=True)
                    ins.then_inc(s["turned"], 1)

                def residual(t, u):
                    this(pe, s["out_ready"], t)
                    two_before(pe, s["kept"], t)
                    for k in range(4):
                        ins = nc.tensor.transpose(psO[u][:, k, :], num[u][:, k * 128:(k + 1) * 128], g.ident[0:P, 0:P])
                    ins.then_inc(s["oturned"], 1)
                    this(pe, s["ofetched"], t)
                    for k in range(4):
                        ins = nc.tensor.matmul(psF[u], oT[u][:, k, :], g.w2[:, k * D:(k + 1) * D], start=(k == 0), stop=(k == 3))
                    ins.then_inc(s["made"], 1)

                def slot(t, u, behind, ahead, ahead2):
                    if behind:
                        residual(t - 1, 1 - u)
                    if ahead2:
                        turn(t + 2, u)

                turn(0, 0)
                turn(1, 1)
                slots(pe, slot)
                residual(NT - 1, 0)

            @block.scalar
            def _(act):
                for q in (s["sq1"], s["nn1"], s["sq2"], s["nn2"], s["sq3"], s["nn3"], s["ofetched"], s["taken"]):
                    act.sem_inc(q, 1)

                def take(t, u):
                    two_before(act, s["turned"], t)
                    nc.scalar.copy(hjT[u], H3[:, :, bass.ds(t * P, P)]).then_inc(s["taken"], 1)

                def norm(t, u, n, ready, ap, squares=None):
                    this(act, s[ready], t)
                    squares = g.o[:, 0:ap.shape[-1]] if squares is None else squares
                    nc.scalar.activation(squares, ap, ACT.Square,
                                         accum_out=nn[u][:, 2 * n:2 * n + 1]).then_inc(s[f"sq{n + 1}"], 1)
                    this(act, s[f"sq{n + 1}"], t)
                    nc.scalar.activation(nn[u][:, 2 * n + 1:2 * n + 2], nn[u][:, 2 * n:2 * n + 1],
                                         ACT.Sqrt).then_inc(s[f"nn{n + 1}"], 1)

                def last(t, u):
                    norm(t, u, 2, "out_ready", num[u])
                    this(act, s["oturned"], t)
                    nc.scalar.copy(oT[u], psO[u]).then_inc(s["ofetched"], 1)

                def slot(t, u, behind, ahead, ahead2):
                    norm(t, u, 1, "cat_ready", cat[u], psC[u])
                    if ahead:
                        norm(t + 1, 1 - u, 0, "turned", psC[1 - u][:, 0:MIX])
                    if behind:
                        last(t - 1, 1 - u)
                    if ahead2:
                        take(t + 2, u)

                take(0, 0)
                take(1, 1)
                norm(0, 0, 0, "turned", psC[0][:, 0:MIX])
                slots(act, slot)
                last(NT - 1, 0)

            @block.vector
            def _(dve):
                V = nc.vector
                for q in (s["cat_ready"], s["out_ready"], s["kept"]):
                    dve.sem_inc(q, 1)

                def scale_rows(t, u):
                    step = Steps(dve, s["step1"], t, 3)
                    this(dve, s["nn1"], t)
                    norm_factor(V, step, nn[u][:, 6:7], nn[u][:, 1:2], ATANH_MAX)
                    step.end()
                    V.tensor_scalar(cat[u], psC[u], nn[u][:, 6:7], None, ALU.mult).then_inc(s["cat_ready"], 1)

                def attend(t, u):
                    step = Steps(dve, s["step2"], t, 8)
                    this(dve, s["nn2"], t)
                    norm_factor(V, step, nn[u][:, 7:8], nn[u][:, 3:4], ATANH_MAX)
                    f = nn[u][:, 7:8]
                    c3 = cat[u].rearrange("p (g c) -> p g c", g=16)
                    q, k, v = (c3[:, :, c * 32:(c + 1) * 32] for c in range(3))
                    n3 = num[u].rearrange("p (g d) -> p g d", g=16)
                    d3 = den[u].rearrange("p (g d) -> p g d", g=16)
                    V.tensor_scalar(c3[:, :, 0:64], c3[:, :, 0:64], f, 0.0, ALU.mult, ALU.max)
                    step(V.tensor_scalar(v, v, f, None, ALU.mult))
                    V.tensor_reduce(ks[u], k, AX, ALU.add)
                    step(V.tensor_scalar(d3, v, 1e-15, None, ALU.add))
                    step(V.reciprocal(den[u], den[u]))
                    step(V.tensor_tensor(n3, q, v, ALU.mult))
                    step(V.tensor_tensor(n3, n3, ks[u].unsqueeze(2).to_broadcast([P, 16, 32]), ALU.mult))
                    step.end()
                    V.tensor_tensor(num[u], num[u], den[u], ALU.mult).then_inc(s["out_ready"], 1)

                def keep(t, u):
                    step = Steps(dve, s["step3"], t, 3)
                    this(dve, s["nn3"], t)
                    norm_factor(V, step, nn[u][:, 8:9], nn[u][:, 5:6], ATANH_MAX)
                    step.end()
                    this(dve, s["made"], t)
                    V.scalar_tensor_tensor(col(FT, t, D), psF[u], nn[u][:, 8:9], brw, ALU.mult, ALU.add).then_inc(s["kept"], 1)

                def slot(t, u, behind, ahead, ahead2):
                    attend(t, u)
                    if ahead:
                        scale_rows(t + 1, 1 - u)
                    if behind:
                        keep(t - 1, 1 - u)

                scale_rows(0, 0)
                slots(dve, slot)
                keep(NT - 1, 0)

    F3 = FT.rearrange("p (t n) -> p t n", t=NT)
    sq = g.b3
    with phase(nc, g, "squared", "summed", "rooted", "tanhed", "step") as (block, s):
        @block.scalar
        def _(act):
            nc.scalar.activation(sq, FT, ACT.Square).then_inc(s["squared"], 1)
            act.wait_ge(s["summed"], 1)
            nc.scalar.activation(nq, n2, ACT.Sqrt).then_inc(s["rooted"], 1)
            act.wait_ge(s["rooted"], 1)
            nc.scalar.activation(za, nq, ACT.Tanh).then_inc(s["tanhed"], 1)

        @block.vector
        def _(dve):
            V = nc.vector
            step = Steps(dve, s["step"])
            dve.wait_ge(s["squared"], 1)
            V.tensor_reduce(n2, sq.rearrange("p (t n) -> p t n", t=NT), AX, ALU.add).then_inc(s["summed"], 1)
            dve.wait_ge(s["tanhed"], 1)
            step(V.tensor_scalar(za, za, MAXNORM, None, ALU.min))
            step(V.tensor_scalar(nq, nq, 1e-15, None, ALU.max))
            step(V.reciprocal(zb, nq))
            step(V.tensor_tensor(za, za, zb, ALU.mult))
            step(V.tensor_tensor(F3, F3, za.unsqueeze(2).to_broadcast([P, NT, D]), ALU.mult))
            step(V.tensor_tensor(x, x, FT, ALU.add))



def vector_phase(nc, g, program):
    with phase(nc, g, "step") as (block, s):
        @block.vector
        def _(dve):
            program(nc.vector, Steps(dve, s["step"]))


def graph_attention_layer(nc, g, d, Wq, Wk, Wv, Wo, gam, bet, first):
    ps = [[g.ps[0:P, 2 + m + 3 * u, 0:D] for u in range(2)] for m in range(3)]
    wts = [g.w1[:, 0:512], g.w1[:, 512:1024], g.w1[:, 1024:1536]]

    def split(V, t, u):
        V.tensor_copy(col(g.b2, t, D), ps[0][u])
        for m in (1, 2):
            ins = V.tensor_copy(g.o[:, m * D:(m + 1) * D], ps[m][u])
        return ins

    tile_pass(nc, g, g.h, 2, [(mm_weights(wts[m], D), ps[m]) for m in range(3)],
              [(w3(wts[m], 2, D), split_k(w, 2)) for m, w in enumerate((Wq, Wk, Wv))], split,
              tables=[(tb, g.o[:, m * D:(m + 1) * D]) for m, tb in ((1, d.k), (2, d.v))])
    edge_scores(nc, g, g.b2, d.k, d.links)
    segment_softmax(nc, g)
    edge_sums(nc, g, d.v, g.sums, True)

    S3 = g.sums.rearrange("p (t c) -> p t c", c=D + 9)
    Z3 = S3[:, :, D:D + 9]

    def normalise(V, step):
        if first:
            step(V.tensor_scalar(g.coef[:, 0:NT], Z3[:, :, 8], 0.0, None, ALU.is_gt))
            step(V.tensor_scalar(g.coef[:, NT:2 * NT], Z3[:, :, 8], 1.0, None, ALU.max))
        z = g.ht[0:P, 0:NT * HEADS]
        step(V.tensor_scalar(z.rearrange("p (t h) -> p t h", h=HEADS), Z3[:, :, 0:8], 1e-9, None, ALU.add))
        step(V.reciprocal(z, z))
        z3 = z.rearrange("p (t h) -> p t h", h=HEADS)
        for h in range(HEADS):
            A = S3[:, :, h * DK:(h + 1) * DK]
            V.tensor_tensor(A, A, z3[:, :, h:h + 1].to_broadcast([P, NT, DK]), ALU.mult)

    vector_phase(nc, g, normalise)
    if first:
        with phase(nc, g, "rooted", "step") as (block, s):
            @block.scalar
            def _(act):
                nc.scalar.activation(g.coef[:, 2 * NT:3 * NT], g.coef[:, NT:2 * NT], ACT.Sqrt).then_inc(s["rooted"], 1)

            @block.vector
            def _(dve):
                step = Steps(dve, s["step"])
                dve.wait_ge(s["rooted"], 1)
                step(nc.vector.reciprocal(g.dinv[:, :], g.coef[:, 2 * NT:3 * NT]))
                step(nc.vector.tensor_tensor(g.dinv[:, :], g.dinv[:, :], g.coef[:, 0:NT], ALU.mult))
    down = [g.ps[0:P, 4 + u, 0:D] for u in range(2)]
    tile_pass(nc, g, g.sums, 2, [(mm_weights(g.w2, D), down)], [(w3(g.w2, 2, D), split_k(Wo, 2))],
              add_into(down, g.h, g.unit), row=D + 9)
    layernorm(nc, g, g.h, g.h, gam, bet)


def routed_ffn(nc, g, a, d):
    xn, x = g.h, g.x
    layernorm(nc, g, x, xn)
    K1 = max(1, int(0.5 * N))
    K1 = K1 - 1 if K1 > 1 else 1
    wr = g.w1[0:P, 0:D]
    br = g.vec[0:P, 0:1]
    wt, rank = g.stat[:, 0:NT], g.stat[:, NT:2 * NT]
    later = g.stat[:, 2 * NT:3 * NT]
    part = g.stat[:, 3 * NT:4 * NT]
    wrow = g.view(19200, N, P)
    junk = g.view(22400, N, P)
    tri = g.view(25600, P, P)
    tri2 = g.view(25800, P, P)
    products, X3 = (b.rearrange("p (t n) -> p t n", t=NT) for b in (g.b2, xn))
    with phase(nc, g, "loaded", "step", "turned", "rowed", "stored", "back", "tri") as (block, s):
        @block.sync
        def _(sp):
            sp.dma_start(wr, a["L0_ffn_wr"].rearrange("n o -> (n o)").partition_broadcast(P)).then_inc(s["loaded"], 16)
            sp.dma_start(br, a["L0_ffn_br"].partition_broadcast(P)).then_inc(s["loaded"], 16)
            sp.wait_ge(s["rowed"], 1)
            sp.dma_start(d.rowa.rearrange("(t p) -> t p", p=P), g.o[0:NT, 0:P]).then_inc(s["stored"], 16)
            sp.wait_ge(s["stored"], 16)
            sp.dma_start(wrow, d.rowa.partition_broadcast(P)).then_inc(s["back"], 16)

        @block.gpsimd
        def _(pool):
            nc.gpsimd.memset(tri, 1.0).then_inc(s["tri"], 1)
            pool.wait_ge(s["tri"], 1)
            nc.gpsimd.affine_select(out=tri, in_=tri, compare_op=ALU.is_gt, fill=0.0, base=0, pattern=[[-1, P]],
                                    channel_multiplier=1).then_inc(s["tri"], 1)

        @block.tensor
        def _(pe):
            pe.wait_ge(s["turned"], 1)
            nc.tensor.transpose(g.ps[0:NT, 0, 0:P], wt, g.ident[0:P, 0:P]).then_inc(s["turned"], 1)

        @block.vector
        def _(dve):
            V = nc.vector
            step = Steps(dve, s["step"])
            dve.wait_ge(s["loaded"], 32)
            step(V.tensor_tensor(products, X3, wr.unsqueeze(1).to_broadcast([P, NT, D]), ALU.mult))
            step(V.tensor_reduce(wt, products, AX, ALU.add))
            V.tensor_scalar(wt, wt, br, None, ALU.add).then_inc(s["turned"], 1)
            dve.wait_ge(s["turned"], 2)
            V.tensor_copy(g.o[0:NT, 0:P], g.ps[0:NT, 0, 0:P]).then_inc(s["rowed"], 1)
            dve.wait_ge(s["back"], 16)
            dve.wait_ge(s["tri"], 2)
            step(V.memset(g.stat[:, NT:2 * NT], 0.0))
            step(V.memset(later, 0.0))
            for t in range(NT):
                me = wt[:, t:t + 1]
                a0, a1 = t * P, (t + 1) * P
                if t:
                    step(V.tensor_scalar(junk[:, 0:a0], wrow[:, 0:a0], me, 0.0, ALU.is_ge, ALU.add, accum_out=rank[:, t:t + 1]))
                step(V.tensor_scalar(junk[:, a0:N], wrow[:, a0:N], me, 0.0, ALU.is_gt, ALU.add, accum_out=later[:, t:t + 1]))
                step(V.scalar_tensor_tensor(tri2, wrow[:, a0:a1], me, tri, ALU.is_equal, ALU.mult))
                step(V.tensor_reduce(part[:, t:t + 1], tri2, AX, ALU.add))
            step(V.tensor_tensor(rank, rank, later, ALU.add))
            step(V.tensor_tensor(rank, rank, part, ALU.add))
            step(V.scalar_tensor_tensor(g.coef[:, 0:NT], rank, float(K1), wt, ALU.is_lt, ALU.mult))
            step(V.tensor_tensor(x, x, xn, ALU.add))
    mlp(nc, g, xn, a["L0_ffn_w1"], a["L0_ffn_b1"], a["L0_ffn_w2"], a["L0_ffn_b2"], ACT.Gelu_apprx_tanh, x, g.coef[:, 0:NT],
        side=fill_penalties(nc, g, d))


def graph_convolution(nc, g, a, d):
    layernorm(nc, g, g.x, g.h)
    ps = [g.ps[0:P, 4 + u, 0:D] for u in range(2)]

    def to_table(V, t, u):
        return V.tensor_scalar(g.o[:, 0:D], ps[u], col(g.dinv, t), None, ALU.mult)

    tile_pass(nc, g, g.h, 2, [(mm_weights(g.w1, D), ps)], [(w3(g.w1, 2, D), split_k(a["L1_gnn_W"], 2))], to_table,
              tables=[(d.q, g.o[:, 0:D])])
    edge_sums(nc, g, d.q, g.b2, False)

    def add(V, step):
        A3 = g.b2.rearrange("p (t n) -> p t n", t=NT)
        step(V.tensor_tensor(A3, A3, g.dinv[:, :].unsqueeze(2).to_broadcast([P, NT, D]), ALU.mult))
        step(V.tensor_tensor(g.x, g.x, g.b2, ALU.add))
    vector_phase(nc, g, add)


def linear_attention(nc, g, a, d, l):
    y, xh = g.h, g.b5
    q, k, v = g.b2, g.b3, g.b4
    layernorm(nc, g, y, xh)
    ps = [[g.ps[0:P, 2 + m + 3 * u, 0:D] for u in range(2)] for m in range(3)]
    wts = [g.w1[:, 0:512], g.w1[:, 512:1024], g.w1[:, 1024:1536]]
    aff = (g.vec[:, 32:34], g.vec[:, 34:36])

    def keep(V, t, u):
        for m, b in enumerate((q, k, v)):
            ins = V.tensor_copy(col(b, t, D), ps[m][u])
        return ins

    tile_pass(nc, g, xh, 2, [(mm_weights(wts[m], D), ps[m]) for m in range(3)],
              [(w3(wts[m], 2, D), split_k(w[l], 2)) for m, w in enumerate((a["L1_mix_Wq"], a["L1_mix_Wk"], a["L1_mix_Wv"]))]
              + [(aff[0], a["L1_mix_ln1_g"][l].rearrange("(k p) -> p k", p=128)),
                 (aff[1], a["L1_mix_ln1_b"][l].rearrange("(k p) -> p k", p=128))], keep, affine=aff,
              side=lift_penalties(nc, g, d, 128 * l, 24))

    S = float(DK) ** -0.25
    Q4 = q.rearrange("p (n d) -> p n d", d=DK)
    K3 = k.rearrange("p (t n) -> p t n", t=NT)
    KT = k.rearrange("p (t n) -> p n t", t=NT)
    qm = g.ht[0:P, 0:NT * HEADS]
    kcol = g.o[:, 0:D]
    kmT = g.vec[:, 0:2]
    bd = g.h1[:, 0:256].rearrange("p (k n) -> p k n", k=2)
    with phase(nc, g, "step", "kcol", "kturn", "kmax", "krow", "ksub", "qsub", "kexp", "qexp", "side_a", "side_b") as (block, s):
        lift_penalties(nc, g, d, 128 * l + 40, 16)(block, s)

        @block.vector
        def _(dve):
            V = nc.vector
            step = Steps(dve, s["step"])
            V.tensor_reduce(kcol, KT, AX, ALU.max).then_inc(s["kcol"], 1)
            step(V.tensor_reduce(qm, Q4, AX, ALU.max))
            V.tensor_tensor(Q4, Q4, qm.unsqueeze(2).to_broadcast([P, NT * HEADS, DK]), ALU.subtract).then_inc(s["qsub"], 1)
            dve.wait_ge(s["kturn"], 1)
            step(V.tensor_reduce(kmT, g.ps[:, 0, 0:2 * P].rearrange("p (k r) -> p k r", r=P), AX, ALU.max))
            for c in range(2):
                ins = V.tensor_scalar(bd[:, c, :], g.ident[:, :], kmT[:, c:c + 1], None, ALU.mult)
            ins.then_inc(s["kmax"], 1)
            dve.wait_ge(s["krow"], 1)
            step(V.tensor_copy(kcol, g.ps[0:P, 1, 0:D]))
            V.tensor_tensor(K3, K3, kcol.unsqueeze(1).to_broadcast([P, NT, D]), ALU.subtract).then_inc(s["ksub"], 1)
            dve.wait_ge(s["qexp"], 1)
            step(V.tensor_reduce(qm, Q4, AX, ALU.add))
            step(V.reciprocal(qm, qm))
            step(V.tensor_tensor(Q4, Q4, qm.unsqueeze(2).to_broadcast([P, NT * HEADS, DK]), ALU.mult))

        @block.tensor
        def _(pe):
            pe.wait_ge(s["kcol"], 1)
            for c in range(2):
                ins = nc.tensor.transpose(g.ps[:, 0, c * P:(c + 1) * P], kcol[:, c * 128:(c + 1) * 128], g.ident[0:P, 0:P])
            ins.then_inc(s["kturn"], 1)
            pe.wait_ge(s["kmax"], 1)
            for c in range(2):
                ins = nc.tensor.matmul(g.ps[0:P, 1, c * 128:(c + 1) * 128], g.ones[:, 0:P], bd[:, c, :], start=True, stop=True)
            ins.then_inc(s["krow"], 1)

        @block.scalar
        def _(act):
            act.wait_ge(s["qsub"], 1)
            nc.scalar.activation(q, q, ACT.Exp, scale=S).then_inc(s["qexp"], 1)
            act.wait_ge(s["ksub"], 1)
            nc.scalar.activation(k, k, ACT.Exp, scale=S).then_inc(s["kexp"], 1)
            act.wait_ge(s["kexp"], 1)

    ctxT = g.h1[:, 0:256].rearrange("p (c n) -> p c n", c=2)
    rk = g.h1[:, 256:512].rearrange("p (c n) -> p c n", c=2)
    wctx = g.w1[:, 0:512]
    hd = g.h1[:, 512:640]
    TS = 5
    vst = g.w1[0:P, 0:TS * D]
    with phase(nc, g, "masked", "zeroed", "made", "step", "ready", "loaded", "fused", "staged", "read") as (block, s):
        @block.sync
        def _(sp):
            sp.dma_start(w3(g.w2, 2, D), split_k(a["L1_mix_Wo"][l], 2)).then_inc(s["loaded"], 16)

        @block.gpsimd
        def _(pool):
            nc.gpsimd.memset(hd, 0.0).then_inc(s["masked"], 1)
            pool.wait_ge(s["masked"], 1)
            for b in range(4):
                nc.gpsimd.memset(hd[32 * b:32 * b + 32, 32 * b:32 * b + 32], 1.0).then_inc(s["masked"], 1)

        @block.scalar
        def _(act):
            act.sem_inc(s["staged"], 1)
            with act.Fori(0, NT // TS) as t:
                before(act, s["read"], t)
                nc.scalar.copy(vst, col(v, t, TS * D)).then_inc(s["staged"], 1)

        @block.tensor
        def _(pe):
            pe.sem_inc(s["read"], 1)
            pe.wait_ge(s["zeroed"], 1)
            z = g.o[0:1, 0:128]
            for c in range(2):
                nc.tensor.matmul(g.ps[:, 2 + c, 0:128], z, z, start=True, stop=False, skip_group_check=True)
                nc.tensor.matmul(g.ps[:, 4 + c, 0:128], z, z, start=True, stop=False, skip_group_check=True)
            with pe.Fori(0, NT // TS) as t:
                this(pe, s["staged"], t)
                for n in range(TS):
                    for c in range(2):
                        kt = k[:, bass.ds(t * (TS * D) + n * D + c * 128, 128)]
                        nc.tensor.matmul(g.ps[:, 2 + c, 0:128], vst[:, n * D + c * 128:n * D + (c + 1) * 128], kt,
                                         start=False, stop=False, skip_group_check=True)
                        ins = nc.tensor.matmul(g.ps[:, 4 + c, 0:128], g.ones[0:P, :], kt, start=False, stop=False,
                                               skip_group_check=True)
                ins.then_inc(s["read"], 1)
            for c in range(2):
                nc.tensor.matmul(g.ps[:, 2 + c, 0:128], z, z, start=False, stop=True, skip_group_check=True)
                ins = nc.tensor.matmul(g.ps[:, 4 + c, 0:128], z, z, start=False, stop=True, skip_group_check=True)
            ins.then_inc(s["made"], 1)
            pe.wait_ge(s["ready"], 1)
            pe.wait_ge(s["loaded"], 16)
            for c in range(2):
                ins = nc.tensor.matmul(g.ps[:, 6 + c, 0:D], ctxT[:, c, :], g.w2[:, c * D:(c + 1) * D], start=True, stop=True)
            ins.then_inc(s["fused"], 1)

        @block.vector
        def _(dve):
            V = nc.vector
            step = Steps(dve, s["step"])
            V.memset(g.o[0:1, 0:128], 0.0).then_inc(s["zeroed"], 1)
            dve.wait_ge(s["masked"], 5)
            dve.wait_ge(s["made"], 1)
            step(V.reciprocal(rk, g.ps[:, 4:6, 0:128]))
            for c in range(2):
                step(V.tensor_tensor(rk[:, c, :], rk[:, c, :], hd, ALU.mult))
            V.tensor_tensor(ctxT, g.ps[:, 2:4, 0:128], rk, ALU.mult).then_inc(s["ready"], 1)
            dve.wait_ge(s["fused"], 1)
            step(V.tensor_copy(wctx.rearrange("p (c n) -> p c n", c=2), g.ps[:, 6:8, 0:D]))

    down = [g.ps[0:P, 4 + u, 0:D] for u in range(2)]
    tile_pass(nc, g, q, 2, [(mm_weights(wctx, D), down)],
              [(g.brow[:, :], a["L1_mix_bo"][l].rearrange("(a n) -> a n", a=1))], add_into(down, y, g.unit), bias=True,
              side=lift_penalties(nc, g, d, 128 * l + 24, 16))


def transformer(nc, g, a, d):
    y = g.h
    for l in range(4):
        linear_attention(nc, g, a, d, l)
        layernorm(nc, g, y, g.b5)
        aff = (g.vec[:, 32:34], g.vec[:, 34:36])
        mlp(nc, g, g.b5, a["L1_mix_W1"][l], a["L1_mix_b1"][l], a["L1_mix_W2"][l], a["L1_mix_b2"][l], ACT.Gelu, y, g.unit, affine=aff,
            side=lift_penalties(nc, g, d, 128 * l + 56, 72),
            extra=[(aff[0], a["L1_mix_ln2_g"][l].rearrange("(k p) -> p k", p=128)),
                   (aff[1], a["L1_mix_ln2_b"][l].rearrange("(k p) -> p k", p=128))])

    def add(V, step):
        step(V.tensor_tensor(g.x, g.x, y, ALU.add))
    vector_phase(nc, g, add)


def experts(nc, g, a, d):
    xn, x = g.h, g.x
    layernorm(nc, g, x, xn)
    H, EX = 4, 4
    small = g.view(12800, 6400, P)
    hg = small[:, 0:NT * 16]
    tab = small[:, 400:400 + NT * 20]
    dtab = small[:, 900:900 + NT * 8]
    ps = [g.ps[0:P, 4 + u, 0:16] for u in range(2)]

    def keep(V, t, u):
        return V.tensor_copy(col(hg, t, 16), ps[u])

    tile_pass(nc, g, xn, 2, [(lambda k: g.w1[:, k * 16:(k + 1) * 16], ps)],
              [(w3(g.w1, 2, 16), split_k(a["L1_ffn_W_gat"], 2))], keep)

    T3 = tab.rearrange("p (t c) -> p t c", c=20)
    D3 = dtab.rearrange("p (t c) -> p t c", c=8)
    H4 = hg.rearrange("p (n e) -> p n e", e=EX)
    tmp = small[:, 1100:1500]
    aS, aD = small[:, 1500:1516], small[:, 1516:1532]
    sc = small[:, 1600:1700]
    arow = g.view(19200, 4 * N, P)
    pen = [g.view(31700 + 3200 * b, N, P) for b in range(2)]
    with phase(nc, g, "loaded", "step", "table", "stored") as (block, s):
        @block.sync
        def _(sp):
            sp.dma_start(aS, a["L1_ffn_att_src"].rearrange("h e -> (h e)").partition_broadcast(P)).then_inc(s["loaded"], 16)
            sp.dma_start(aD, a["L1_ffn_att_dst"].rearrange("h e -> (h e)").partition_broadcast(P)).then_inc(s["loaded"], 16)
            sp.wait_ge(s["table"], 1)
            sp.dma_start(d.tab.rearrange("(t p) c -> p t c", p=P), T3).then_inc(s["stored"], 16)
            for h in range(H):
                sp.dma_start(d.arow[h * N:(h + 1) * N].rearrange("(t p) -> p t", p=P), T3[:, :, 16 + h],
                             allow_slow_non_contiguous=True).then_inc(s["stored"], 16)
            sp.wait_ge(s["stored"], 16 * 5)

        @block.vector
        def _(dve):
            V = nc.vector
            step = Steps(dve, s["step"])
            dve.wait_ge(s["loaded"], 32)
            t4 = tmp.rearrange("p (t c) -> p t c", c=16)
            h3 = hg.rearrange("p (t c) -> p t c", c=16)
            for n, w in enumerate((aD, aS)):
                step(V.tensor_tensor(t4, h3, w.unsqueeze(1).to_broadcast([P, NT, 16]), ALU.mult))
                step(V.tensor_reduce(sc, tmp.rearrange("p (n e) -> p n e", e=EX), AX, ALU.add))
                out = (D3[:, :, 0:4], T3[:, :, 16:20])[n]
                step(V.tensor_copy(out, sc.rearrange("p (t h) -> p t h", h=H)))
            V.tensor_copy(T3[:, :, 0:16], h3).then_inc(s["table"], 1)

    EC = E2 // 128
    sI = g.view(31700, EC).bitcast(I32)
    dI = g.view(32300, EC).bitcast(I32)
    sF, dF = g.view(32900, EC), g.view(33500, EC)
    srcI, dstI = g.srcv_e, g.dstv_e
    ei = a["L1_ffn_edge_index"]
    with phase(nc, g, "loaded", "step") as (block, s):
        @block.sync
        def _(sp):
            sp.dma_start(sI, ei[0].rearrange("(p c) -> p c", p=128)).then_inc(s["loaded"], 16)
            sp.dma_start(dI, ei[1].rearrange("(p c) -> p c", p=128)).then_inc(s["loaded"], 16)

        @block.vector
        def _(dve):
            V = nc.vector
            step = Steps(dve, s["step"])
            dve.wait_ge(s["loaded"], 32)
            step(V.tensor_copy(sF, sI))
            step(V.tensor_copy(dF, dI))
            step(V.tensor_scalar(sF, sF, float(N - 1), None, ALU.min))
            step(V.tensor_copy(srcI, sF))
            step(V.tensor_scalar(dF, dF, float(N - 1), None, ALU.min))
            step(V.tensor_copy(dstI, dF))
            step(V.tensor_scalar(g.dlo, dI, 127, None, ALU.bitwise_and))
            step(V.tensor_scalar(g.dhi, dI, 7, None, ALU.logical_shift_right))

    mx = small[:, 1700:1700 + NT * H]
    sums = g.ps[0:P, :, :].rearrange("p b c -> p (b c)")[:, 0:N]
    with phase(nc, g, "loaded", "pen0", "pen1", "used0", "used1") as (block, s):
        lp, us = [s["pen0"], s["pen1"]], [s["used0"], s["used1"]]

        @block.sync
        def _(sp):
            for h in range(H):
                sp.dma_start(arow[:, h * N:(h + 1) * N], d.arow[h * N:(h + 1) * N].partition_broadcast(P)).then_inc(s["loaded"], 16)
            for t in range(NT):
                if t >= 2:
                    sp.wait_ge(us[t % 2], H * (t // 2))
                sp.dma_start(pen[t % 2], d.pen[t * P * N:(t + 1) * P * N].rearrange("(p n) -> p n", p=P)).then_inc(lp[t % 2], 16)

        @block.vector
        def _(dve):
            dve.wait_ge(s["loaded"], 64)
            for t in range(NT):
                dve.wait_ge(lp[t % 2], 16 * (t // 2 + 1))
                for h in range(H):
                    if t or h:
                        before_ = (t, h - 1) if h else (t - 1, H - 1)
                        dve.wait_ge(us[before_[0] % 2], H * (before_[0] // 2) + before_[1] + 1)
                    nc.vector.tensor_tensor_reduce(sums, pen[t % 2],
                                                   arow[:, h * N:(h + 1) * N], 1.0, -BIG, ALU.add, ALU.max,
                                                   mx[:, t * H + h:t * H + h + 1]).then_inc(us[t % 2], 1)

    lk = small[:, 1800:1900]
    wself = small[:, 1900:2000]
    agg = small[:, 2100:2600]
    A3 = agg.rearrange("p (t c) -> p t c", c=20)
    with phase(nc, g, "step", "shifted", "expd", "table", "stored") as (block, s):
        @block.vector
        def _(dve):
            V = nc.vector
            step = Steps(dve, s["step"])
            m3 = mx.rearrange("p (t h) -> p t h", h=H)
            l3 = lk.rearrange("p (t h) -> p t h", h=H)
            step(V.tensor_tensor(m3, m3, T3[:, :, 16:20], ALU.max))
            step(V.tensor_tensor(m3, m3, D3[:, :, 0:4], ALU.add))
            step(V.tensor_copy(l3, m3))
            V.scalar_tensor_tensor(D3[:, :, 4:8], l3, 0.2, m3, ALU.mult, ALU.max).then_inc(s["table"], 1)
            dve.wait_ge(s["table"], 1)
            step(V.tensor_tensor(m3, T3[:, :, 16:20], D3[:, :, 0:4], ALU.add))
            step(V.tensor_copy(l3, m3))
            step(V.scalar_tensor_tensor(l3, l3, 0.2, m3, ALU.mult, ALU.max))
            V.tensor_tensor(l3, l3, D3[:, :, 4:8], ALU.subtract).then_inc(s["shifted"], 1)

        @block.scalar
        def _(act):
            act.wait_ge(s["shifted"], 1)
            nc.scalar.activation(wself, lk, ACT.Exp).then_inc(s["expd"], 1)
            act.wait_ge(s["expd"], 1)

        @block.sync
        def _(sp):
            sp.wait_ge(s["table"], 1)
            sp.dma_start(d.dtab.rearrange("(t p) c -> p t c", p=P), D3).then_inc(s["stored"], 16)
            sp.wait_ge(s["stored"], 16)

    GB, NB = 8, 25

    def buffers(u):
        v = lambda off, n: g.view(19200 + 6000 * u + off, n)
        b = Names()
        b.rows = v(0, GB * 20).rearrange("p (j c) -> p j c", c=20)
        b.drows = v(160, GB * 8).rearrange("p (j c) -> p j c", c=8)
        b.ee = v(224, GB * 4).rearrange("p (j c) -> p j c", c=4)
        b.e2 = v(256, GB * 4).rearrange("p (j c) -> p j c", c=4)
        b.pay = v(288, GB * 20).rearrange("p (j c) -> p j c", c=20)
        b.ohh = v(448, GB * NB).rearrange("p (j t) -> p j t", t=NB)
        b.ohl = [v(656 + 128 * j, 128) for j in range(GB)]
        b.big = [v(1680 + 500 * j, 500) for j in range(GB)]
        b.ix = g.ht[:, 2 * GB * u:2 * GB * (u + 1)].bitcast(I32)
        return b

    bufs = [buffers(0), buffers(1)]
    loF, hiF = g.loF, g.hiF
    total = g.ps[:, 3, 0:NB * 20]
    ALLD = g.view(31700, NB * 20)
    sets = [f"{n}{u}" for n in ("gathered", "raw", "expd", "made", "summed", "step") for u in range(2)]
    names = ["zeroed", "indexed", "final", "copied", "stored", "back", "red"] + sets
    with phase(nc, g, *names) as (block, s):
        gathered, raw, expd, made, summed, stepped = ([s[f"{n}{u}"] for u in range(2)]
                                                      for n in ("gathered", "raw", "expd", "made", "summed", "step"))

        @block.gpsimd
        def _(pool):
            with pool.Fori(0, EC // (2 * GB)) as i:
                for u, b in enumerate(bufs):
                    before(pool, made[u], i)
                    c = i * (2 * GB) + u * GB
                    nc.gpsimd.tensor_copy(b.ix[:, 0:GB], srcI[:, bass.ds(c, GB)]).then_inc(s["indexed"], 1)
                    nc.gpsimd.tensor_copy(b.ix[:, GB:2 * GB], dstI[:, bass.ds(c, GB)]).then_inc(s["indexed"], 1)
                    hold(pool, s["indexed"], i * 4 + 2 * (u + 1))
                    for j in range(GB):
                        nc.gpsimd.indirect_dma_start(b.rows[:, j, :], None, d.tab,
                                                     bass.IndirectOffsetOnAxis(b.ix[:, j:j + 1], 0)).then_inc(gathered[u], 16)
                        nc.gpsimd.indirect_dma_start(b.drows[:, j, :], None, d.dtab,
                                                     bass.IndirectOffsetOnAxis(b.ix[:, GB + j:GB + j + 1], 0)).then_inc(gathered[u], 16)

        @block.scalar
        def _(act):
            for q in expd:
                act.sem_inc(q, 1)
            with act.Fori(0, EC // (2 * GB)) as i:
                for u, b in enumerate(bufs):
                    this(act, raw[u], i)
                    nc.scalar.activation(b.pay[:, :, 16:20], b.ee, ACT.Exp).then_inc(expd[u], 1)

        @block.vector
        def _(dve):
            V = nc.vector
            V.memset(g.o[0:1, 0:500], 0.0).then_inc(s["zeroed"], 1)
            V.tensor_copy(loF, g.dlo)
            V.tensor_copy(hiF, g.dhi).then_inc(s["zeroed"], 1)
            dve.wait_ge(s["zeroed"], 2)
            for q in raw + made:
                dve.sem_inc(q, 1)
            with dve.Fori(0, EC // (2 * GB)) as i:
                for u, b in enumerate(bufs):
                    step = Steps(dve, stepped[u], i, 4)
                    c = i * (2 * GB) + u * GB
                    landed(dve, gathered[u], i, 32 * GB)
                    step(V.tensor_tensor(b.ee, b.rows[:, :, 16:20], b.drows[:, :, 0:4], ALU.add))
                    step(V.scalar_tensor_tensor(b.e2, b.ee, 0.2, b.ee, ALU.mult, ALU.max))
                    before(dve, summed[u], i)
                    V.tensor_tensor(b.ee, b.e2, b.drows[:, :, 4:8], ALU.subtract).then_inc(raw[u], 1)
                    for j in range(GB):
                        V.tensor_scalar(b.ohl[j], g.iota[:, :], loF[:, bass.ds(c + j, 1)], None, ALU.is_equal)
                    step(V.tensor_tensor(b.ohh, g.iota[:, 0:NB].unsqueeze(1).to_broadcast([128, GB, NB]),
                                         hiF[:, bass.ds(c, GB)].unsqueeze(2).to_broadcast([128, GB, NB]), ALU.is_equal))
                    this(dve, expd[u], i)
                    r4 = b.rows[:, :, 0:16].rearrange("p j (h e) -> p j h e", h=H)
                    p4 = b.pay[:, :, 0:16].rearrange("p j (h e) -> p j h e", h=H)
                    for j in range(GB):
                        ins = V.tensor_tensor(p4[:, j], r4[:, j], b.pay[:, j, 16:20].unsqueeze(2).to_broadcast([128, H, EX]),
                                              ALU.mult)
                    step(ins)
                    for j in range(GB):
                        ins = V.tensor_tensor(b.big[j].rearrange("p (t c) -> p t c", c=20),
                                              b.ohh[:, j, :].unsqueeze(2).to_broadcast([128, NB, 20]),
                                              b.pay[:, j, :].unsqueeze(1).to_broadcast([128, NB, 20]), ALU.mult)
                    ins.then_inc(made[u], 1)
                    step.end()
            dve.wait_ge(s["final"], 1)
            V.tensor_copy(ALLD, total).then_inc(s["copied"], 1)
            dve.wait_ge(s["back"], 16)
            step2 = Steps(dve, s["red"])
            own = g.view(32300, NT * 20, P).rearrange("p (t c) -> p t c", c=20)
            for h in range(H):
                o = own[:, :, 4 * h:4 * h + 4]
                w = wself.rearrange("p (t h) -> p t h", h=H)[:, :, h:h + 1].to_broadcast([P, NT, EX])
                step2(V.tensor_tensor(o, T3[:, :, 4 * h:4 * h + 4], w, ALU.mult))
            step2(V.tensor_copy(own[:, :, 16:20], wself.rearrange("p (t h) -> p t h", h=H)))
            step2(V.tensor_tensor(A3, A3, own, ALU.add))

        @block.tensor
        def _(pe):
            for q in summed:
                pe.sem_inc(q, 1)
            pe.wait_ge(s["zeroed"], 1)
            nc.tensor.matmul(total, g.o[0:1, 0:128], g.o[0:1, 0:500], start=True, stop=False, skip_group_check=True)
            with pe.Fori(0, EC // (2 * GB)) as i:
                for u, b in enumerate(bufs):
                    this(pe, made[u], i)
                    for j in range(GB):
                        ins = nc.tensor.matmul(total, b.ohl[j], b.big[j], start=False, stop=False, skip_group_check=True)
                    ins.then_inc(summed[u], 1)
            nc.tensor.matmul(total, g.o[0:1, 0:128], g.o[0:1, 0:500], start=False, stop=True,
                             skip_group_check=True).then_inc(s["final"], 1)

        @block.sync
        def _(sp):
            sp.wait_ge(s["copied"], 1)
            sp.dma_start(d.agg.rearrange("(t p) c -> p t c", p=128), ALLD.rearrange("p (t c) -> p t c", c=20)).then_inc(s["stored"], 16)
            sp.wait_ge(s["stored"], 16)
            sp.dma_start(A3, d.agg[0:N, :].rearrange("(t p) c -> p t c", p=P)).then_inc(s["back"], 16)

    rz = small[:, 2600:2700]
    s16 = small[:, 2700:3100]
    sq = small[:, 3100:3500]
    m1, v1, r1, q1 = (small[:, 3500 + 25 * n:3525 + 25 * n] for n in range(4))
    par = small[:, 3600:3648]
    scr = small[:, 3700:3800]
    cmpb = small[:, 3800:4200]
    rk4 = small[:, 4200:4300]
    ex = small[:, 4300:4400]
    gate = small[:, 4400:4500]
    lower = small[:, 4500:4516]
    with phase(nc, g, "loaded", "lowset", "step", "var", "std", "shifted", "expd") as (block, s):
        @block.sync
        def _(sp):
            for n, b in enumerate((a["L1_ffn_b_gat"], a["L1_ffn_ln_gamma"], a["L1_ffn_ln_beta"])):
                sp.dma_start(par[:, 16 * n:16 * n + 16], b.partition_broadcast(P)).then_inc(s["loaded"], 16)

        @block.gpsimd
        def _(pool):
            nc.gpsimd.memset(lower, 0.0).then_inc(s["lowset"], 1)
            pool.wait_ge(s["lowset"], 1)
            for n in range(1, EX):
                nc.gpsimd.memset(lower[:, n * EX:n * EX + n], 1.0).then_inc(s["lowset"], 1)

        @block.scalar
        def _(act):
            act.wait_ge(s["var"], 1)
            nc.scalar.activation(q1, v1, ACT.Sqrt, bias=g.eps[0:P, :], scale=1.0 / 16).then_inc(s["std"], 1)
            act.wait_ge(s["shifted"], 1)
            nc.scalar.activation(ex, scr, ACT.Exp).then_inc(s["expd"], 1)

        @block.vector
        def _(dve):
            V = nc.vector
            step = Steps(dve, s["step"])
            step(V.tensor_scalar(rz.rearrange("p (t h) -> p t h", h=H), A3[:, :, 16:20], 1e-16, None, ALU.add))
            step(V.reciprocal(rz, rz))
            S3 = s16.rearrange("p (t c) -> p t c", c=16)
            Q3 = sq.rearrange("p (t c) -> p t c", c=16)
            w16 = [P, NT, 16]
            step(V.tensor_copy(S3, A3[:, :, 0:16]))
            s4 = s16.rearrange("p (n e) -> p n e", e=EX)
            step(V.tensor_tensor(s4, s4, rz.unsqueeze(2).to_broadcast([P, NT * H, EX]), ALU.mult))
            dve.wait_ge(s["loaded"], 48)
            step(V.tensor_tensor(S3, S3, par[:, 0:16].unsqueeze(1).to_broadcast(w16), ALU.add))
            step(V.tensor_reduce(m1, S3, AX, ALU.add))
            step(V.tensor_scalar(m1, m1, 1.0 / 16, None, ALU.mult))
            step(V.tensor_tensor(S3, S3, m1.unsqueeze(2).to_broadcast(w16), ALU.subtract))
            step(V.tensor_tensor(sq, s16, s16, ALU.mult))
            V.tensor_reduce(v1, Q3, AX, ALU.add).then_inc(s["var"], 1)
            dve.wait_ge(s["std"], 1)
            step(V.reciprocal(r1, q1))
            step(V.tensor_tensor(S3, S3, r1.unsqueeze(2).to_broadcast(w16), ALU.mult))
            step(V.tensor_tensor(S3, S3, par[:, 16:32].unsqueeze(1).to_broadcast(w16), ALU.mult))
            step(V.tensor_tensor(S3, S3, par[:, 32:48].unsqueeze(1).to_broadcast(w16), ALU.add))
            sc3 = scr.rearrange("p (t e) -> p t e", e=EX)
            step(V.tensor_tensor(sc3, S3[:, :, 0:4], S3[:, :, 4:8], ALU.add))
            step(V.tensor_tensor(sc3, sc3, S3[:, :, 8:12], ALU.add))
            step(V.tensor_tensor(sc3, sc3, S3[:, :, 12:16], ALU.add))
            step(V.tensor_scalar(scr, scr, 0.25, None, ALU.mult))
            dve.wait_ge(s["lowset"], EX)
            k3 = rk4.rearrange("p (t e) -> p t e", e=EX)
            c3 = cmpb.rearrange("p (t e) -> p t e", e=16)
            for i in range(EX):
                me = sc3[:, :, i:i + 1].to_broadcast([P, NT, EX])
                gt, eq = c3[:, :, 0:4], c3[:, :, 4:8]
                step(V.tensor_tensor(gt, sc3, me, ALU.is_gt))
                step(V.tensor_tensor(eq, sc3, me, ALU.is_equal))
                step(V.tensor_tensor(eq, eq, lower[:, i * EX:(i + 1) * EX].unsqueeze(1).to_broadcast([P, NT, EX]), ALU.mult))
                step(V.tensor_tensor(gt, gt, eq, ALU.add))
                step(V.tensor_reduce(k3[:, :, i:i + 1], gt, AX, ALU.add))
            step(V.tensor_reduce(m1, sc3, AX, ALU.max))
            V.tensor_tensor(sc3, sc3, m1.unsqueeze(2).to_broadcast([P, NT, EX]), ALU.subtract).then_inc(s["shifted"], 1)
            dve.wait_ge(s["expd"], 1)
            step(V.scalar_tensor_tensor(ex, rk4, 2.0, ex, ALU.is_lt, ALU.mult))
            e3 = ex.rearrange("p (t e) -> p t e", e=EX)
            step(V.tensor_reduce(m1, e3, AX, ALU.add))
            step(V.reciprocal(r1, m1))
            step(V.tensor_tensor(gate.rearrange("p (e t) -> p t e", e=EX), e3, r1.unsqueeze(2).to_broadcast([P, NT, EX]), ALU.mult))
    for e in range(EX):
        mlp(nc, g, xn, a["L1_ffn_W1"][e], a["L1_ffn_b1"][e], a["L1_ffn_W2"][e], a["L1_ffn_b2"][e], ACT.Gelu, x,
            gate[:, e * NT:(e + 1) * NT])


def gps_program(nc, a, out):
    d = Names()

    def dram(name, shape, dt=F32):
        return nc.dram_tensor(name, shape, dt, kind="Internal").ap()

    d.key, d.w, d.keys = dram("key", [ET]), dram("w", [NV], I32), dram("keys", [NV * P + 16])
    d.q, d.k, d.v = dram("q_rows", [N, D]), dram("k_rows", [N, D]), dram("v_rows", [N, D])
    d.rowa, d.arow = dram("rowa", [N]), dram("arow", [4 * N])
    d.pen, d.tab, d.dtab, d.agg = dram("pen", [N * N]), dram("tab", [N, 20]), dram("dtab", [N, 8]), dram("agg", [25 * 128, 20])
    d.links = dram("links", [128, SEQ + 1])
    with ExitStack() as ctx:
        g = setup(nc, ctx)
        EC = E2 // 128
        g.loF, g.hiF = g.view(35300, EC), g.view(34700, EC)
        constants(nc, g)
        plan_visits(nc, g, a["src"], a["dst"], d)
        with phase(nc, g, "loaded") as (block, s):
            @block.sync
            def _(sp):
                sp.dma_start(g.x.rearrange("p (t n) -> p t n", t=NT),
                             a["x"].rearrange("(t p) n -> p t n", p=P)).then_inc(s["loaded"], 16)
                sp.wait_ge(s["loaded"], 16)

        layernorm(nc, g, g.x, g.h)
        spill(nc, g, d.links)
        mix(nc, g, g.h, g.x, a["L0_mix_w_qkv"], a["L0_mix_bn_gamma"], a["L0_mix_bn_beta"], a["L0_mix_w_dw"], a["L0_mix_w_pw"],
            a["L0_mix_w_res"], a["L0_mix_b_res"])
        for l in range(2):
            graph_attention_layer(nc, g, d, a["L0_gnn_Wq"][l], a["L0_gnn_Wk"][l], a["L0_gnn_Wv"][l], a["L0_gnn_Wo"][l],
                                  a["L0_gnn_ln_g"][l], a["L0_gnn_ln_b"][l], l == 0)
        mlp(nc, g, g.h, a["L0_gnn_w1"], a["L0_gnn_b1"], a["L0_gnn_w2"], a["L0_gnn_b2"], ACT.Relu, g.x, g.unit)
        routed_ffn(nc, g, a, d)

        graph_convolution(nc, g, a, d)
        penalty_indices(nc, g, a)
        transformer(nc, g, a, d)
        experts(nc, g, a, d)
        store(nc, g, g.x, out)


_NAMES = ["x", "src", "dst", "L0_gnn_Wq", "L0_gnn_Wk", "L0_gnn_Wv", "L0_gnn_Wo", "L0_gnn_ln_g", "L0_gnn_ln_b", "L0_gnn_w1",
          "L0_gnn_b1", "L0_gnn_w2", "L0_gnn_b2", "L0_mix_w_qkv", "L0_mix_bn_gamma", "L0_mix_bn_beta", "L0_mix_w_dw",
          "L0_mix_w_pw", "L0_mix_w_res", "L0_mix_b_res", "L0_ffn_wr", "L0_ffn_br", "L0_ffn_w1", "L0_ffn_b1", "L0_ffn_w2",
          "L0_ffn_b2", "L1_gnn_W", "L1_mix_Wq", "L1_mix_Wk", "L1_mix_Wv", "L1_mix_Wo", "L1_mix_bo", "L1_mix_ln1_g",
          "L1_mix_ln1_b", "L1_mix_W1", "L1_mix_b1", "L1_mix_W2", "L1_mix_b2", "L1_mix_ln2_g", "L1_mix_ln2_b",
          "L1_ffn_W_gat", "L1_ffn_att_src", "L1_ffn_att_dst", "L1_ffn_b_gat", "L1_ffn_ln_gamma", "L1_ffn_ln_beta",
          "L1_ffn_W1", "L1_ffn_b1", "L1_ffn_W2", "L1_ffn_b2", "L1_ffn_edge_index"]


def _layout(name, a):
    if name == "L0_mix_w_qkv":
        a = a.transpose(2, 1, 0)
    if name == "L0_mix_w_dw":
        a = a.reshape(MIX, 5).transpose(1, 0)
    if name == "L0_mix_w_pw":
        a = a.reshape(6, 4, 32, 32).transpose(1, 3, 0, 2)
    if name == "L0_mix_w_res":
        a = a.reshape(D, 2 * D).transpose(1, 0)
    return np.ascontiguousarray(a)


def kernel(**inputs):
    import concourse.bacc as bacc
    from concourse.bass_utils import run_bass_kernel_spmd

    nc = bacc.Bacc("TRN2", target_bir_lowering=False, num_devices=1)
    arrays, aps = {}, {}
    for name in _NAMES:
        v = _layout(name, np.asarray(inputs[name]))
        arrays["in_" + name] = v
        aps[name] = nc.dram_tensor("in_" + name, v.shape, mybir.dt.from_np(v.dtype), kind="ExternalInput").ap()
    out = nc.dram_tensor("out", (N, D), F32, kind="ExternalOutput").ap()
    gps_program(nc, aps, out)
    return run_bass_kernel_spmd(nc, [arrays], core_ids=[0]).results[0]["out"]
```
